# Optimizing a Trainium2 kernel written in Bass

```python
import numpy as np
import jax
import jax.numpy as jnp

def _softmax(x, axis=-1):
    return jax.nn.softmax(x, axis=axis)

def _gelu(x):
    return jax.nn.gelu(x, approximate=True)

def _silu(x):
    return jax.nn.silu(x)

def _sigmoid(x):
    return jax.nn.sigmoid(x)

def _layernorm(x, axis=-1, eps=1e-05):
    m = jnp.mean(x, axis=axis, keepdims=True)
    v = jnp.var(x, axis=axis, keepdims=True)
    return (x - m) / jnp.sqrt(v + eps)

def _scatter_add(tgt, idx, src, axis=0):
    return tgt.at[idx].add(src)

def _segment_sum(src, seg, n):
    return jax.ops.segment_sum(src, seg, n)
kernel_name = 'mk_adaln_d1_jaxref_r8_a07717'

def setup_inputs(seed: int=0):
    np.random.seed(seed)
    _w = jnp.asarray

    def _L0_attn_setup():
        import jax, jax.numpy as jnp
        import numpy as np
        H = 4

        def rmsnorm(x, scale, eps=1e-08):
            norm = jnp.linalg.norm(x, axis=-1, keepdims=True) / jnp.sqrt(jnp.float32(x.shape[-1]))
            return scale * (x / (norm + eps))

        def wkv_scan(q, k, v, w):
            B, T, _, D = q.shape
            qT = jnp.swapaxes(q, 0, 1)
            kT = jnp.swapaxes(k, 0, 1)
            vT = jnp.swapaxes(v, 0, 1)

            def step(carry, inp):
                A, z = carry
                qt, kt, vt = inp
                A = w[None, :, :, None] * A + kt[..., None] * vt[..., None, :]
                z = w[None] * z + kt
                S = jnp.einsum('bhd,bhde->bhe', qt, A)
                return ((A, z), (S, z))
            A0 = jnp.zeros((B, H, D, D), q.dtype)
            z0 = jnp.zeros((B, H, D), q.dtype)
            _, (S, Z) = jax.lax.scan(step, (A0, z0), (qT, kT, vT))
            return (jnp.swapaxes(S, 0, 1), jnp.swapaxes(Z, 0, 1))
        key = jax.random.key(seed)
        ks = jax.random.split(key, 12)
        B, T, C = (4, 256, 128)
        inv_sqrt_c = 1.0 / np.sqrt(C)
        return {'x': jax.random.normal(ks[0], (B, T, C), jnp.float32), 'time_decay': jax.random.normal(ks[1], (C,), jnp.float32) * 0.5, 'mix_q': jax.random.uniform(ks[2], (1, 1, C), jnp.float32), 'mix_k': jax.random.uniform(ks[3], (1, 1, C), jnp.float32), 'mix_v': jax.random.uniform(ks[4], (1, 1, C), jnp.float32), 'mix_g': jax.random.uniform(ks[5], (1, 1, C), jnp.float32), 'Wq': jax.random.normal(ks[6], (C, C), jnp.float32) * inv_sqrt_c, 'Wk': jax.random.normal(ks[7], (C, C), jnp.float32) * inv_sqrt_c, 'Wv': jax.random.normal(ks[8], (C, C), jnp.float32) * inv_sqrt_c, 'Wg': jax.random.normal(ks[9], (C, C), jnp.float32) * inv_sqrt_c, 'Wo': jax.random.normal(ks[10], (C, C), jnp.float32) * inv_sqrt_c, 'norm_scale': jnp.ones((C,), jnp.float32)}
    _L0_attn_in = _L0_attn_setup()

    def _L0_ffn_setup():
        import jax, jax.numpy as jnp
        import numpy as np
        B, T, C = (2, 128, 128)
        H = 512
        E_R, E_S, K = (8, 2, 2)

        def _rmsnorm(x, g):
            eps = jnp.finfo(x.dtype).eps
            return x * jax.lax.rsqrt(jnp.mean(x * x, axis=-1, keepdims=True) + eps) * g

        def _experts_mlp(x, g, W1, b1, W2, b2):
            xn = _rmsnorm(x, g)
            h = jnp.einsum('btc,ech->bteh', xn, W1) + b1
            h = jax.nn.gelu(h, approximate=False)
            return jnp.einsum('bteh,ehc->btec', h, W2) + b2
        key = jax.random.key(seed)
        ks = jax.random.split(key, 12)
        s = 0.02
        return {'u': jax.random.normal(ks[0], (B, T, C), dtype=jnp.float32), 'g_shared': jnp.ones((C,), jnp.float32), 'W1_s': jax.random.normal(ks[1], (E_S, C, H), jnp.float32) * s, 'b1_s': jax.random.normal(ks[2], (E_S, H), jnp.float32) * s, 'W2_s': jax.random.normal(ks[3], (E_S, H, C), jnp.float32) * s, 'b2_s': jax.random.normal(ks[4], (E_S, C), jnp.float32) * s, 'g_routed': jnp.ones((C,), jnp.float32), 'W1_r': jax.random.normal(ks[5], (E_R, C, H), jnp.float32) * s, 'b1_r': jax.random.normal(ks[6], (E_R, H), jnp.float32) * s, 'W2_r': jax.random.normal(ks[7], (E_R, H, C), jnp.float32) * s, 'b2_r': jax.random.normal(ks[8], (E_R, C), jnp.float32) * s, 'centroids': jax.random.normal(ks[9], (C, E_R), jnp.float32) * s}
    _L0_ffn_in = _L0_ffn_setup()
    _L0_c = _w((lambda *s: np.random.randn(*s).astype(np.float32) * 0.05)(16, 128))
    _L0_wmod = _w((lambda *s: np.random.randn(*s).astype(np.float32) * 0.05)(128, 6 * 128) * 128 ** (-0.5))
    _d = {'L0_attn_x': _L0_attn_in['x'], 'L0_attn_time_decay': _L0_attn_in['time_decay'], 'L0_attn_mix_q': _L0_attn_in['mix_q'], 'L0_attn_mix_k': _L0_attn_in['mix_k'], 'L0_attn_mix_v': _L0_attn_in['mix_v'], 'L0_attn_mix_g': _L0_attn_in['mix_g'], 'L0_attn_Wq': _L0_attn_in['Wq'], 'L0_attn_Wk': _L0_attn_in['Wk'], 'L0_attn_Wv': _L0_attn_in['Wv'], 'L0_attn_Wg': _L0_attn_in['Wg'], 'L0_attn_Wo': _L0_attn_in['Wo'], 'L0_attn_norm_scale': _L0_attn_in['norm_scale'], 'L0_ffn_g_shared': _L0_ffn_in['g_shared'], 'L0_ffn_W1_s': _L0_ffn_in['W1_s'], 'L0_ffn_b1_s': _L0_ffn_in['b1_s'], 'L0_ffn_W2_s': _L0_ffn_in['W2_s'], 'L0_ffn_b2_s': _L0_ffn_in['b2_s'], 'L0_ffn_g_routed': _L0_ffn_in['g_routed'], 'L0_ffn_W1_r': _L0_ffn_in['W1_r'], 'L0_ffn_b1_r': _L0_ffn_in['b1_r'], 'L0_ffn_W2_r': _L0_ffn_in['W2_r'], 'L0_ffn_b2_r': _L0_ffn_in['b2_r'], 'L0_ffn_centroids': _L0_ffn_in['centroids'], 'L0_c': _L0_c, 'L0_wmod': _L0_wmod}
    _x0 = _d['L0_attn_x']
    _d['L0_attn_x'] = jax.random.normal(jax.random.fold_in(jax.random.key(seed), 1), (16, 256, 128), dtype=_x0.dtype)
    del _x0
    return _d

def reference(L0_attn_x, L0_attn_time_decay, L0_attn_mix_q, L0_attn_mix_k, L0_attn_mix_v, L0_attn_mix_g, L0_attn_Wq, L0_attn_Wk, L0_attn_Wv, L0_attn_Wg, L0_attn_Wo, L0_attn_norm_scale, L0_ffn_g_shared, L0_ffn_W1_s, L0_ffn_b1_s, L0_ffn_W2_s, L0_ffn_b2_s, L0_ffn_g_routed, L0_ffn_W1_r, L0_ffn_b1_r, L0_ffn_W2_r, L0_ffn_b2_r, L0_ffn_centroids, L0_c, L0_wmod):

    def _L0_attn_ref(x, time_decay, mix_q, mix_k, mix_v, mix_g, Wq, Wk, Wv, Wg, Wo, norm_scale):
        import jax, jax.numpy as jnp
        import numpy as np
        H = 4

        def rmsnorm(x, scale, eps=1e-08):
            norm = jnp.linalg.norm(x, axis=-1, keepdims=True) / jnp.sqrt(jnp.float32(x.shape[-1]))
            return scale * (x / (norm + eps))

        def wkv_scan(q, k, v, w):
            B, T, _, D = q.shape
            qT = jnp.swapaxes(q, 0, 1)
            kT = jnp.swapaxes(k, 0, 1)
            vT = jnp.swapaxes(v, 0, 1)

            def step(carry, inp):
                A, z = carry
                qt, kt, vt = inp
                A = w[None, :, :, None] * A + kt[..., None] * vt[..., None, :]
                z = w[None] * z + kt
                S = jnp.einsum('bhd,bhde->bhe', qt, A)
                return ((A, z), (S, z))
            A0 = jnp.zeros((B, H, D, D), q.dtype)
            z0 = jnp.zeros((B, H, D), q.dtype)
            _, (S, Z) = jax.lax.scan(step, (A0, z0), (qT, kT, vT))
            return (jnp.swapaxes(S, 0, 1), jnp.swapaxes(Z, 0, 1))
        B, T, C = x.shape
        D = C // H
        xx = jnp.pad(x, ((0, 0), (1, 0), (0, 0)))[:, :-1]
        xq = x * mix_q + xx * (1.0 - mix_q)
        xk = x * mix_k + xx * (1.0 - mix_k)
        xv = x * mix_v + xx * (1.0 - mix_v)
        xg = x * mix_g + xx * (1.0 - mix_g)
        q = xq @ Wq.T
        k = xk @ Wk.T
        v = xv @ Wv.T
        g = jax.nn.sigmoid(xg @ Wg.T)
        q_exp = jnp.exp(rmsnorm(q, norm_scale))
        k_exp = jnp.exp(rmsnorm(k, norm_scale))
        w = jnp.exp(-jnp.exp(time_decay)).reshape(H, D)
        qh = q_exp.reshape(B, T, H, D)
        kh = k_exp.reshape(B, T, H, D)
        vh = v.reshape(B, T, H, D)
        S, Z = wkv_scan(qh, kh, vh, w)
        Z_scalar = jnp.sum(qh * Z, axis=-1, keepdims=True)
        att = (S / Z_scalar).reshape(B, T, C)
        att = g * att
        return att @ Wo.T

    def _L0_ffn_ref(u, g_shared, W1_s, b1_s, W2_s, b2_s, g_routed, W1_r, b1_r, W2_r, b2_r, centroids):
        import jax, jax.numpy as jnp
        import numpy as np
        B, T, C = (2, 128, 128)
        H = 512
        E_R, E_S, K = (8, 2, 2)

        def _rmsnorm(x, g):
            eps = jnp.finfo(x.dtype).eps
            return x * jax.lax.rsqrt(jnp.mean(x * x, axis=-1, keepdims=True) + eps) * g

        def _experts_mlp(x, g, W1, b1, W2, b2):
            xn = _rmsnorm(x, g)
            h = jnp.einsum('btc,ech->bteh', xn, W1) + b1
            h = jax.nn.gelu(h, approximate=False)
            return jnp.einsum('bteh,ehc->btec', h, W2) + b2
        h_s = _experts_mlp(u, g_shared, W1_s, b1_s, W2_s, b2_s).sum(axis=-2)
        scores = jax.nn.sigmoid(u @ centroids)
        gpk, i_topk = jax.lax.top_k(scores, K)
        gk = gpk / scores.sum(axis=-1, keepdims=True)
        routed_all = _experts_mlp(u, g_routed, W1_r, b1_r, W2_r, b2_r)
        routed_topk = jnp.take_along_axis(routed_all, i_topk[..., None], axis=2)
        h_r = (gk[..., None] * routed_topk).sum(axis=-2)
        return u + h_s + h_r
    x = L0_attn_x
    mod = (_silu(L0_c) @ L0_wmod).reshape(L0_c.shape[0], 6, 1, -1)
    sa, ca, ga, sb, cb, gb = (mod[:, 0], mod[:, 1], mod[:, 2], mod[:, 3], mod[:, 4], mod[:, 5])
    ga = (2 * (ga >= 0) - 1) * jnp.maximum(jnp.abs(ga), 0.25)
    gb = (2 * (gb >= 0) - 1) * jnp.maximum(jnp.abs(gb), 0.25)
    h = _layernorm(x, axis=-1) * (1 + ca) + sa
    x = x + ga * _L0_attn_ref(h, L0_attn_time_decay, L0_attn_mix_q, L0_attn_mix_k, L0_attn_mix_v, L0_attn_mix_g, L0_attn_Wq, L0_attn_Wk, L0_attn_Wv, L0_attn_Wg, L0_attn_Wo, L0_attn_norm_scale)
    h = _layernorm(x, axis=-1) * (1 + cb) + sb
    x = x + gb * _L0_ffn_ref(h, L0_ffn_g_shared, L0_ffn_W1_s, L0_ffn_b1_s, L0_ffn_W2_s, L0_ffn_b2_s, L0_ffn_g_routed, L0_ffn_W1_r, L0_ffn_b1_r, L0_ffn_W2_r, L0_ffn_b2_r, L0_ffn_centroids)
    return x

_drawn_inputs = setup_inputs


def setup_inputs(seed=0):
    import zlib

    import numpy as np

    out = dict(_drawn_inputs(seed))
    spreads = {'L0_attn_norm_scale': (1.0, 0.6),
     'L0_ffn_g_shared': (1.0, 0.6),
     'L0_ffn_g_routed': (1.0, 0.6)}
    factors = {'L0_attn_time_decay': 6.922,
     'L0_attn_mix_q': 8.0,
     'L0_attn_mix_k': 6.029,
     'L0_attn_mix_g': 4.112,
     'L0_attn_Wq': 4.719,
     'L0_attn_Wk': 3.794,
     'L0_ffn_W1_s': 2.936,
     'L0_ffn_b1_s': 8.0,
     'L0_ffn_W2_s': 2.85,
     'L0_ffn_b2_s': 8.0,
     'L0_ffn_W1_r': 8.0,
     'L0_ffn_b1_r': 8.0,
     'L0_ffn_W2_r': 8.0,
     'L0_ffn_b2_r': 44.936,
     'L0_ffn_centroids': 8.0}
    for name, (base, spread) in spreads.items():
        noise = np.random.default_rng([zlib.crc32(name.encode()), seed]).standard_normal(out[name].shape)
        drawn = base * np.exp(spread * noise) if base else spread * noise
        out[name] = jnp.asarray(drawn.astype(out[name].dtype))
    for name, factor in factors.items():
        out[name] = (out[name] * factor).astype(out[name].dtype)
    return out
```

```python
import concourse.bass as bass
from concourse import mybir
from contextlib import ExitStack

F32 = mybir.dt.float32
I32 = mybir.dt.int32
U32 = mybir.dt.uint32
ALU = mybir.AluOpType
ACT = mybir.ActivationFunctionType
AX = mybir.AxisListType

P = 128
NB = 16
T = 256
C = 128
NH = 4
D = C // NH
NT = T // P
CH = 32
NCH = T // CH
BL = 8
NBL = T // BL
NE_S, NE_R = 2, 8
NE = NE_S + NE_R
HID = 512
HC = HID // P
FT = 512
NF = NB * T // FT
FS = FT // P

LN_EPS = 1e-5
RMS_EPS = 1e-8
FFN_EPS = 1.1920929e-07

LAG_OFF = [NBL * sum(BL - m for m in range(l)) for l in range(BL + 1)]
LAGS = LAG_OFF[BL]
PZW = LAGS + T
LG = PZW

STAGES = 9


def reached(n):
    return not isinstance(n, int) or n > 0


class Batch:

    def __init__(self, m, r):
        self.n, self.par, self.quad = 4 * m + r, r % 2, r
        self.turn = 2 * m + r // 2 + 1

        self.fourth = m + 1

    @staticmethod
    def at(n, loop=0):
        return Batch(loop + n // 4, n % 4)


def pipeline(eng, step):
    first = STAGES - 1
    loops = (NB - first) // 4

    def fixed(i):
        step([Batch.at(i - s) if 0 <= i - s < NB else None for s in range(STAGES)])

    for i in range(first):
        fixed(i)
    with eng.Fori(0, loops) as j:
        for i in range(first, first + 4):
            step([Batch.at(i - s, j) for s in range(STAGES)])
    for i in range(first + 4 * loops, NB + STAGES - 1):
        fixed(i)


def adaln_kernel(nc, x, vecs, cT, wqkvg, wo, wmod, w1s, b1, w2s, b2, w1r, w2r, cent, out):
    ctx = ExitStack()
    with ctx:
        def sb(name, shape, dt=F32):
            return ctx.enter_context(nc.sbuf_tensor(name, shape, dt))

        def pb(name, shape):
            return ctx.enter_context(nc.psum_tensor(name, shape, F32))

        def sem(name):
            return ctx.enter_context(nc.semaphore(name))

        modrow_dram = nc.dram_tensor("modrow_dram", (NB, 4 * C), F32, kind="Internal").ap()

        vec = sb("vec", [P, 8])
        MIX = {"q": 1, "k": 2, "v": 3, "g": 4}
        cTt = sb("cTt", [P, NB])
        silu_e = sb("silu_e", [P, NB])
        silu_r = sb("silu_r", [P, NB])
        siluT = sb("siluT", [P, NB])
        W4 = sb("W4", [P, 4, C])
        WoT = sb("WoT", [P, C])
        wm = sb("wm", [P, 6 * C])
        W1 = sb("W1", [P, NE, HID])
        W2 = sb("W2", [P, NE, HC, C])
        b1t = sb("b1t", [P, NE * HC])
        b2t = sb("b2t", [P, NE * C])
        centt = sb("centt", [P, NE_R])
        ident = sb("ident", [P, P])
        blkones = sb("blkones", [P, P])
        iota33 = sb("iota33", [P, CH + 1])
        iota_r = sb("iota_r", [P, CH])
        iota8 = sb("iota8", [P, NE_R])
        expd = sb("expd", [P, 1])
        nexpd = sb("nexpd", [P, 1])
        pw = sb("pw", [P, CH + 1])
        pwr = sb("pwr", [P, CH])
        wrow = sb("wrow", [P, T])
        w32 = sb("w32", [P, D, NCH - 1])
        halfc = sb("halfc", [P, 4])
        nhalfc = sb("nhalfc", [P, 4])
        mask8 = sb("mask8", [P, T], I32)
        modT = sb("modT", [P, 2, NB])
        mrow = sb("mrow", [NB, 4, C])
        msgn = sb("msgn", [NB, 2, C])
        mneg = sb("mneg", [NB, 2, C])
        mabs = sb("mabs", [NB, 2, C])

        Fin = sb("Fin", [P, NB * NT * C])
        zT = sb("zT", [P, NB * T])
        lgt = sb("lgt", [P, NB * NT * NE_R])

        scope = ExitStack()

        def pbuf(name, shape, dt=F32):
            return scope.enter_context(nc.sbuf_tensor(name, shape, dt))

        xb = [pbuf(f"xb{i}", [P, NT, C]) for i in range(2)]
        st1 = [pbuf(f"st1{i}", [P, NT, 6]) for i in range(2)]
        mv1 = [pbuf(f"mv1{i}", [P, NT, 2]) for i in range(2)]
        ve1 = [pbuf(f"ve1{i}", [P, NT]) for i in range(2)]
        rs1 = [pbuf(f"rs1{i}", [P, NT]) for i in range(2)]
        xn = [pbuf(f"xn{i}", [P, NT, C]) for i in range(2)]
        hT = [pbuf(f"hT{i}", [P, T + 1]) for i in range(2)]
        dT = [pbuf(f"dT{i}", [P, T]) for i in range(2)]
        tv = [pbuf(f"tv{i}", [P, 2, T]) for i in range(2)]
        xm = {c: [pbuf(f"xm{c}{i}", [P, T]) for i in range(2)] for c in "qkvg"}
        sq = pbuf("sq", [P, C])
        ssq = [pbuf(f"ssq{i}", [P, 4]) for i in range(2)]
        nrm = [pbuf(f"nrm{i}", [P, 4]) for i in range(2)]
        nre = [pbuf(f"nre{i}", [P, 4]) for i in range(2)]
        rqk = [pbuf(f"rqk{i}", [P, 4]) for i in range(2)]
        eg = [pbuf(f"eg{i}", [P, T]) for i in range(4)]
        vc = [pbuf(f"vc{i}", [P, T]) for i in range(4)]
        vT = [pbuf(f"vT{i}", [P, T]) for i in range(4)]
        qn = [pbuf(f"qn{i}", [P, 4, C]) for i in range(2)]
        qk = [pbuf(f"qk{i}", [P, 2 * T]) for i in range(2)]
        zc = [pbuf(f"zc{i}", [P, T]) for i in range(2)]
        pz = [pbuf(f"pz{i}", [P, PZW]) for i in range(2)]
        it_s, it_t, it_x, it_m, it_y = (pz[1][:, n * T:(n + 1) * T].bitcast(I32) for n in range(5))
        lo = {n: [pbuf(f"{n}{i}", [P, T]) for i in range(2)] for n in ("q8", "k8", "q16", "k16")}
        q32 = [pbuf(f"q32{i}", [P, T]) for i in range(4)]
        k32 = pbuf("k32", [P, T])
        kT = [pbuf(f"kT{i}", [P, T]) for i in range(2)]
        ue = [pbuf(f"ue{i}", [P, D, NCH - 1]) for i in range(2)]
        Ast = [pbuf(f"Ast{i}", [P, D, NCH - 1]) for i in range(2)]
        sc = [pbuf(f"sc{i}", [P, T]) for i in range(2)]
        den = [pbuf(f"den{i}", [P, T]) for i in range(2)]
        rden = [pbuf(f"rden{i}", [P, T]) for i in range(2)]
        slag = [pbuf(f"slag{i}", [P, T]) for i in range(2)]
        tlag = pbuf("tlag", [P, LAGS - T])
        ssum = [pbuf(f"ssum{i}", [P, T]) for i in range(2)]
        att = [pbuf(f"att{i}", [P, T]) for i in range(2)]
        rows = [pbuf(f"rows{i}", [P, 4, C]) for i in range(4)]
        wog = [pbuf(f"wog{i}", [P, C]) for i in range(2)]
        xr = [pbuf(f"xr{i}", [P, NT, C]) for i in range(2)]
        x2 = [pbuf(f"x2{i}", [P, NT, C]) for i in range(2)]
        st2 = [pbuf(f"st2{i}", [P, NT, 6]) for i in range(2)]
        mv2 = [pbuf(f"mv2{i}", [P, NT, 2]) for i in range(2)]
        ve2 = [pbuf(f"ve2{i}", [P, NT]) for i in range(2)]
        rs2 = [pbuf(f"rs2{i}", [P, NT]) for i in range(2)]
        xn2 = [pbuf(f"xn2{i}", [P, NT, C]) for i in range(2)]
        uu = [pbuf(f"uu{i}", [P, NT, C]) for i in range(2)]
        squ = pbuf("squ", [P, C])
        ssu = [pbuf(f"ssu{i}", [P, NT]) for i in range(2)]
        seu = [pbuf(f"seu{i}", [P, NT]) for i in range(2)]
        ru = [pbuf(f"ru{i}", [P, NT]) for i in range(2)]
        iru = [pbuf(f"iru{i}", [P, NT]) for i in range(4)]
        zz = [pbuf(f"zz{i}", [P, NT, C]) for i in range(2)]
        gu = [pbuf(f"gu{i}", [P, NT, C]) for i in range(2)]
        zTs = [pbuf(f"zTs{i}", [P, T]) for i in range(2)]

        scope.close()

        score = sb("score", [P, NB * NT, NE_R])
        ssc = sb("ssc", [P, NB * NT])
        rsc = sb("rsc", [P, NB * NT])
        top = sb("top", [P, NB * NT, 8])
        topi = sb("topi", [P, NB * NT, 8], U32)
        topf = sb("topf", [P, NB * NT, 2])
        hot = sb("hot", [P, 2, NB * NT, NE_R])
        gk = sb("gk", [P, NB * NT, 2])
        gate = sb("gate", [P, NB * NT, NE_R])
        hid = [sb(f"hid{i}", [P, HC, FT]) for i in range(2)]
        yb = [sb(f"yb{i}", [P, FS, C]) for i in range(2)]
        acc = sb("acc", [P, FS, C])
        grow = sb("grow", [P, 2, C])
        fout = sb("fout", [P, FS, C])

        psA = pb("psA", [P, 512])
        psQK = pb("psQK", [P, 512])
        psV = pb("psV", [P, 512])
        psT = pb("psT", [P, 512])
        psB = pb("psB", [P, 1536])
        psL = pb("psL", [P, 512])

        names = """passed_dve passed_pool passed_pe ld_w1 ld_w2 ld_c0 ld_c1 ld_c2 ld_out
            iota_done consts_v expd_done nexpd_done pw_done tabs_done silu_exp silu_one silu_rec silu_done
            mask_a mask_b mask_c mask_d mod_mm mod_row_a mod_row_b mod_row_c mod_row_st mod_done zero_done w1g_done
            ln1_st ln1_ag ln1_ve ln1_pow ln1_xn t1_mm hT_done d_done mix_qk tv_done mix_vg
            proj_mm sq_done eg_done vc_done nrm_pow nre_done rqk_done qn_done vT_done
            t2_mm qk_exp zscan qz_done lag_done lvl_q k32_done q32_done kT_done
            u_mm lvl_mm bc_mm u_cp sc16 scan_done sc_done den_done rden_done lagmul lag0 lagadd
            s_mm ssum_done att_done wog_done
            w_mm x2_done ln2_st ln2_ag ln2_ve ln2_pow ln2_xn um_done u_done squ_done seu_done u_pow iru_done z_done gu_done fin_done
            t3_mm zTs_done zT_done lg_mm lg_done
            sig_done rt_a rt_b rt_c rt_d rt_e rt_f rt_g gate_done
            h_mm gelu_done y_mm yb_done acc_done grow_free gacc_done fout_done""".split()
        S = {n: sem(n) for n in names}
        ld_x = [sem(f"ld_x{i}") for i in range(2)]
        ld_xr = [sem(f"ld_xr{i}") for i in range(2)]
        ld_rows = [sem(f"ld_rows{i}") for i in range(4)]
        ld_g = sem("ld_g")
        st_o = sem("st_o")

        block = ctx.enter_context(nc.Block())

        @block.sync
        def _(sp):
            def load_x(b):
                if reached(b.n - 1):
                    sp.wait_ge(S["ln1_xn"], b.n - 1)
                sp.dma_start(xb[b.par][:], x[bass.ds(b.n, 1)].rearrange("o (t p) c -> p (o t) c", p=P))\
                  .then_inc(ld_x[b.par], 16)

            def load_xr(b):
                if reached(b.n - 1):
                    sp.wait_ge(S["x2_done"], b.n - 1)
                sp.dma_start(xr[b.par][:], x[bass.ds(b.n, 1)].rearrange("o (t p) c -> p (o t) c", p=P))\
                  .then_inc(ld_xr[b.par], 16)

            def load_rows(b):
                if reached(b.n - 3):
                    sp.wait_ge(S["gu_done"], b.n - 3)
                sp.dma_start(rows[b.quad][:].rearrange("p k c -> p (k c)"),
                             modrow_dram[bass.ds(b.n, 1), :].partition_broadcast(P)
                             .rearrange("p o n -> p (o n)")).then_inc(ld_rows[b.quad], 16)

            sp.dma_start(cTt[:], cT).then_inc(S["ld_c0"], 16)
            sp.dma_start(vec[:], vecs).then_inc(S["ld_c0"], 16)
            sp.dma_start(wm[:], wmod).then_inc(S["ld_c0"], 16)
            sp.dma_start(W4[:], wqkvg).then_inc(S["ld_c1"], 16)
            sp.dma_start(WoT[:], wo).then_inc(S["ld_c1"], 16)
            sp.dma_start(centt[:], cent).then_inc(S["ld_c1"], 16)
            sp.wait_ge(S["mod_row_st"], 3)
            sp.dma_start(modrow_dram, mrow[:].rearrange("b k c -> b (k c)")).then_inc(S["ld_out"], 16)
            sp.dma_start(b1t[:], b1).then_inc(S["ld_c2"], 16)
            sp.dma_start(b2t[:], b2.partition_broadcast(P)).then_inc(S["ld_c2"], 16)
            sp.dma_start(W1[:, 0:NE_S, :], w1s.rearrange("e c h -> c e h")).then_inc(S["ld_w1"], 16)
            sp.dma_start(W1[:, NE_S:NE, :], w1r.rearrange("e c h -> c e h")).then_inc(S["ld_w1"], 16)
            sp.dma_start(W2[:, 0:NE_S], w2s.rearrange("e (k p) c -> p e k c", p=P)).then_inc(S["ld_w2"], 16)
            sp.dma_start(W2[:, NE_S:NE], w2r.rearrange("e (k p) c -> p e k c", p=P)).then_inc(S["ld_w2"], 16)
            sp.wait_ge(S["ld_out"], 16)

            def step(st):
                if st[0] is not None:
                    load_x(st[0])
                if st[5] is not None:
                    load_xr(st[5])
                if st[4] is not None:
                    load_rows(st[4])

            pipeline(sp, step)

            sp.wait_ge(S["lg_done"], NB)
            def ffn_step(f):
                if reached(f):
                    sp.wait_ge(S["gacc_done"], f)
                sp.dma_start(grow[:], modrow_dram[bass.ds(2 * f, 2), 3 * C:4 * C].partition_broadcast(P)
                             ).then_inc(ld_g, 16)
                sp.wait_ge(S["fout_done"], f + 1)
                sp.dma_start(out[bass.ds(2 * f, 2)].rearrange("b (t p) c -> p (b t) c", p=P), fout[:])\
                  .then_inc(st_o, 16)

            ffn_step(0)
            with sp.Fori(1, NF) as f:
                ffn_step(f)
            sp.wait_ge(st_o, 16 * NF)

        @block.gpsimd
        def _(pool):
            pool.memset(ident[:], 0.0).then_inc(S["iota_done"], 1)
            pool.memset(blkones[:], 0.0).then_inc(S["iota_done"], 1)
            pool.memset(halfc[:], 0.5).then_inc(S["iota_done"], 1)
            pool.memset(nhalfc[:], -0.5).then_inc(S["iota_done"], 1)
            pool.iota(iota33[:], [[1, CH + 1]], base=0, channel_multiplier=0,
                      allow_small_or_imprecise_dtypes=True).then_inc(S["iota_done"], 1)
            pool.iota(iota_r[:], [[-1, CH]], base=CH - 1, channel_multiplier=0,
                      allow_small_or_imprecise_dtypes=True).then_inc(S["iota_done"], 1)
            pool.iota(iota8[:], [[1, NE_R]], base=0, channel_multiplier=0,
                      allow_small_or_imprecise_dtypes=True).then_inc(S["iota_done"], 1)
            pool.iota(it_s, [[0, T]], base=0, channel_multiplier=1).then_inc(S["iota_done"], 1)
            pool.iota(it_t, [[1, T]], base=0, channel_multiplier=0).then_inc(S["iota_done"], 1)
            pool.wait_ge(S["iota_done"], 9)
            pool.affine_select(out=ident[:], in_=ident[:], compare_op=ALU.not_equal, fill=1.0, base=0,
                               pattern=[[-1, P]], channel_multiplier=1).then_inc(S["iota_done"], 1)

            def powers(b):
                pool.wait_ge(S["ln1_ve"], b.n + 1)
                if reached(b.n - 1):
                    pool.wait_ge(S["ln1_xn"], b.n - 1)
                pool.tensor_tensor(rs1[b.par][:], ve1[b.par][:], nhalfc[:, 0:NT], ALU.pow).then_inc(S["ln1_pow"], 1)

            def mix(b):
                p = b.par
                pool.wait_ge(S["hT_done"], b.n + 1)
                if reached(b.n - 1):
                    pool.wait_ge(S["mix_qk"], 2 * (b.n - 1))
                    pool.wait_ge(S["mix_vg"], 2 * (b.n - 1))
                pool.tensor_tensor(dT[p][:], hT[p][:, 1:T + 1], hT[p][:, 0:T], ALU.subtract).then_inc(S["d_done"], 1)
                pool.wait_ge(S["d_done"], b.n + 1)
                pool.sem_inc(S["passed_pool"], 1)
                for n, c in enumerate("vg"):
                    pool.tensor_scalar(tv[p][:, n, :], dT[p][:], vec[:, MIX[c]:MIX[c] + 1], None, ALU.mult)\
                        .then_inc(S["tv_done"], 1)
                pool.wait_ge(S["tv_done"], 2 * b.n + 2)
                if reached(b.n - 1):
                    pool.wait_ge(S["proj_mm"], b.n - 1)
                for n, c in enumerate("vg"):
                    pool.tensor_tensor(xm[c][p][:], tv[p][:, n, :], hT[p][:, 0:T], ALU.add)\
                        .then_inc(S["mix_vg"], 1)

            def norms(b):
                pool.wait_ge(S["sq_done"], 4 * b.n + 4)
                if reached(b.n - 1):
                    pool.wait_ge(S["nre_done"], b.n - 1)
                pool.tensor_tensor(nrm[b.par][:], ssq[b.par][:], halfc[:], ALU.pow).then_inc(S["nrm_pow"], 1)

            def operands(b):
                p = b.par
                pool.wait_ge(S["qk_exp"], b.n + 1)
                if reached(b.n - 1):
                    pool.wait_ge(S["lvl_mm"], b.n - 1)
                for name, c, side, table in (("q16", 16, 1, pw[:, 1:17]), ("k16", 16, 0, pwr[:, 16:32]),
                                             ("q8", 8, 1, pw[:, 1:9]), ("k8", 8, 0, pwr[:, 24:32])):
                    src = qk[p][:, 0:T] if side else qk[p][:, T:2 * T]
                    half = slice(c, 2 * c) if side else slice(0, c)
                    pool.tensor_tensor(
                        lo[name][p][:].rearrange("p (n s) -> p n s", s=2 * c)[:, :, half],
                        src.rearrange("p (n s) -> p n s", s=2 * c)[:, :, half],
                        table.unsqueeze(1).broadcast_to([P, T // (2 * c), c]), ALU.mult).then_inc(S["lvl_q"], 1)
                pool.wait_ge(S["zscan"], b.n + 1)
                if reached(b.n - 1):
                    pool.wait_ge(S["bc_mm"], b.n - 1)
                pool.tensor_tensor(pz[p][:, LAGS:PZW], qk[p][:, 0:T], zc[p][:], ALU.mult).then_inc(S["qz_done"], 1)

            def add_lags(b):
                p = b.par
                pool.wait_ge(S["lag0"], b.n + 1)
                pool.wait_ge(S["lagmul"], (BL - 1) * (b.n + 1))
                for l in range(1, BL):
                    if l > 1:
                        pool.wait_ge(S["lagadd"], (BL - 1) * b.n + l - 1)
                    dst = slag[p][:].rearrange("p (n s) -> p n s", s=BL)[:, :, l:BL]
                    o = LAG_OFF[l] - T
                    src = tlag[:, o:o + NBL * (BL - l)].rearrange("p (n s) -> p n s", s=BL - l)
                    pool.tensor_tensor(dst, dst, src, ALU.add).then_inc(S["lagadd"], 1)

            def scale_wo(b):
                p = b.par
                pool.wait_ge(ld_rows[b.quad], 16 * b.fourth)
                if reached(b.n - 1):
                    pool.wait_ge(S["w_mm"], b.n - 1)
                pool.tensor_tensor(wog[p][:], WoT[:], rows[b.quad][:, 0, :], ALU.mult).then_inc(S["wog_done"], 1)

            def divide(b):
                p = b.par
                pool.wait_ge(S["ssum_done"], b.n + 1)
                pool.wait_ge(S["rden_done"], b.n + 1)
                if reached(b.n - 1):
                    pool.wait_ge(S["w_mm"], b.n - 1)
                pool.tensor_tensor(att[p][:], ssum[p][:], rden[p][:], ALU.mult).then_inc(S["att_done"], 1)

            def second_norm(b):
                p = b.par
                pool.wait_ge(S["ln2_ve"], b.n + 1)
                if reached(b.n - 1):
                    pool.wait_ge(S["ln2_xn"], b.n - 1)
                pool.tensor_tensor(rs2[p][:], ve2[p][:], nhalfc[:, 0:NT], ALU.pow).then_inc(S["ln2_pow"], 1)

            def modulate(b):
                p = b.par
                pool.wait_ge(S["ln2_xn"], b.n + 1)
                pool.tensor_tensor(xn2[p][:], xn2[p][:], rows[b.quad][:, 2, :].unsqueeze(1).broadcast_to([P, NT, C]),
                                   ALU.mult).then_inc(S["um_done"], 1)
                pool.wait_ge(S["um_done"], b.n + 1)
                if reached(b.n - 1):
                    pool.wait_ge(S["z_done"], b.n - 1)
                    pool.wait_ge(S["gu_done"], b.n - 1)
                pool.tensor_tensor(uu[p][:], xn2[p][:], rows[b.quad][:, 1, :].unsqueeze(1).broadcast_to([P, NT, C]),
                                   ALU.add).then_inc(S["u_done"], 1)
                pool.wait_ge(S["u_done"], b.n + 1)
                if reached(b.n - 1):
                    pool.wait_ge(S["fin_done"], b.n - 1)
                pool.tensor_tensor(gu[p][:], uu[p][:], rows[b.quad][:, 3, :].unsqueeze(1).broadcast_to([P, NT, C]),
                                   ALU.mult).then_inc(S["gu_done"], 1)
                pool.wait_ge(S["seu_done"], b.n + 1)
                if reached(b.n - 1):
                    pool.wait_ge(S["z_done"], b.n - 1)
                pool.tensor_tensor(ru[p][:], seu[p][:], nhalfc[:, 0:NT], ALU.pow).then_inc(S["u_pow"], 1)

            def step(st):
                for s, work in ((5, divide), (6, second_norm), (0, powers), (1, mix), (5, scale_wo),
                                (6, modulate), (2, norms), (3, operands), (4, add_lags)):
                    if st[s] is not None:
                        work(st[s])

            pool.wait_ge(S["ld_c0"], 48)
            pool.wait_ge(S["ld_c1"], 48)
            pool.wait_ge(S["tabs_done"], 2)
            pool.wait_ge(S["zero_done"], 10)
            pipeline(pool, step)

        @block.scalar
        def _(act):
            act.wait_ge(S["ld_c0"], 48)
            act.activation(silu_e[:], cTt[:], ACT.Exp, scale=-1.0).then_inc(S["silu_exp"], 1)
            act.activation(expd[:], vec[:, 0:1], ACT.Exp).then_inc(S["expd_done"], 1)
            act.wait_ge(S["nexpd_done"], 1)
            act.wait_ge(S["iota_done"], 9)
            act.activation(pw[:], iota33[:], ACT.Exp, scale=nexpd[:, 0:1]).then_inc(S["pw_done"], 1)
            act.activation(pwr[:], iota_r[:], ACT.Exp, scale=nexpd[:, 0:1]).then_inc(S["pw_done"], 1)

            def evac_h(b):
                p = b.par
                act.wait_ge(S["t1_mm"], b.n + 1)
                if reached(b.n - 1):
                    act.wait_ge(S["mix_qk"], 2 * (b.n - 1))
                    act.wait_ge(S["mix_vg"], 2 * (b.n - 1))
                act.activation(hT[p][:, 1:T + 1], psA[:, 0:T], ACT.Identity, scale=modT[:, 1, bass.ds(b.n, 1)],
                               bias=modT[:, 0, bass.ds(b.n, 1)]).then_inc(S["hT_done"], 1)

            def after_proj(b):
                p = b.par
                act.wait_ge(S["proj_mm"], b.n + 1)
                if reached(b.n - 1):
                    act.wait_ge(S["nrm_pow"], b.n - 1)
                for n in range(4):
                    if n or reached(b.n):
                        act.wait_ge(S["sq_done"], 4 * b.n + n)
                    act.activation(sq[:], psQK[:, n * C:(n + 1) * C], ACT.Square, scale=float(C) ** -0.5,
                                   accum_out=ssq[p][:, n:n + 1]).then_inc(S["sq_done"], 1)

            def evac_vg(b):
                act.wait_ge(S["proj_mm"], b.n + 1)
                if reached(b.n - 3):
                    act.wait_ge(S["den_done"], b.n - 3)
                act.activation(eg[b.quad][:], psV[:, T:2 * T], ACT.Exp, scale=-1.0).then_inc(S["eg_done"], 1)
                if reached(b.n - 3):
                    act.wait_ge(S["lagmul"], (BL - 1) * (b.n - 3))
                act.activation(vc[b.quad][:], psV[:, 0:T], ACT.Copy).then_inc(S["vc_done"], 1)

            def scale_qk(b):
                p = b.par
                act.wait_ge(S["rqk_done"], b.n + 1)
                if reached(b.n - 1):
                    act.wait_ge(S["t2_mm"], b.n - 1)
                for n in range(4):
                    act.activation(qn[p][:, n, :], psQK[:, n * C:(n + 1) * C], ACT.Copy, scale=rqk[p][:, n:n + 1])\
                       .then_inc(S["qn_done"], 1)

            def exp_qk(b):
                p = b.par
                act.wait_ge(S["t2_mm"], b.n + 1)
                if reached(b.n - 1):
                    act.wait_ge(S["lvl_q"], 4 * (b.n - 1))
                    act.wait_ge(S["qz_done"], b.n - 1)
                    act.wait_ge(S["lag_done"], BL * (b.n - 1))
                    act.wait_ge(S["q32_done"], b.n - 1)
                    act.wait_ge(S["k32_done"], b.n - 1)
                act.activation(qk[p][:], psT[:], ACT.Exp, scale=vec[:, 5:6]).then_inc(S["qk_exp"], 1)

            def copy_chunks(b):
                p = b.par
                act.wait_ge(S["u_mm"], b.n + 1)
                if reached(b.n - 1):
                    act.wait_ge(S["scan_done"], b.n - 1)
                act.activation(ue[p][:].rearrange("p e j -> p j e"),
                               psA[:, 0:D * (NCH - 1)].rearrange("p (j e) -> p j e", e=D), ACT.Copy)\
                   .then_inc(S["u_cp"], 1)
                act.wait_ge(S["lvl_mm"], b.n + 1)
                if reached(b.n - 1):
                    act.wait_ge(S["s_mm"], b.n - 1)
                act.activation(sc[p][:], psL[:, 0:T], ACT.Copy).then_inc(S["sc16"], 1)

            def square_u(b):
                p = b.par
                act.wait_ge(S["u_done"], b.n + 1)
                if reached(b.n - 1):
                    act.wait_ge(S["seu_done"], b.n - 1)
                for t in range(NT):
                    if t or reached(b.n):
                        act.wait_ge(S["squ_done"], NT * b.n + t)
                    act.activation(squ[:], uu[p][:, t, :], ACT.Square, scale=float(C) ** -0.5,
                                   accum_out=ssu[p][:, t:t + 1]).then_inc(S["squ_done"], 1)

            def evac_z(b):
                p = b.par
                act.wait_ge(S["t3_mm"], b.n + 1)
                act.activation(zTs[p][:], psA[:, 0:T], ACT.Copy).then_inc(S["zTs_done"], 1)
                act.activation(zT[:, bass.ds(b.n * T, T)], psA[:, 0:T], ACT.Copy).then_inc(S["zT_done"], 1)

            def step(st):
                for s, work in ((1, evac_h), (7, evac_z), (2, evac_vg), (2, after_proj), (6, square_u),
                                (3, exp_qk), (2, scale_qk), (4, copy_chunks)):
                    if st[s] is not None:
                        work(st[s])

            act.wait_ge(S["ld_c1"], 48)
            act.wait_ge(S["mod_done"], 2)
            act.wait_ge(S["zero_done"], 10)
            pipeline(act, step)

            act.wait_ge(S["lg_done"], NB)
            act.activation(score[:].rearrange("p t e -> p (t e)"), lgt[:], ACT.Sigmoid).then_inc(S["sig_done"], 1)
            act.wait_ge(S["ld_c2"], 32)
            def ffn_step(f):
                for e in range(NE):
                    k = NE * f + e
                    for c in range(HC):
                        act.wait_ge(S["h_mm"], HC * k + c + 1)
                        if reached(k - 1 if e >= 2 else NE * f):
                            act.wait_ge(S["y_mm"], k - 1 if e >= 2 else NE * f)
                        psH = psB[:, c * 512:(c + 1) * 512] if c < 3 else psL[:]
                        act.activation(hid[e % 2][:, c, :], psH, ACT.Gelu, bias=b1t[:, e * HC + c:e * HC + c + 1])\
                           .then_inc(S["gelu_done"], 1)

            ffn_step(0)
            with act.Fori(1, NF) as f:
                ffn_step(f)
        @block.vector
        def _(dve):
            for p in range(2):
                dve.memset(hT[p][:, 0:1], 0.0).then_inc(S["zero_done"], 1)
                for n in lo:
                    dve.memset(lo[n][p][:], 0.0).then_inc(S["zero_done"], 1)
            dve.wait_ge(S["silu_exp"], 1)
            dve.tensor_scalar_add(silu_r[:], silu_e[:], 1.0).then_inc(S["silu_one"], 1)
            dve.wait_ge(S["silu_one"], 1)
            dve.reciprocal(silu_e[:], silu_r[:]).then_inc(S["silu_rec"], 1)
            dve.wait_ge(S["silu_rec"], 1)
            dve.tensor_tensor(siluT[:], silu_e[:], cTt[:], ALU.mult).then_inc(S["silu_done"], 1)
            dve.wait_ge(S["expd_done"], 1)
            dve.tensor_scalar(nexpd[:], expd[:], 1e30, -1.0, ALU.min, ALU.mult).then_inc(S["nexpd_done"], 1)
            dve.wait_ge(S["iota_done"], 9)
            for h in range(NH):
                dve.memset(blkones[h * D:(h + 1) * D, h * D:(h + 1) * D], 1.0).then_inc(S["consts_v"], 1)
            dve.tensor_tensor(it_x, it_s, it_t, ALU.bitwise_xor).then_inc(S["mask_a"], 1)
            dve.wait_ge(S["mask_a"], 1)
            dve.tensor_scalar(it_m, it_x, 24, 8, ALU.bitwise_and, ALU.bitwise_xor).then_inc(S["mask_b"], 1)
            dve.tensor_scalar(it_y, it_t, 8, 8, ALU.bitwise_and, ALU.bitwise_xor).then_inc(S["mask_b"], 1)
            dve.wait_ge(S["mask_b"], 2)
            dve.tensor_tensor(it_x, it_m, it_y, ALU.bitwise_or).then_inc(S["mask_c"], 1)
            dve.wait_ge(S["mask_c"], 1)
            dve.tensor_scalar(mask8[:], it_x, 0, None, ALU.is_equal).then_inc(S["mask_d"], 1)
            dve.wait_ge(S["pw_done"], 2)
            dve.tensor_copy(wrow[:], pw[:, 1:2].broadcast_to([P, T])).then_inc(S["tabs_done"], 1)
            dve.memset(w32[:, :, 0:1], 0.0).then_inc(S["consts_v"], 1)
            dve.tensor_copy(w32[:, :, 1:NCH - 1], pw[:, CH:CH + 1].unsqueeze(2).broadcast_to([P, D, NCH - 2]))\
                .then_inc(S["tabs_done"], 1)
            dve.wait_ge(S["mod_mm"], 3)
            dve.tensor_copy(modT[:, 0, :], psA[:, 0:NB]).then_inc(S["mod_done"], 1)
            dve.tensor_scalar_add(modT[:, 1, :], psA[:, NB:2 * NB], 1.0).then_inc(S["mod_done"], 1)
            mg = psQK[0:NB, :].rearrange("b (k c) -> b k c", c=C)
            dve.tensor_copy(mrow[:, 1, :], mg[:, 1, :]).then_inc(S["mod_row_st"], 1)
            dve.tensor_scalar_add(mrow[:, 2, :], mg[:, 2, :], 1.0).then_inc(S["mod_row_st"], 1)
            dve.tensor_scalar(msgn[:], mg[:, 0:4:3, :], 0.0, 2.0, ALU.is_ge, ALU.mult).then_inc(S["mod_row_a"], 1)
            dve.tensor_scalar(mneg[:], mg[:, 0:4:3, :], -1.0, 0.25, ALU.mult, ALU.max).then_inc(S["mod_row_a"], 1)
            dve.wait_ge(S["mod_row_a"], 2)
            dve.tensor_tensor(mabs[:], mg[:, 0:4:3, :], mneg[:], ALU.max).then_inc(S["mod_row_b"], 1)
            dve.wait_ge(S["mod_row_b"], 1)
            dve.scalar_tensor_tensor(mrow[:, 0:4:3, :], msgn[:], 1.0, mabs[:], ALU.subtract, ALU.mult)\
                .then_inc(S["mod_row_st"], 1)
            dve.wait_ge(S["ld_w1"], 32)
            dve.tensor_scalar(W1[:, 0:NE_S, :], W1[:, 0:NE_S, :], vec[:, 6:7], None, ALU.mult)\
                .then_inc(S["w1g_done"], 1)
            dve.tensor_scalar(W1[:, NE_S:NE, :], W1[:, NE_S:NE, :], vec[:, 7:8], None, ALU.mult)\
                .then_inc(S["w1g_done"], 1)
            dve.wait_ge(S["consts_v"], NH + 1)
            dve.wait_ge(S["tabs_done"], 2)
            dve.wait_ge(S["mask_d"], 1)

            def stats(src, st, mv, ve, n, s_st, s_ag, s_ve, s_used):
                for t in range(NT):
                    dve.bn_stats(st[:, t, :], src[:, t, :]).then_inc(s_st, 1)
                dve.wait_ge(s_st, NT * n + NT)
                if reached(n - 1):
                    dve.wait_ge(s_used, n - 1)
                dve.sem_inc(S["passed_dve"], 1)
                for t in range(NT):
                    dve.bn_aggr(mv[:, t, :], st[:, t, :]).then_inc(s_ag, 1)
                dve.wait_ge(s_ag, NT * n + NT)
                dve.tensor_scalar_add(ve[:], mv[:, :, 1], LN_EPS).then_inc(s_ve, 1)

            def ln1_stats(b):
                p = b.par
                dve.wait_ge(ld_x[p], 16 * b.turn)
                stats(xb[p], st1[p], mv1[p], ve1[p], b.n, S["ln1_st"], S["ln1_ag"], S["ln1_ve"], S["ln1_xn"])

            def ln1_apply(b):
                p = b.par
                dve.wait_ge(S["ln1_pow"], b.n + 1)
                if reached(b.n - 1):
                    dve.wait_ge(S["t1_mm"], b.n - 1)
                for t in range(NT):
                    ins = dve.tensor_scalar(xn[p][:, t, :], xb[p][:, t, :], mv1[p][:, t, 0:1], rs1[p][:, t:t + 1],
                                            ALU.subtract, ALU.mult)
                ins.then_inc(S["ln1_xn"], 1)

            def mix_qk(b):
                p = b.par
                dve.wait_ge(S["d_done"], b.n + 1)
                if reached(b.n - 1):
                    dve.wait_ge(S["proj_mm"], b.n - 1)
                for c in "qk":
                    dve.scalar_tensor_tensor(xm[c][p][:], dT[p][:], vec[:, MIX[c]:MIX[c] + 1], hT[p][:, 0:T],
                                             ALU.mult, ALU.add).then_inc(S["mix_qk"], 1)

            def qk_norm(b):
                p = b.par
                dve.wait_ge(S["nrm_pow"], b.n + 1)
                dve.tensor_scalar_add(nre[p][:], nrm[p][:], RMS_EPS).then_inc(S["nre_done"], 1)
                dve.wait_ge(S["nre_done"], b.n + 1)
                if reached(b.n - 1):
                    dve.wait_ge(S["qn_done"], 4 * (b.n - 1))
                dve.reciprocal(rqk[p][:], nre[p][:]).then_inc(S["rqk_done"], 1)

            def turn_v(b):
                dve.wait_ge(S["vc_done"], b.n + 1)
                if reached(b.n - 3):
                    dve.wait_ge(S["s_mm"], b.n - 3)
                dve.transpose(vT[b.quad][:], vc[b.quad][:]).then_inc(S["vT_done"], 1)

            def operands(b):
                p = b.par
                q, k = qk[p][:, 0:T], qk[p][:, T:2 * T]
                dve.wait_ge(S["qk_exp"], b.n + 1)
                if reached(b.n - 1):
                    dve.wait_ge(S["qz_done"], b.n - 1)
                dve.tensor_tensor_scan(zc[p][:], wrow[:], k, 0.0, ALU.mult, ALU.add).then_inc(S["zscan"], 1)
                if reached(b.n):
                    dve.wait_ge(S["kT_done"], b.n)
                dve.tensor_tensor(k32[:].rearrange("p (n s) -> p n s", s=CH), k.rearrange("p (n s) -> p n s", s=CH),
                                  pwr[:].unsqueeze(1).broadcast_to([P, NCH, CH]), ALU.mult).then_inc(S["k32_done"], 1)
                if reached(b.n - 3):
                    dve.wait_ge(S["s_mm"], b.n - 3)
                dve.tensor_tensor(q32[b.quad][:].rearrange("p (n s) -> p n s", s=CH),
                                  q.rearrange("p (n s) -> p n s", s=CH),
                                  pw[:, 1:CH + 1].unsqueeze(1).broadcast_to([P, NCH, CH]), ALU.mult)\
                    .then_inc(S["q32_done"], 1)
                dve.wait_ge(S["k32_done"], b.n + 1)
                if reached(b.n - 1):
                    dve.wait_ge(S["u_mm"], b.n - 1)
                dve.transpose(kT[p][:], k32[:]).then_inc(S["kT_done"], 1)
                if reached(b.n - 1):
                    dve.wait_ge(S["bc_mm"], b.n - 1)
                q3 = q.rearrange("p (n s) -> p n s", s=BL)
                k3 = k.rearrange("p (n s) -> p n s", s=BL)
                for l in range(BL):
                    dst = pz[p][:, LAG_OFF[l]:LAG_OFF[l + 1]].rearrange("p (n s) -> p n s", s=BL - l)
                    if l == 0:
                        ins = dve.tensor_tensor(dst, q3, k3, ALU.mult)
                    else:
                        ins = dve.scalar_tensor_tensor(dst, k3[:, :, 0:BL - l], pw[:, l:l + 1], q3[:, :, l:BL],
                                                       ALU.mult, ALU.mult)
                    ins.then_inc(S["lag_done"], 1)

            def chunk_states(b):
                p = b.par
                dve.wait_ge(S["u_cp"], b.n + 1)
                if reached(b.n - 1):
                    dve.wait_ge(S["s_mm"], b.n - 1)
                dve.tensor_tensor_scan(Ast[p][:].rearrange("p e j -> p (e j)"), w32[:].rearrange("p e j -> p (e j)"),
                                       ue[p][:].rearrange("p e j -> p (e j)"), 0.0, ALU.mult, ALU.add)\
                    .then_inc(S["scan_done"], 1)
                dve.wait_ge(S["sc16"], b.n + 1)
                dve.sem_inc(S["passed_dve"], 1)
                dve.copy_predicated(sc[p][:], mask8[:], psL[:, T:2 * T]).then_inc(S["sc_done"], 1)

            def lag_sums(b):
                p = b.par
                dve.wait_ge(S["bc_mm"], b.n + 1)
                dve.wait_ge(S["eg_done"], b.n + 1)
                if reached(b.n - 1):
                    dve.wait_ge(S["rden_done"], b.n - 1)
                dve.scalar_tensor_tensor(den[p][:], eg[b.quad][:], 1.0, psB[:, LAGS:PZW], ALU.add, ALU.mult)\
                    .then_inc(S["den_done"], 1)
                if reached(b.n - 1):
                    dve.wait_ge(S["ssum_done"], b.n - 1)
                if reached(b.n):
                    dve.wait_ge(S["lagadd"], (BL - 1) * b.n)
                dve.wait_ge(S["vc_done"], b.n + 1)
                dve.tensor_tensor(slag[p][:], psB[:, 0:T], vc[b.quad][:], ALU.mult).then_inc(S["lag0"], 1)
                v3 = vc[b.quad][:].rearrange("p (n s) -> p n s", s=BL)
                for l in range(1, BL):
                    o = LAG_OFF[l]
                    n = NBL * (BL - l)
                    dve.tensor_tensor(tlag[:, o - T:o - T + n].rearrange("p (n s) -> p n s", s=BL - l),
                                      psB[:, o:o + n].rearrange("p (n s) -> p n s", s=BL - l),
                                      v3[:, :, 0:BL - l], ALU.mult).then_inc(S["lagmul"], 1)
                dve.wait_ge(S["den_done"], b.n + 1)
                if reached(b.n - 1):
                    dve.wait_ge(S["att_done"], b.n - 1)
                dve.reciprocal(rden[p][:], den[p][:]).then_inc(S["rden_done"], 1)

            def sum_up(b):
                p = b.par
                dve.wait_ge(S["s_mm"], b.n + 1)
                dve.wait_ge(S["lagadd"], (BL - 1) * (b.n + 1))
                if reached(b.n - 1):
                    dve.wait_ge(S["att_done"], b.n - 1)
                dve.tensor_tensor(ssum[p][:], psV[:, 0:T], slag[p][:], ALU.add).then_inc(S["ssum_done"], 1)

            def residual(b):
                p = b.par
                dve.wait_ge(S["w_mm"], b.n + 1)
                dve.wait_ge(ld_xr[p], 16 * b.turn)
                if reached(b.n - 1):
                    dve.wait_ge(S["fin_done"], b.n - 1)
                dve.tensor_tensor(x2[p][:].rearrange("p t c -> p (t c)"), psT[:, 0:T],
                                  xr[p][:].rearrange("p t c -> p (t c)"), ALU.add).then_inc(S["x2_done"], 1)
                dve.wait_ge(S["x2_done"], b.n + 1)
                stats(x2[p], st2[p], mv2[p], ve2[p], b.n, S["ln2_st"], S["ln2_ag"], S["ln2_ve"], S["ln2_xn"])

            def ln2_apply(b):
                p = b.par
                dve.wait_ge(S["ln2_pow"], b.n + 1)
                if reached(b.n - 1):
                    dve.wait_ge(S["u_done"], b.n - 1)
                for t in range(NT):
                    ins = dve.tensor_scalar(xn2[p][:, t, :], x2[p][:, t, :], mv2[p][:, t, 0:1], rs2[p][:, t:t + 1],
                                            ALU.subtract, ALU.mult)
                ins.then_inc(S["ln2_xn"], 1)

            def mean_square(b):
                p = b.par
                dve.wait_ge(S["squ_done"], NT * b.n + NT)
                if reached(b.n - 1):
                    dve.wait_ge(S["u_pow"], b.n - 1)
                dve.tensor_scalar_add(seu[p][:], ssu[p][:], FFN_EPS).then_inc(S["seu_done"], 1)

            def finish_u(b):
                p = b.par
                dve.wait_ge(S["gu_done"], b.n + 1)
                dve.tensor_tensor(Fin[:, bass.ds(b.n * (NT * C), NT * C)], gu[p][:].rearrange("p t c -> p (t c)"),
                                  x2[p][:].rearrange("p t c -> p (t c)"), ALU.add).then_inc(S["fin_done"], 1)
                dve.wait_ge(S["u_pow"], b.n + 1)
                if reached(b.n - 1):
                    dve.wait_ge(S["lg_done"], b.n - 1)
                dve.reciprocal(iru[b.quad][:], ru[p][:]).then_inc(S["iru_done"], 1)
                if reached(b.n - 1):
                    dve.wait_ge(S["t3_mm"], b.n - 1)
                for t in range(NT):
                    ins = dve.tensor_scalar(zz[p][:, t, :], uu[p][:, t, :], ru[p][:, t:t + 1], None, ALU.mult)
                ins.then_inc(S["z_done"], 1)

            def logits(b):
                dve.wait_ge(S["lg_mm"], b.n + 1)
                dve.wait_ge(S["iru_done"], b.n + 1)
                for t in range(NT):
                    ins = dve.tensor_scalar(lgt[:, bass.ds(b.n * (NT * NE_R) + t * NE_R, NE_R)],
                                            psB[:, LG + t * NE_R:LG + (t + 1) * NE_R], iru[b.quad][:, t:t + 1], None,
                                            ALU.mult)
                ins.then_inc(S["lg_done"], 1)

            def step(st):
                for s, work in ((5, sum_up), (6, residual), (0, ln1_stats), (1, mix_qk), (6, ln2_apply),
                                (0, ln1_apply), (8, logits), (2, turn_v), (6, mean_square), (2, qk_norm),
                                (6, finish_u), (3, operands), (4, chunk_states), (4, lag_sums)):
                    if st[s] is not None:
                        work(st[s])

            pipeline(dve, step)

            NTT = NB * NT
            dve.wait_ge(S["sig_done"], 1)
            dve.tensor_reduce(ssc[:], score[:], AX.X, ALU.add).then_inc(S["rt_a"], 1)
            for t in range(NTT):
                dve.max(top[:, t, :], score[:, t, :]).then_inc(S["rt_b"], 1)
            dve.wait_ge(S["rt_a"], 1)
            dve.reciprocal(rsc[:], ssc[:]).then_inc(S["rt_c"], 1)
            dve.wait_ge(S["rt_b"], NTT)
            for t in range(NTT):
                dve.max_index(topi[:, t, :], top[:, t, :], score[:, t, :]).then_inc(S["rt_d"], 1)
            dve.wait_ge(S["rt_c"], 1)
            dve.wait_ge(S["rt_d"], NTT)
            dve.tensor_copy(topf[:], topi[:, :, 0:2]).then_inc(S["rt_e"], 1)
            dve.tensor_tensor(gk[:], top[:, :, 0:2], rsc[:].unsqueeze(2).broadcast_to([P, NTT, 2]), ALU.mult)\
                .then_inc(S["rt_e"], 1)
            dve.wait_ge(S["rt_e"], 2)
            for n in range(2):
                dve.tensor_tensor(hot[:, n], iota8[:].unsqueeze(1).broadcast_to([P, NTT, NE_R]),
                                  topf[:, :, n:n + 1].broadcast_to([P, NTT, NE_R]), ALU.is_equal)\
                    .then_inc(S["rt_f"], 1)
            dve.wait_ge(S["rt_f"], 2)
            for n in range(2):
                dve.tensor_tensor(hot[:, n], hot[:, n], gk[:, :, n:n + 1].broadcast_to([P, NTT, NE_R]), ALU.mult)\
                    .then_inc(S["rt_g"], 1)
            dve.wait_ge(S["rt_g"], 2)
            dve.tensor_tensor(gate[:], hot[:, 0], hot[:, 1], ALU.add).then_inc(S["gate_done"], 1)
            dve.wait_ge(S["gate_done"], 1)

            dve.wait_ge(S["ld_c2"], 32)
            gate_f = gate[:].rearrange("p t e -> p (t e)")
            def ffn_step(f):
                for e in range(NE):
                    k = NE * f + e
                    psY = (psA, psQK)[e % 2]
                    dve.wait_ge(S["y_mm"], k + 1)
                    if reached(FS * (k - 1) if e >= 2 else FS * NE * f):
                        dve.wait_ge(S["acc_done"], FS * (k - 1) if e >= 2 else FS * NE * f)
                    dve.tensor_tensor(yb[e % 2][:], psY[:].rearrange("p (t c) -> p t c", c=C),
                                      b2t[:, e * C:(e + 1) * C].unsqueeze(1).broadcast_to([P, FS, C]), ALU.add)\
                        .then_inc(S["yb_done"], 1)
                    dve.wait_ge(S["yb_done"], k + 1)
                    if e:
                        dve.wait_ge(S["acc_done"], FS * k)
                    else:
                        if reached(f):
                            dve.wait_ge(S["fout_done"], f)
                    for t in range(FS):
                        if e == 0:
                            ins = dve.tensor_copy(acc[:, t, :], yb[0][:, t, :])
                        elif e < NE_S:
                            ins = dve.tensor_tensor(acc[:, t, :], acc[:, t, :], yb[e % 2][:, t, :], ALU.add)
                        else:
                            g = gate_f[:, bass.ds(f * (FS * NE_R) + (t * NE_R + e - NE_S), 1)]
                            ins = dve.scalar_tensor_tensor(acc[:, t, :], yb[e % 2][:, t, :], g, acc[:, t, :],
                                                           ALU.mult, ALU.add)
                        ins.then_inc(S["acc_done"], 1)
                dve.wait_ge(ld_g, 16 * (f + 1))
                dve.wait_ge(S["acc_done"], FS * NE * (f + 1))
                dve.tensor_tensor(acc[:].rearrange("p (b t) c -> p b t c", t=NT),
                                  acc[:].rearrange("p (b t) c -> p b t c", t=NT),
                                  grow[:].unsqueeze(2).broadcast_to([P, 2, NT, C]), ALU.mult)\
                    .then_inc(S["gacc_done"], 1)
                dve.wait_ge(S["gacc_done"], f + 1)
                if reached(16 * f):
                    dve.wait_ge(st_o, 16 * f)
                dve.tensor_tensor(fout[:].rearrange("p t c -> p (t c)"), acc[:].rearrange("p t c -> p (t c)"),
                                  Fin[:, bass.ds(f * (FS * C), FS * C)], ALU.add).then_inc(S["fout_done"], 1)

            ffn_step(0)
            with dve.Fori(1, NF) as f:
                ffn_step(f)
        @block.tensor
        def _(pe):
            def mm(dst, lhsT, rhs, start=True, stop=True):
                return pe.matmul(dst, lhsT, rhs, start=start, stop=stop)

            pe.wait_ge(S["ld_c0"], 48)
            pe.wait_ge(S["silu_done"], 1)
            mm(psA[:, 0:NB], wm[:, 0:C], siluT[:]).then_inc(S["mod_mm"], 1)
            mm(psA[:, NB:2 * NB], wm[:, C:2 * C], siluT[:]).then_inc(S["mod_mm"], 1)
            mm(psQK[0:NB, :], siluT[:], wm[:, 2 * C:6 * C]).then_inc(S["mod_mm"], 1)
            pe.wait_ge(S["iota_done"], 10)
            pe.wait_ge(S["ld_c1"], 48)
            pe.wait_ge(S["consts_v"], NH + 1)
            pe.wait_ge(S["mod_done"], 2)
            pe.wait_ge(S["mod_row_st"], 3)

            def turn_x(b):
                pe.wait_ge(S["ln1_xn"], b.n + 1)
                if reached(b.n):
                    pe.wait_ge(S["hT_done"], b.n)
                if reached(b.n - 3):
                    pe.wait_ge(S["u_cp"], b.n - 3)
                for t in range(NT):
                    ins = pe.transpose(psA[:, t * P:(t + 1) * P], xn[b.par][:, t, :], ident[:])
                ins.then_inc(S["t1_mm"], 1)

            def project(b):
                p = b.par
                pe.wait_ge(S["mix_qk"], 2 * b.n + 2)
                pe.wait_ge(S["mix_vg"], 2 * b.n + 2)
                if reached(b.n):
                    pe.wait_ge(S["qn_done"], 4 * b.n)
                    pe.wait_ge(S["vc_done"], b.n)
                    pe.wait_ge(S["eg_done"], b.n)
                if reached(b.n - 2):
                    pe.wait_ge(S["ssum_done"], b.n - 2)
                for n, c in enumerate("qk"):
                    for t in range(NT):
                        o = (2 * n + t) * C
                        mm(psQK[:, o:o + C], xm[c][p][:, t * P:(t + 1) * P], W4[:, n, :])
                mm(psV[:, 0:T], W4[:, 2, :], xm["v"][p][:])
                mm(psV[:, T:2 * T], W4[:, 3, :], xm["g"][p][:]).then_inc(S["proj_mm"], 1)

            def turn_qk(b):
                pe.wait_ge(S["qn_done"], 4 * b.n + 4)
                if reached(b.n - 2):
                    pe.wait_ge(S["x2_done"], b.n - 2)
                if reached(b.n):
                    pe.wait_ge(S["qk_exp"], b.n)
                for n in range(4):
                    ins = pe.transpose(psT[:, n * C:(n + 1) * C], qn[b.par][:, n, :], ident[:])
                ins.then_inc(S["t2_mm"], 1)

            def scores(b):
                p = b.par
                pe.wait_ge(S["kT_done"], b.n + 1)
                pe.wait_ge(S["vT_done"], b.n + 1)
                pe.wait_ge(S["hT_done"], least(b.n + 4))
                if reached(b.n - 2):
                    pe.wait_ge(S["zT_done"], b.n - 2)
                if reached(b.n):
                    pe.wait_ge(S["u_cp"], b.n)
                pe.sem_inc(S["passed_pe"], 1)
                for j in range(NCH - 1):
                    for h in range(NH):
                        hs = slice(h * D, (h + 1) * D)
                        ins = mm(psA[hs, j * D:(j + 1) * D], kT[p][hs, j * CH:(j + 1) * CH],
                                 vT[b.quad][hs, j * D:(j + 1) * D])
                ins.then_inc(S["u_mm"], 1)
                pe.wait_ge(S["lvl_q"], 4 * b.n + 4)
                if reached(b.n):
                    pe.wait_ge(S["sc_done"], b.n)
                pe.sem_inc(S["passed_pe"], 1)
                for n, (kk, qq) in enumerate((("k16", "q16"), ("k8", "q8"))):
                    for j in range(NCH):
                        for h in range(NH):
                            hs = slice(h * D, (h + 1) * D)
                            js = slice(j * CH, (j + 1) * CH)
                            ins = mm(psL[hs, n * T + j * CH:n * T + (j + 1) * CH], lo[kk][p][hs, js], lo[qq][p][hs, js])
                ins.then_inc(S["lvl_mm"], 1)
                if reached(b.n - 3):
                    pe.wait_ge(S["lg_done"], b.n - 3)
                pe.wait_ge(S["lag_done"], BL * b.n + BL)
                pe.wait_ge(S["qz_done"], b.n + 1)
                if reached(b.n):
                    pe.wait_ge(S["lagmul"], (BL - 1) * b.n)
                    pe.wait_ge(S["lag0"], b.n)
                    pe.wait_ge(S["den_done"], b.n)
                for o in range(0, PZW, 512):
                    n = min(512, PZW - o)
                    ins = mm(psB[:, o:o + n], blkones[:], pz[p][:, o:o + n])
                ins.then_inc(S["bc_mm"], 1)

            def attend(b):
                p = b.par
                pe.wait_ge(S["sc_done"], b.n + 1)
                pe.wait_ge(S["scan_done"], b.n + 1)
                pe.wait_ge(S["q32_done"], b.n + 1)
                pe.wait_ge(S["vc_done"], least(b.n + 3))
                pe.wait_ge(S["eg_done"], least(b.n + 3))
                if reached(b.n):
                    pe.wait_ge(S["ssum_done"], b.n)
                pe.sem_inc(S["passed_pe"], 1)
                st_j = Ast[p][:].rearrange("p e j -> p j e")
                for j in range(NCH):
                    js = slice(j * CH, (j + 1) * CH)
                    for h in range(NH):
                        hs = slice(h * D, (h + 1) * D)
                        dst = psV[hs, j * CH:(j + 1) * CH]
                        ins = mm(dst, vT[b.quad][hs, js], sc[p][hs, js], start=True, stop=(j == 0))
                        if j:
                            ins = mm(dst, st_j[hs, j - 1, :], q32[b.quad][hs, js], start=False, stop=True)
                ins.then_inc(S["s_mm"], 1)

            def out_proj(b):
                p = b.par
                pe.wait_ge(S["att_done"], b.n + 1)
                pe.wait_ge(S["wog_done"], b.n + 1)
                pe.wait_ge(S["qk_exp"], least(b.n + 3))
                if reached(b.n):
                    pe.wait_ge(S["x2_done"], b.n)
                for t in range(NT):
                    ins = mm(psT[:, t * P:(t + 1) * P], att[p][:, t * P:(t + 1) * P], wog[p][:])
                ins.then_inc(S["w_mm"], 1)

            def turn_z(b):
                pe.wait_ge(S["z_done"], b.n + 1)
                pe.wait_ge(S["hT_done"], least(b.n + 7))
                pe.wait_ge(S["u_cp"], least(b.n + 3))
                if reached(b.n):
                    pe.wait_ge(S["zT_done"], b.n)
                for t in range(NT):
                    ins = pe.transpose(psA[:, t * P:(t + 1) * P], zz[b.par][:, t, :], ident[:])
                ins.then_inc(S["t3_mm"], 1)

            def route(b):
                pe.wait_ge(S["zTs_done"], b.n + 1)
                pe.wait_ge(S["lagmul"], (BL - 1) * least(b.n + 4))
                if isinstance(b.n, int) and reached(b.n):
                    pe.wait_ge(S["lg_done"], b.n)
                for t in range(NT):
                    ins = mm(psB[:, LG + t * NE_R:LG + (t + 1) * NE_R], zTs[b.par][:, t * P:(t + 1) * P], centt[:])
                ins.then_inc(S["lg_mm"], 1)

            def step(st):
                for s, work in ((5, attend), (6, out_proj), (1, turn_x), (7, turn_z), (2, project), (3, turn_qk),
                                (8, route), (4, scores)):
                    if st[s] is not None:
                        work(st[s])

            pipeline(pe, step)

            pe.wait_ge(S["w1g_done"], 2)
            pe.wait_ge(S["ld_w2"], 32)
            pe.wait_ge(S["zT_done"], NB)
            pe.wait_ge(S["lg_done"], NB)
            pe.wait_ge(S["lagmul"], (BL - 1) * NB)

            def ffn_step(f):
                def up(e):
                    k = NE * f + e
                    for c in range(HC):
                        psH = psB[:, c * 512:(c + 1) * 512] if c < 3 else psL[:]
                        if reached(HC * (k - 1) + c + 1 if e else HC * k):
                            pe.wait_ge(S["gelu_done"], HC * (k - 1) + c + 1 if e else HC * k)
                        mm(psH, W1[:, e, c * P:(c + 1) * P], zT[:, bass.ds(f * FT, FT)]).then_inc(S["h_mm"], 1)

                def down(e):
                    k = NE * f + e
                    pe.wait_ge(S["gelu_done"], HC * (k + 1))
                    if e >= 2:
                        if reached(k - 1):
                            pe.wait_ge(S["yb_done"], k - 1)
                    else:
                        if reached(NE * f):
                            pe.wait_ge(S["yb_done"], NE * f)
                    psY = (psA, psQK)[e % 2]
                    for t in range(FS):
                        for c in range(HC):
                            ins = mm(psY[:, t * C:(t + 1) * C], hid[e % 2][:, c, t * P:(t + 1) * P], W2[:, e, c, :],
                                     start=(c == 0), stop=(c == HC - 1))
                    ins.then_inc(S["y_mm"], 1)

                up(0)
                for e in range(NE):
                    if e + 1 < NE:
                        up(e + 1)
                    down(e)

            ffn_step(0)
            with pe.Fori(1, NF) as f:
                ffn_step(f)
def least(n):
    return min(n, NB) if isinstance(n, int) else n


def launch_inputs(a):
    import numpy as np

    def flat(name):
        return a["L0_attn_" + name].reshape(-1)

    vecs = np.stack([flat("time_decay"), flat("mix_q"), flat("mix_k"), flat("mix_v"), flat("mix_g"),
                     flat("norm_scale"), a["L0_ffn_g_shared"], a["L0_ffn_g_routed"]], axis=1)
    b1 = np.concatenate([a["L0_ffn_b1_s"], a["L0_ffn_b1_r"]]).reshape(NE * HC, P).T
    b2 = np.concatenate([a["L0_ffn_b2_s"], a["L0_ffn_b2_r"]]).reshape(1, NE * C)
    return {
        "x": a["L0_attn_x"], "vecs": vecs, "cT": a["L0_c"].T,
        "wqkvg": np.stack([a["L0_attn_W" + n].T for n in "qkvg"], axis=1),
        "wo": a["L0_attn_Wo"].T, "wmod": a["L0_wmod"],
        "w1s": a["L0_ffn_W1_s"], "b1": b1, "w2s": a["L0_ffn_W2_s"], "b2": b2,
        "w1r": a["L0_ffn_W1_r"], "w2r": a["L0_ffn_W2_r"], "cent": a["L0_ffn_centroids"],
    }


def kernel(**inputs):
    import numpy as np
    import concourse.bacc as bacc
    from concourse.bass_utils import run_bass_kernel_spmd

    nc = bacc.Bacc("TRN2", target_bir_lowering=False, num_devices=1)
    given = launch_inputs({k: np.asarray(v) for k, v in inputs.items()})
    arrays, args = {}, {}
    for name, a in given.items():
        a = np.ascontiguousarray(a)
        arrays[f"in_{name}"] = a
        args[name] = nc.dram_tensor(f"in_{name}", a.shape, mybir.dt.from_np(a.dtype), kind="ExternalInput").ap()
    args["out"] = nc.dram_tensor("out_0", (NB, T, C), F32, kind="ExternalOutput").ap()
    adaln_kernel(nc, **args)
    r = run_bass_kernel_spmd(nc, [arrays], core_ids=[0])
    return r.results[0]["out_0"]
```

```python
import concourse.bass as bass
from concourse import mybir
from contextlib import ExitStack

F32 = mybir.dt.float32
I32 = mybir.dt.int32
U32 = mybir.dt.uint32
ALU = mybir.AluOpType
ACT = mybir.ActivationFunctionType
AX = mybir.AxisListType

P = 128
NB = 16
T = 256
C = 128
NH = 4
D = C // NH
NT = T // P
CH = 32
NCH = T // CH
BL = 8
NBL = T // BL
NE_S, NE_R = 2, 8
NE = NE_S + NE_R
HID = 512
HC = HID // P
FT = 512
NF = NB * T // FT
FS = FT // P
TOP = 2
RT = 256
RS = RT // P
NTILE = (TOP * NB * T + NE_R * (RT - 1)) // RT
SH_FIRST = 6
RW = C + 2
WR = HID + HC + HC * C

LN_EPS = 1e-5
RMS_EPS = 1e-8
FFN_EPS = 1.1920929e-07

LAG_OFF = [NBL * sum(BL - m for m in range(l)) for l in range(BL + 1)]
LAGS = LAG_OFF[BL]
PZW = LAGS + T
LG = PZW

STAGES = 9


def reached(n):
    return not isinstance(n, int) or n > 0


class Group:

    def __init__(self, m, r):
        self.n, self.par, self.turn = 2 * m + r, r, m + 1


def groups(eng, step, first, last):
    if first == 0:
        step(Group(0, 0))
        step(Group(0, 1))
        first = 2
    with eng.Fori(first // 2, last // 2) as m:
        step(Group(m, 0))
        step(Group(m, 1))


class Tile:

    def __init__(self, m, r):
        self.m, self.n, self.par, self.quad, self.fourth = m, 4 * m + r, r % 2, r, m + 1
        self.turn = 2 * m + r // 2 + 1


def routed_tiles(eng, step):
    for r in range(4):
        step(Tile(0, r))
    with eng.Fori(1, NTILE // 4) as m:
        for r in range(4):
            step(Tile(m, r))
    for r in range(NTILE % 4):
        step(Tile(NTILE // 4, r))


class Batch:

    def __init__(self, m, r):
        self.n, self.par, self.quad = 4 * m + r, r % 2, r
        self.turn = 2 * m + r // 2 + 1

        self.fourth = m + 1

    @staticmethod
    def at(n, loop=0):
        return Batch(loop + n // 4, n % 4)


def pipeline(eng, step):
    first = STAGES - 1
    loops = (NB - first) // 4

    def fixed(i):
        step([Batch.at(i - s) if 0 <= i - s < NB else None for s in range(STAGES)])

    for i in range(first):
        fixed(i)
    with eng.Fori(0, loops) as j:
        for i in range(first, first + 4):
            step([Batch.at(i - s, j) for s in range(STAGES)])
    for i in range(first + 4 * loops, NB + STAGES - 1):
        fixed(i)


def adaln_kernel(nc, x, vecs, cT, wqkvg, wo, wmod, w1s, b1, w2s, b2, wr, b2r, cent, out):
    ctx = ExitStack()
    with ctx:
        def sb(name, shape, dt=F32):
            return ctx.enter_context(nc.sbuf_tensor(name, shape, dt))

        def pb(name, shape):
            return ctx.enter_context(nc.psum_tensor(name, shape, F32))

        def sem(name):
            return ctx.enter_context(nc.semaphore(name))

        modrow_dram = nc.dram_tensor("modrow_dram", (NB, 4 * C), F32, kind="Internal").ap()

        z_dram = nc.dram_tensor("z_dram", (NB, T, C), F32, kind="Internal").ap()
        xs_dram = nc.dram_tensor("xs_dram", (NTILE * RT, RW), F32, kind="Internal").ap()
        ys_dram = nc.dram_tensor("ys_dram", (TOP * NB * T + NTILE * RT, C), F32, kind="Internal").ap()

        vec = sb("vec", [P, 8])
        MIX = {"q": 1, "k": 2, "v": 3, "g": 4}
        cTt = sb("cTt", [P, NB])
        silu_e = sb("silu_e", [P, NB])
        silu_r = sb("silu_r", [P, NB])
        siluT = sb("siluT", [P, NB])
        W4 = sb("W4", [P, 4, C])
        WoT = sb("WoT", [P, C])
        wm = sb("wm", [P, 6 * C])
        W1 = sb("W1", [P, NE_S, HID])
        W2 = sb("W2", [P, NE_S, HC, C])
        b1t = sb("b1t", [P, NE_S * HC])
        b2t = sb("b2t", [P, NE_S * C])
        zeros = sb("zeros", [P, RW])
        below = sb("below", [P, P])
        onesm = sb("onesm", [P, P])
        centt = sb("centt", [P, NE_R])
        ident = sb("ident", [P, P])
        blkones = sb("blkones", [P, P])
        iota33 = sb("iota33", [P, CH + 1])
        iota_r = sb("iota_r", [P, CH])
        iota8 = sb("iota8", [P, NE_R])
        iota_t = sb("iota_t", [P, NTILE])
        expd = sb("expd", [P, 1])
        nexpd = sb("nexpd", [P, 1])
        pw = sb("pw", [P, CH + 1])
        pwr = sb("pwr", [P, CH])
        wrow = sb("wrow", [P, T])
        w32 = sb("w32", [P, D, NCH - 1])
        halfc = sb("halfc", [P, 4])
        nhalfc = sb("nhalfc", [P, 4])
        mask8 = sb("mask8", [P, T], I32)
        modT = sb("modT", [P, 2, NB])
        mrow = sb("mrow", [NB, 4, C])
        msgn = sb("msgn", [NB, 2, C])
        mneg = sb("mneg", [NB, 2, C])
        mabs = sb("mabs", [NB, 2, C])

        Fin = sb("Fin", [P, NB * NT * C])
        zT = sb("zT", [P, NB * T])
        lgt = sb("lgt", [P, NB * NT * NE_R])

        scope = ExitStack()

        def pbuf(name, shape, dt=F32):
            return scope.enter_context(nc.sbuf_tensor(name, shape, dt))

        xb = [pbuf(f"xb{i}", [P, NT, C]) for i in range(2)]
        st1 = [pbuf(f"st1{i}", [P, NT, 6]) for i in range(2)]
        mv1 = [pbuf(f"mv1{i}", [P, NT, 2]) for i in range(2)]
        ve1 = [pbuf(f"ve1{i}", [P, NT]) for i in range(2)]
        rs1 = [pbuf(f"rs1{i}", [P, NT]) for i in range(2)]
        xn = [pbuf(f"xn{i}", [P, NT, C]) for i in range(2)]
        hT = [pbuf(f"hT{i}", [P, T + 1]) for i in range(2)]
        dT = [pbuf(f"dT{i}", [P, T]) for i in range(2)]
        tv = [pbuf(f"tv{i}", [P, 2, T]) for i in range(2)]
        xm = {c: [pbuf(f"xm{c}{i}", [P, T]) for i in range(2)] for c in "qkvg"}
        sq = pbuf("sq", [P, C])
        ssq = [pbuf(f"ssq{i}", [P, 4]) for i in range(2)]
        nrm = [pbuf(f"nrm{i}", [P, 4]) for i in range(2)]
        nre = [pbuf(f"nre{i}", [P, 4]) for i in range(2)]
        rqk = [pbuf(f"rqk{i}", [P, 4]) for i in range(2)]
        eg = [pbuf(f"eg{i}", [P, T]) for i in range(4)]
        vc = [pbuf(f"vc{i}", [P, T]) for i in range(4)]
        vT = [pbuf(f"vT{i}", [P, T]) for i in range(4)]
        qn = [pbuf(f"qn{i}", [P, 4, C]) for i in range(2)]
        qk = [pbuf(f"qk{i}", [P, 2 * T]) for i in range(2)]
        zc = [pbuf(f"zc{i}", [P, T]) for i in range(2)]
        pz = [pbuf(f"pz{i}", [P, PZW]) for i in range(2)]
        it_s, it_t, it_x, it_m, it_y = (pz[1][:, n * T:(n + 1) * T].bitcast(I32) for n in range(5))
        lo = {n: [pbuf(f"{n}{i}", [P, T]) for i in range(2)] for n in ("q8", "k8", "q16", "k16")}
        q32 = [pbuf(f"q32{i}", [P, T]) for i in range(4)]
        k32 = pbuf("k32", [P, T])
        kT = [pbuf(f"kT{i}", [P, T]) for i in range(2)]
        ue = [pbuf(f"ue{i}", [P, D, NCH - 1]) for i in range(2)]
        Ast = [pbuf(f"Ast{i}", [P, D, NCH - 1]) for i in range(2)]
        sc = [pbuf(f"sc{i}", [P, T]) for i in range(2)]
        den = [pbuf(f"den{i}", [P, T]) for i in range(2)]
        rden = [pbuf(f"rden{i}", [P, T]) for i in range(2)]
        slag = [pbuf(f"slag{i}", [P, T]) for i in range(2)]
        tlag = pbuf("tlag", [P, LAGS - T])
        ssum = [pbuf(f"ssum{i}", [P, T]) for i in range(2)]
        att = [pbuf(f"att{i}", [P, T]) for i in range(2)]
        rows = [pbuf(f"rows{i}", [P, 4, C]) for i in range(4)]
        wog = [pbuf(f"wog{i}", [P, C]) for i in range(2)]
        xr = [pbuf(f"xr{i}", [P, NT, C]) for i in range(2)]
        x2 = [pbuf(f"x2{i}", [P, NT, C]) for i in range(2)]
        st2 = [pbuf(f"st2{i}", [P, NT, 6]) for i in range(2)]
        mv2 = [pbuf(f"mv2{i}", [P, NT, 2]) for i in range(2)]
        ve2 = [pbuf(f"ve2{i}", [P, NT]) for i in range(2)]
        rs2 = [pbuf(f"rs2{i}", [P, NT]) for i in range(2)]
        xn2 = [pbuf(f"xn2{i}", [P, NT, C]) for i in range(2)]
        uu = [pbuf(f"uu{i}", [P, NT, C]) for i in range(2)]
        squ = pbuf("squ", [P, C])
        ssu = [pbuf(f"ssu{i}", [P, NT]) for i in range(2)]
        seu = [pbuf(f"seu{i}", [P, NT]) for i in range(2)]
        ru = [pbuf(f"ru{i}", [P, NT]) for i in range(2)]
        iru = [pbuf(f"iru{i}", [P, NT]) for i in range(4)]
        zz = [pbuf(f"zz{i}", [P, NT, C]) for i in range(2)]
        gu = [pbuf(f"gu{i}", [P, NT, C]) for i in range(2)]
        zTs = [pbuf(f"zTs{i}", [P, T]) for i in range(2)]

        scope.close()

        score = sb("score", [P, NB * NT, NE_R])
        ssc = sb("ssc", [P, NB * NT])
        rsc = sb("rsc", [P, NB * NT])
        top = sb("top", [P, NB * NT, 8])
        topi = sb("topi", [P, NB * NT, 8], U32)
        topf = sb("topf", [P, NB * NT, 2])
        hot = sb("hot", [P, TOP, NB * NT, NE_R])
        extra = sb("extra", [P, TOP, NB * NT, 2])
        own_row = sb("own_row", [P, TOP, NB * NT])
        empty_row = sb("empty_row", [P, NTILE * RS])
        hits = sb("hits", [P, NB * NT, NE_R])
        gk = sb("gk", [P, NB * NT, TOP])
        total = sb("total", [P, NE_R, NB * NT])
        inner = sb("inner", [P, NE_R, NB * NT])
        incl = sb("incl", [P, NE_R, NB * NT])
        base = sb("base", [P, NE_R, NB * NT])
        place = sb("place", [P, NB * NT, NE_R])
        hplace = sb("hplace", [P, TOP, NB * NT, NE_R])
        slotf = sb("slotf", [P, TOP, NB * NT])
        slot = sb("slot", [P, TOP, NB * NT], U32)
        tiles_i = sb("tiles_i", [P, 2, NE_R], I32)
        tiles = sb("tiles", [P, NE_R])
        ends = sb("ends", [P, NE_R])
        begins = sb("begins", [P, NE_R])
        past = sb("past", [P, NTILE, NE_R])
        expf = sb("expf", [P, NTILE])
        expert = sb("expert", [P, NTILE], I32)

        hid = [[sb(f"hid{e}{i}", [P, HC, FT]) for i in range(2)] for e in range(NE_S)]
        b2s = sb("b2s", [P, C])
        zg = [sb(f"zg{i}", [P, TOP, FS, RW]) for i in range(2)]
        slot_z = [sb(f"slot_z{i}", [P, TOP, FS], U32) for i in range(2)]
        wres = sb("wres", [P, NE_R, WR + C])
        wrt = [sb(f"wrt{i}", [P, WR + C]) for i in range(4)]
        xin = [sb(f"xin{i}", [P, RS, RW]) for i in range(4)]
        xT = [sb(f"xT{i}", [P, RT]) for i in range(2)]
        rhid = [sb(f"rhid{i}", [P, HC, RT]) for i in range(2)]
        yr = [sb(f"yr{i}", [P, RS, C]) for i in range(4)]
        yb = [sb(f"yb{i}", [P, RS, C]) for i in range(2)]
        yrow = [sb(f"yrow{i}", [P, RS], U32) for i in range(4)]
        yg = [z[:].rearrange("p n t r -> p (n t r)")[:, 0:FS * TOP * C].rearrange("p (t n c) -> p t n c", n=TOP, c=C)
              for z in zg]
        acc = [sb(f"acc{i}", [P, FS, C]) for i in range(2)]
        grow = sb("grow", [P, NB, C])

        psA = pb("psA", [P, 512])
        psQK = pb("psQK", [P, 512])
        psV = pb("psV", [P, 512])
        psT = pb("psT", [P, 512])
        psB = pb("psB", [P, 1536])
        psL = pb("psL", [P, 512])

        names = """passed_dve passed_pool passed_pe ld_w1 ld_w2 ld_c0 ld_c1 ld_c2 ld_out
            iota_done consts_v expd_done nexpd_done pw_done tabs_done silu_exp silu_step silu_done
            mask_step mod_mm mod_row_step mod_row_st mod_done zero_done w1g_done
            ln1_st ln1_ag ln1_ve ln1_pow ln1_xn t1_mm hT_done d_done mix_qk tv_done mix_vg
            proj_mm sq_done eg_done vc_done nrm_pow nre_done rqk_done qn_done vT_done
            t2_mm qk_exp zscan qz_done lag_done lvl_q k32_done q32_done kT_done
            u_mm lvl_mm bc_mm u_cp sc16 scan_done sc_done den_done rden_done lagmul lag0 lagadd
            s_mm ssum_done att_done wog_done
            w_mm x2_done ln2_st ln2_ag ln2_ve ln2_pow ln2_xn um_done u_done squ_done seu_done u_pow iru_done z_done gu_done fin_done
            t3_mm zTs_done zT_done lg_mm lg_done
            sig_done rt_sum rt_b rt_d rt_e rt_f hits_done rank_mm rows_iota ld_wr extra_done slots_copied zeros_done ld_g
            inner_done rank_step slot_done expert_step expert_done
            h_mm gelu_done y_mm shared_done b2s_done 
            xt_mm xT_done wrt_done rh_mm rgelu_done ry_mm yb_done yr_done shared_gb shared_sum sum_k sum_gb fout_done""".split()
        S = {n: sem(n) for n in names}
        ld_x = [sem(f"ld_x{i}") for i in range(2)]
        ld_xr = [sem(f"ld_xr{i}") for i in range(2)]
        ld_rows = [sem(f"ld_rows{i}") for i in range(4)]
        st_z = [sem(f"st_z{i}") for i in range(2)]
        ld_z = [sem(f"ld_z{i}") for i in range(2)]
        scat = [sem(f"scat{i}") for i in range(2)]
        ld_tile = [sem(f"ld_tile{i}") for i in range(4)]
        st_y = [sem(f"st_y{i}") for i in range(4)]
        ld_y = [sem(f"ld_y{i}") for i in range(2)]
        st_o = [sem(f"st_o{i}") for i in range(2)]

        def routed_h(i, c):
            bank = (psB[:, 0:512], psB[:, 512:1024], psB[:, 1024:1536], psL[:])[2 * i.par + c // 2]
            return bank[:, (c % 2) * RT:(c % 2 + 1) * RT]

        block = ctx.enter_context(nc.Block())

        @block.sync
        def _(sp):
            def load_x(b):
                if reached(b.n - 1):
                    sp.wait_ge(S["ln1_xn"], b.n - 1)
                sp.dma_start(xb[b.par][:], x[bass.ds(b.n, 1)].rearrange("o (t p) c -> p (o t) c", p=P))\
                  .then_inc(ld_x[b.par], 16)

            def load_xr(b):
                if reached(b.n - 1):
                    sp.wait_ge(S["x2_done"], b.n - 1)
                sp.dma_start(xr[b.par][:], x[bass.ds(b.n, 1)].rearrange("o (t p) c -> p (o t) c", p=P))\
                  .then_inc(ld_xr[b.par], 16)

            def load_rows(b):
                if reached(b.n - 3):
                    sp.wait_ge(S["gu_done"], b.n - 3)
                sp.dma_start(rows[b.quad][:].rearrange("p k c -> p (k c)"),
                             modrow_dram[bass.ds(b.n, 1), :].partition_broadcast(P)
                             .rearrange("p o n -> p (o n)")).then_inc(ld_rows[b.quad], 16)

            sp.dma_start(cTt[:], cT).then_inc(S["ld_c0"], 16)
            sp.dma_start(vec[:], vecs).then_inc(S["ld_c0"], 16)
            sp.dma_start(wm[:], wmod).then_inc(S["ld_c0"], 16)
            sp.dma_start(W4[:], wqkvg).then_inc(S["ld_c1"], 16)
            sp.dma_start(WoT[:], wo).then_inc(S["ld_c1"], 16)
            sp.dma_start(centt[:], cent).then_inc(S["ld_c1"], 16)
            sp.wait_ge(S["mod_row_st"], 3)
            sp.dma_start(modrow_dram, mrow[:].rearrange("b k c -> b (k c)")).then_inc(S["ld_out"], 16)
            sp.dma_start(b1t[:], b1).then_inc(S["ld_c2"], 16)
            sp.dma_start(b2t[:], b2.partition_broadcast(P)).then_inc(S["ld_c2"], 16)
            sp.dma_start(W1[:], w1s.rearrange("e c h -> c e h")).then_inc(S["ld_w1"], 16)
            sp.dma_start(W2[:], w2s.rearrange("e (k p) c -> p e k c", p=P)).then_inc(S["ld_w2"], 16)
            sp.wait_ge(S["zeros_done"], 1)
            sp.dma_start(xs_dram.rearrange("(n p) c -> p n c", p=P),
                         zeros[:].unsqueeze(1).broadcast_to([P, NTILE * RS, RW])).then_inc(S["ld_out"], 16)
            sp.wait_ge(S["ld_out"], 32)

            def store_z(b):
                sp.wait_ge(S["z_done"], b.n + 1)
                sp.dma_start(z_dram[bass.ds(b.n, 1)].rearrange("o (t p) c -> p (o t) c", p=P), zz[b.par][:])\
                  .then_inc(st_z[b.par], 16)

            def step(st):
                if st[0] is not None:
                    load_x(st[0])
                if st[5] is not None:
                    load_xr(st[5])
                if st[4] is not None:
                    load_rows(st[4])
                if st[7] is not None:
                    store_z(st[7])

            pipeline(sp, step)

            sp.wait_ge(S["lg_done"], NB)
            for p in range(2):
                sp.wait_ge(st_z[p], 16 * (NB // 2))
            sp.dma_start(grow[:], modrow_dram[:, 3 * C:4 * C].partition_broadcast(P)).then_inc(S["ld_g"], 16)

            sp.dma_start(wres[:, :, 0:WR], wr.rearrange("e p n -> p e n")).then_inc(S["ld_wr"], 16)
            sp.dma_start(wres[:, :, WR:WR + C], b2r.partition_broadcast(P)).then_inc(S["ld_wr"], 16)

            def load_z(g):
                if reached(g.n - 1):
                    sp.wait_ge(scat[g.par], 16 * TOP * FS * (g.turn - 1))
                for n in range(TOP):
                    sp.dma_start(zg[g.par][:, n, :, 0:C],
                                 z_dram[bass.ds(2 * g.n, 2)].rearrange("b (t p) c -> p (b t) c", p=P))\
                      .then_inc(ld_z[g.par], 16)

            groups(sp, load_z, 0, NF)

            for p in range(2):
                sp.wait_ge(scat[p], 16 * TOP * FS * (NF // 2))

            def load_tile(i):
                q = i.quad
                if reached(i.n - 3):
                    sp.wait_ge(S["yr_done"], i.n - 3)
                sp.dma_start(xin[q][:], xs_dram[bass.ds(i.n * RT, RT), :].rearrange("(k p) c -> p k c", p=P))\
                  .then_inc(ld_tile[q], 16)
            routed_tiles(sp, load_tile)

            for q in range(4):
                sp.wait_ge(st_y[q], 16 * RS * ((NTILE - q + 3) // 4))

            def finish(g):
                if reached(g.n - 1):
                    sp.wait_ge(S["sum_k"], g.n - 1)
                sp.dma_start(yg[g.par].rearrange("p t k c -> p t (k c)"),
                             ys_dram[bass.ds(g.n * (TOP * FT), TOP * FT), :]
                             .rearrange("(t p k) c -> p t (k c)", p=P, k=TOP)).then_inc(ld_y[g.par], 16)
                if not (isinstance(g.n, int) and g.n == 0):
                    store_out(g.n - 1, 1 - g.par)

            def store_out(n, par):
                sp.wait_ge(S["fout_done"], n + 1)
                sp.dma_start(out[bass.ds(2 * n, 2)].rearrange("b (t p) c -> p (b t) c", p=P),
                             Fin[:, bass.ds(n * (FS * C), FS * C)].rearrange("p (t c) -> p t c", c=C))\
                  .then_inc(st_o[par], 16)

            groups(sp, finish, 0, NF)
            store_out(NF - 1, 1)
            for p in range(2):
                sp.wait_ge(st_o[p], 16 * (NF // 2))

        @block.gpsimd
        def _(pool):
            pool.memset(ident[:], 0.0).then_inc(S["iota_done"], 1)
            pool.memset(blkones[:], 0.0).then_inc(S["iota_done"], 1)
            pool.memset(halfc[:], 0.5).then_inc(S["iota_done"], 1)
            pool.memset(nhalfc[:], -0.5).then_inc(S["iota_done"], 1)
            pool.iota(iota33[:], [[1, CH + 1]], base=0, channel_multiplier=0,
                      allow_small_or_imprecise_dtypes=True).then_inc(S["iota_done"], 1)
            pool.iota(iota_r[:], [[-1, CH]], base=CH - 1, channel_multiplier=0,
                      allow_small_or_imprecise_dtypes=True).then_inc(S["iota_done"], 1)
            pool.iota(iota8[:], [[1, NE_R]], base=0, channel_multiplier=0,
                      allow_small_or_imprecise_dtypes=True).then_inc(S["iota_done"], 1)
            pool.iota(iota_t[:], [[1, NTILE]], base=0, channel_multiplier=0,
                      allow_small_or_imprecise_dtypes=True).then_inc(S["iota_done"], 1)
            pool.memset(zeros[:], 0.0).then_inc(S["zeros_done"], 1)
            pool.memset(below[:], 1.0).then_inc(S["iota_done"], 1)
            pool.memset(onesm[:], 1.0).then_inc(S["iota_done"], 1)
            pool.iota(it_s, [[0, T]], base=0, channel_multiplier=1).then_inc(S["iota_done"], 1)
            pool.iota(it_t, [[1, T]], base=0, channel_multiplier=0).then_inc(S["iota_done"], 1)
            pool.wait_ge(S["iota_done"], 12)
            pool.affine_select(out=ident[:], in_=ident[:], compare_op=ALU.not_equal, fill=1.0, base=0,
                               pattern=[[-1, P]], channel_multiplier=1).then_inc(S["iota_done"], 1)
            pool.affine_select(out=below[:], in_=below[:], compare_op=ALU.is_gt, fill=0.0, base=0,
                               pattern=[[1, P]], channel_multiplier=-1).then_inc(S["iota_done"], 1)

            def powers(b):
                pool.wait_ge(S["ln1_ve"], b.n + 1)
                if reached(b.n - 1):
                    pool.wait_ge(S["ln1_xn"], b.n - 1)
                pool.tensor_tensor(rs1[b.par][:], ve1[b.par][:], nhalfc[:, 0:NT], ALU.pow).then_inc(S["ln1_pow"], 1)

            def mix(b):
                p = b.par
                pool.wait_ge(S["hT_done"], b.n + 1)
                if reached(b.n - 1):
                    pool.wait_ge(S["mix_qk"], 2 * (b.n - 1))
                    pool.wait_ge(S["mix_vg"], 2 * (b.n - 1))
                pool.tensor_tensor(dT[p][:], hT[p][:, 1:T + 1], hT[p][:, 0:T], ALU.subtract).then_inc(S["d_done"], 1)
                pool.wait_ge(S["d_done"], b.n + 1)
                pool.sem_inc(S["passed_pool"], 1)
                for n, c in enumerate("vg"):
                    pool.tensor_scalar(tv[p][:, n, :], dT[p][:], vec[:, MIX[c]:MIX[c] + 1], None, ALU.mult)\
                        .then_inc(S["tv_done"], 1)
                pool.wait_ge(S["tv_done"], 2 * b.n + 2)
                if reached(b.n - 1):
                    pool.wait_ge(S["proj_mm"], b.n - 1)
                for n, c in enumerate("vg"):
                    pool.tensor_tensor(xm[c][p][:], tv[p][:, n, :], hT[p][:, 0:T], ALU.add)\
                        .then_inc(S["mix_vg"], 1)

            def norms(b):
                pool.wait_ge(S["sq_done"], 4 * b.n + 4)
                if reached(b.n - 1):
                    pool.wait_ge(S["nre_done"], b.n - 1)
                pool.tensor_tensor(nrm[b.par][:], ssq[b.par][:], halfc[:], ALU.pow).then_inc(S["nrm_pow"], 1)

            def operands(b):
                p = b.par
                pool.wait_ge(S["qk_exp"], b.n + 1)
                if reached(b.n - 1):
                    pool.wait_ge(S["lvl_mm"], b.n - 1)
                for name, c, side, table in (("q16", 16, 1, pw[:, 1:17]), ("k16", 16, 0, pwr[:, 16:32]),
                                             ("q8", 8, 1, pw[:, 1:9]), ("k8", 8, 0, pwr[:, 24:32])):
                    src = qk[p][:, 0:T] if side else qk[p][:, T:2 * T]
                    half = slice(c, 2 * c) if side else slice(0, c)
                    pool.tensor_tensor(
                        lo[name][p][:].rearrange("p (n s) -> p n s", s=2 * c)[:, :, half],
                        src.rearrange("p (n s) -> p n s", s=2 * c)[:, :, half],
                        table.unsqueeze(1).broadcast_to([P, T // (2 * c), c]), ALU.mult).then_inc(S["lvl_q"], 1)
                pool.wait_ge(S["zscan"], b.n + 1)
                if reached(b.n - 1):
                    pool.wait_ge(S["bc_mm"], b.n - 1)
                pool.tensor_tensor(pz[p][:, LAGS:PZW], qk[p][:, 0:T], zc[p][:], ALU.mult).then_inc(S["qz_done"], 1)

            def add_lags(b):
                p = b.par
                pool.wait_ge(S["lag0"], b.n + 1)
                pool.wait_ge(S["lagmul"], (BL - 1) * (b.n + 1))
                for l in range(1, BL):
                    if l > 1:
                        pool.wait_ge(S["lagadd"], (BL - 1) * b.n + l - 1)
                    dst = slag[p][:].rearrange("p (n s) -> p n s", s=BL)[:, :, l:BL]
                    o = LAG_OFF[l] - T
                    src = tlag[:, o:o + NBL * (BL - l)].rearrange("p (n s) -> p n s", s=BL - l)
                    pool.tensor_tensor(dst, dst, src, ALU.add).then_inc(S["lagadd"], 1)

            def scale_wo(b):
                p = b.par
                pool.wait_ge(ld_rows[b.quad], 16 * b.fourth)
                if reached(b.n - 1):
                    pool.wait_ge(S["w_mm"], b.n - 1)
                pool.tensor_tensor(wog[p][:], WoT[:], rows[b.quad][:, 0, :], ALU.mult).then_inc(S["wog_done"], 1)

            def divide(b):
                p = b.par
                pool.wait_ge(S["ssum_done"], b.n + 1)
                pool.wait_ge(S["rden_done"], b.n + 1)
                if reached(b.n - 1):
                    pool.wait_ge(S["w_mm"], b.n - 1)
                pool.tensor_tensor(att[p][:], ssum[p][:], rden[p][:], ALU.mult).then_inc(S["att_done"], 1)

            def second_norm(b):
                p = b.par
                pool.wait_ge(S["ln2_ve"], b.n + 1)
                if reached(b.n - 1):
                    pool.wait_ge(S["ln2_xn"], b.n - 1)
                pool.tensor_tensor(rs2[p][:], ve2[p][:], nhalfc[:, 0:NT], ALU.pow).then_inc(S["ln2_pow"], 1)

            def modulate(b):
                p = b.par
                pool.wait_ge(S["ln2_xn"], b.n + 1)
                pool.tensor_tensor(xn2[p][:], xn2[p][:], rows[b.quad][:, 2, :].unsqueeze(1).broadcast_to([P, NT, C]),
                                   ALU.mult).then_inc(S["um_done"], 1)
                pool.wait_ge(S["um_done"], b.n + 1)
                if reached(b.n - 1):
                    pool.wait_ge(S["z_done"], b.n - 1)
                    pool.wait_ge(S["gu_done"], b.n - 1)
                pool.tensor_tensor(uu[p][:], xn2[p][:], rows[b.quad][:, 1, :].unsqueeze(1).broadcast_to([P, NT, C]),
                                   ALU.add).then_inc(S["u_done"], 1)
                pool.wait_ge(S["u_done"], b.n + 1)
                if reached(b.n - 1):
                    pool.wait_ge(S["fin_done"], b.n - 1)
                pool.tensor_tensor(gu[p][:], uu[p][:], rows[b.quad][:, 3, :].unsqueeze(1).broadcast_to([P, NT, C]),
                                   ALU.mult).then_inc(S["gu_done"], 1)
                pool.wait_ge(S["seu_done"], b.n + 1)
                if reached(b.n - 1):
                    pool.wait_ge(S["z_done"], b.n - 1)
                pool.tensor_tensor(ru[p][:], seu[p][:], nhalfc[:, 0:NT], ALU.pow).then_inc(S["u_pow"], 1)

            def step(st):
                for s, work in ((5, divide), (6, second_norm), (0, powers), (1, mix), (5, scale_wo),
                                (6, modulate), (2, norms), (3, operands), (4, add_lags)):
                    if st[s] is not None:
                        work(st[s])

            pool.wait_ge(S["ld_c0"], 48)
            pool.wait_ge(S["ld_c1"], 48)
            pool.wait_ge(S["tabs_done"], 2)
            pool.wait_ge(S["zero_done"], 10)
            pipeline(pool, step)

            pool.wait_ge(S["lg_done"], NB)
            pool.iota(own_row[:], [[1, TOP], [TOP * P, NB * NT]], base=-TOP * NB * T, channel_multiplier=TOP,
                      allow_small_or_imprecise_dtypes=True).then_inc(S["rows_iota"], 1)
            pool.iota(empty_row[:], [[P, NTILE * RS]], base=TOP * NB * T, channel_multiplier=1,
                      allow_small_or_imprecise_dtypes=True).then_inc(S["rows_iota"], 1)
            pool.wait_ge(S["slot_done"], 1)
            pool.wait_ge(S["extra_done"], 2)

            def scatter(g):
                p = g.par
                if reached(g.n - 1):
                    pool.wait_ge(scat[p], 16 * TOP * FS * (g.turn - 1))
                pool.sem_inc(S["passed_pool"], 1)
                pool.tensor_copy(slot_z[p][:], slot[:, :, bass.ds(g.n * FS, FS)]).then_inc(S["slots_copied"], 1)
                pool.tensor_copy(zg[p][:, :, :, C:RW], extra[:, :, bass.ds(g.n * FS, FS), :]).then_inc(S["slots_copied"], 1)
                pool.wait_ge(S["slots_copied"], 2 * (g.n + 1))
                pool.wait_ge(ld_z[p], 16 * TOP * g.turn)
                pool.sem_inc(S["passed_pool"], 1)
                for t in range(FS):
                    for n in range(TOP):
                        pool.indirect_dma_start(
                            out=xs_dram, out_offset=bass.IndirectOffsetOnAxis(ap=slot_z[p][:, n, t:t + 1], axis=0),
                            in_=zg[p][:, n, t, :], in_offset=None).then_inc(scat[p], 16)

            groups(pool, scatter, 0, NF)

            def return_tile(i):
                q = i.quad
                pool.wait_ge(S["yr_done"], i.n + 1)
                pool.sem_inc(S["passed_pool"], 1)
                for k in range(RS):
                    pool.indirect_dma_start(
                        out=ys_dram, out_offset=bass.IndirectOffsetOnAxis(ap=yrow[q][:, k:k + 1], axis=0),
                        in_=yr[q][:, k, :], in_offset=None).then_inc(st_y[q], 16)

            routed_tiles(pool, return_tile)

        @block.scalar
        def _(act):
            act.wait_ge(S["ld_c0"], 48)
            act.activation(silu_e[:], cTt[:], ACT.Exp, scale=-1.0).then_inc(S["silu_exp"], 1)
            act.activation(expd[:], vec[:, 0:1], ACT.Exp).then_inc(S["expd_done"], 1)
            act.wait_ge(S["nexpd_done"], 1)
            act.wait_ge(S["iota_done"], 12)
            act.activation(pw[:], iota33[:], ACT.Exp, scale=nexpd[:, 0:1]).then_inc(S["pw_done"], 1)
            act.activation(pwr[:], iota_r[:], ACT.Exp, scale=nexpd[:, 0:1]).then_inc(S["pw_done"], 1)

            def evac_h(b):
                p = b.par
                act.wait_ge(S["t1_mm"], b.n + 1)
                if reached(b.n - 1):
                    act.wait_ge(S["mix_qk"], 2 * (b.n - 1))
                    act.wait_ge(S["mix_vg"], 2 * (b.n - 1))
                act.activation(hT[p][:, 1:T + 1], psA[:, 0:T], ACT.Identity, scale=modT[:, 1, bass.ds(b.n, 1)],
                               bias=modT[:, 0, bass.ds(b.n, 1)]).then_inc(S["hT_done"], 1)

            def after_proj(b):
                p = b.par
                act.wait_ge(S["proj_mm"], b.n + 1)
                if reached(b.n - 1):
                    act.wait_ge(S["nrm_pow"], b.n - 1)
                for n in range(4):
                    if n or reached(b.n):
                        act.wait_ge(S["sq_done"], 4 * b.n + n)
                    act.activation(sq[:], psQK[:, n * C:(n + 1) * C], ACT.Square, scale=float(C) ** -0.5,
                                   accum_out=ssq[p][:, n:n + 1]).then_inc(S["sq_done"], 1)

            def evac_vg(b):
                act.wait_ge(S["proj_mm"], b.n + 1)
                if reached(b.n - 3):
                    act.wait_ge(S["den_done"], b.n - 3)
                act.activation(eg[b.quad][:], psV[:, T:2 * T], ACT.Exp, scale=-1.0).then_inc(S["eg_done"], 1)
                if reached(b.n - 3):
                    act.wait_ge(S["lagmul"], (BL - 1) * (b.n - 3))
                act.activation(vc[b.quad][:], psV[:, 0:T], ACT.Copy).then_inc(S["vc_done"], 1)

            def scale_qk(b):
                p = b.par
                act.wait_ge(S["rqk_done"], b.n + 1)
                if reached(b.n - 1):
                    act.wait_ge(S["t2_mm"], b.n - 1)
                for n in range(4):
                    act.activation(qn[p][:, n, :], psQK[:, n * C:(n + 1) * C], ACT.Copy, scale=rqk[p][:, n:n + 1])\
                       .then_inc(S["qn_done"], 1)

            def exp_qk(b):
                p = b.par
                act.wait_ge(S["t2_mm"], b.n + 1)
                if reached(b.n - 1):
                    act.wait_ge(S["lvl_q"], 4 * (b.n - 1))
                    act.wait_ge(S["qz_done"], b.n - 1)
                    act.wait_ge(S["lag_done"], BL * (b.n - 1))
                    act.wait_ge(S["q32_done"], b.n - 1)
                    act.wait_ge(S["k32_done"], b.n - 1)
                act.activation(qk[p][:], psT[:], ACT.Exp, scale=vec[:, 5:6]).then_inc(S["qk_exp"], 1)

            def copy_chunks(b):
                p = b.par
                act.wait_ge(S["u_mm"], b.n + 1)
                if reached(b.n - 1):
                    act.wait_ge(S["scan_done"], b.n - 1)
                act.activation(ue[p][:].rearrange("p e j -> p j e"),
                               psA[:, 0:D * (NCH - 1)].rearrange("p (j e) -> p j e", e=D), ACT.Copy)\
                   .then_inc(S["u_cp"], 1)
                act.wait_ge(S["lvl_mm"], b.n + 1)
                if reached(b.n - 1):
                    act.wait_ge(S["s_mm"], b.n - 1)
                act.activation(sc[p][:], psL[:, 0:T], ACT.Copy).then_inc(S["sc16"], 1)

            def square_u(b):
                p = b.par
                act.wait_ge(S["u_done"], b.n + 1)
                if reached(b.n - 1):
                    act.wait_ge(S["seu_done"], b.n - 1)
                for t in range(NT):
                    if t or reached(b.n):
                        act.wait_ge(S["squ_done"], NT * b.n + t)
                    act.activation(squ[:], uu[p][:, t, :], ACT.Square, scale=float(C) ** -0.5,
                                   accum_out=ssu[p][:, t:t + 1]).then_inc(S["squ_done"], 1)

            def evac_z(b):
                p = b.par
                act.wait_ge(S["t3_mm"], b.n + 1)
                act.activation(zTs[p][:], psA[:, 0:T], ACT.Copy).then_inc(S["zTs_done"], 1)
                act.activation(zT[:, bass.ds(b.n * T, T)], psA[:, 0:T], ACT.Copy).then_inc(S["zT_done"], 1)

            def step(st):
                for s, work in ((1, evac_h), (7, evac_z), (2, evac_vg), (2, after_proj), (6, square_u),
                                (3, exp_qk), (2, scale_qk), (4, copy_chunks)):
                    if st[s] is not None:
                        work(st[s])

            act.wait_ge(S["ld_c1"], 48)
            act.wait_ge(S["mod_done"], 2)
            act.wait_ge(S["zero_done"], 10)
            pipeline(act, step)

            act.wait_ge(S["lg_done"], NB)
            act.activation(score[:].rearrange("p t e -> p (t e)"), lgt[:], ACT.Sigmoid).then_inc(S["sig_done"], 1)
            act.wait_ge(S["ld_c2"], 32)

            def gelu_shared(g):
                for e in range(NE_S):
                    for c in range(HC):
                        act.wait_ge(S["h_mm"], HC * (NE_S * g.n + e) + c + 1)
                        if reached(g.n - 1):
                            act.wait_ge(S["y_mm"], g.n - 1)
                        psH = psB[:, c * 512:(c + 1) * 512] if c < 3 else psL[:]
                        act.activation(hid[e][g.par][:, c, :], psH, ACT.Gelu, bias=b1t[:, e * HC + c:e * HC + c + 1])\
                           .then_inc(S["gelu_done"], 1)

            groups(act, gelu_shared, 0, SH_FIRST)

            def gelu_routed(i):
                for half in range(2):
                    act.wait_ge(S["rh_mm"], 2 * i.n + half + 1)
                    if reached(i.n - 1):
                        act.wait_ge(S["ry_mm"], i.n - 1)
                    for c in (2 * half, 2 * half + 1):
                        ins = act.activation(rhid[i.par][:, c, :], routed_h(i, c), ACT.Gelu,
                                             bias=wrt[i.quad][:, HID + c:HID + c + 1])
                    ins.then_inc(S["rgelu_done"], 1)

            routed_tiles(act, gelu_routed)
            for n in range(SH_FIRST, NF):
                gelu_shared(Group(n // 2, n % 2))
        @block.vector
        def _(dve):
            for p in range(2):
                dve.memset(hT[p][:, 0:1], 0.0).then_inc(S["zero_done"], 1)
                for n in lo:
                    dve.memset(lo[n][p][:], 0.0).then_inc(S["zero_done"], 1)
            dve.wait_ge(S["silu_exp"], 1)
            dve.tensor_scalar_add(silu_r[:], silu_e[:], 1.0).then_inc(S["silu_step"], 1)
            dve.wait_ge(S["silu_step"], 1)
            dve.reciprocal(silu_e[:], silu_r[:]).then_inc(S["silu_step"], 1)
            dve.wait_ge(S["silu_step"], 2)
            dve.tensor_tensor(siluT[:], silu_e[:], cTt[:], ALU.mult).then_inc(S["silu_done"], 1)
            dve.wait_ge(S["expd_done"], 1)
            dve.tensor_scalar(nexpd[:], expd[:], 1e30, -1.0, ALU.min, ALU.mult).then_inc(S["nexpd_done"], 1)
            dve.wait_ge(S["iota_done"], 12)
            for h in range(NH):
                dve.memset(blkones[h * D:(h + 1) * D, h * D:(h + 1) * D], 1.0).then_inc(S["consts_v"], 1)
            dve.tensor_tensor(it_x, it_s, it_t, ALU.bitwise_xor).then_inc(S["mask_step"], 1)
            dve.wait_ge(S["mask_step"], 1)
            dve.tensor_scalar(it_m, it_x, 24, 8, ALU.bitwise_and, ALU.bitwise_xor).then_inc(S["mask_step"], 1)
            dve.tensor_scalar(it_y, it_t, 8, 8, ALU.bitwise_and, ALU.bitwise_xor).then_inc(S["mask_step"], 1)
            dve.wait_ge(S["mask_step"], 3)
            dve.tensor_tensor(it_x, it_m, it_y, ALU.bitwise_or).then_inc(S["mask_step"], 1)
            dve.wait_ge(S["mask_step"], 4)
            dve.tensor_scalar(mask8[:], it_x, 0, None, ALU.is_equal).then_inc(S["mask_step"], 1)
            dve.wait_ge(S["pw_done"], 2)
            dve.tensor_copy(wrow[:], pw[:, 1:2].broadcast_to([P, T])).then_inc(S["tabs_done"], 1)
            dve.memset(w32[:, :, 0:1], 0.0).then_inc(S["consts_v"], 1)
            dve.tensor_copy(w32[:, :, 1:NCH - 1], pw[:, CH:CH + 1].unsqueeze(2).broadcast_to([P, D, NCH - 2]))\
                .then_inc(S["tabs_done"], 1)
            dve.wait_ge(S["mod_mm"], 3)
            dve.tensor_copy(modT[:, 0, :], psA[:, 0:NB]).then_inc(S["mod_done"], 1)
            dve.tensor_scalar_add(modT[:, 1, :], psA[:, NB:2 * NB], 1.0).then_inc(S["mod_done"], 1)
            mg = psQK[0:NB, :].rearrange("b (k c) -> b k c", c=C)
            dve.tensor_copy(mrow[:, 1, :], mg[:, 1, :]).then_inc(S["mod_row_st"], 1)
            dve.tensor_scalar_add(mrow[:, 2, :], mg[:, 2, :], 1.0).then_inc(S["mod_row_st"], 1)
            dve.tensor_scalar(msgn[:], mg[:, 0:4:3, :], 0.0, 2.0, ALU.is_ge, ALU.mult).then_inc(S["mod_row_step"], 1)
            dve.tensor_scalar(mneg[:], mg[:, 0:4:3, :], -1.0, 0.25, ALU.mult, ALU.max).then_inc(S["mod_row_step"], 1)
            dve.wait_ge(S["mod_row_step"], 2)
            dve.tensor_tensor(mabs[:], mg[:, 0:4:3, :], mneg[:], ALU.max).then_inc(S["mod_row_step"], 1)
            dve.wait_ge(S["mod_row_step"], 3)
            dve.scalar_tensor_tensor(mrow[:, 0:4:3, :], msgn[:], 1.0, mabs[:], ALU.subtract, ALU.mult)\
                .then_inc(S["mod_row_st"], 1)
            dve.wait_ge(S["consts_v"], NH + 1)
            dve.wait_ge(S["tabs_done"], 2)
            dve.wait_ge(S["mask_step"], 5)

            def stats(src, st, mv, ve, n, s_st, s_ag, s_ve, s_used):
                for t in range(NT):
                    dve.bn_stats(st[:, t, :], src[:, t, :]).then_inc(s_st, 1)
                dve.wait_ge(s_st, NT * n + NT)
                if reached(n - 1):
                    dve.wait_ge(s_used, n - 1)
                dve.sem_inc(S["passed_dve"], 1)
                for t in range(NT):
                    dve.bn_aggr(mv[:, t, :], st[:, t, :]).then_inc(s_ag, 1)
                dve.wait_ge(s_ag, NT * n + NT)
                dve.tensor_scalar_add(ve[:], mv[:, :, 1], LN_EPS).then_inc(s_ve, 1)

            def ln1_stats(b):
                p = b.par
                dve.wait_ge(ld_x[p], 16 * b.turn)
                stats(xb[p], st1[p], mv1[p], ve1[p], b.n, S["ln1_st"], S["ln1_ag"], S["ln1_ve"], S["ln1_xn"])

            def ln1_apply(b):
                p = b.par
                dve.wait_ge(S["ln1_pow"], b.n + 1)
                if reached(b.n - 1):
                    dve.wait_ge(S["t1_mm"], b.n - 1)
                for t in range(NT):
                    ins = dve.tensor_scalar(xn[p][:, t, :], xb[p][:, t, :], mv1[p][:, t, 0:1], rs1[p][:, t:t + 1],
                                            ALU.subtract, ALU.mult)
                ins.then_inc(S["ln1_xn"], 1)

            def mix_qk(b):
                p = b.par
                dve.wait_ge(S["d_done"], b.n + 1)
                if reached(b.n - 1):
                    dve.wait_ge(S["proj_mm"], b.n - 1)
                for c in "qk":
                    dve.scalar_tensor_tensor(xm[c][p][:], dT[p][:], vec[:, MIX[c]:MIX[c] + 1], hT[p][:, 0:T],
                                             ALU.mult, ALU.add).then_inc(S["mix_qk"], 1)

            def qk_norm(b):
                p = b.par
                dve.wait_ge(S["nrm_pow"], b.n + 1)
                dve.tensor_scalar_add(nre[p][:], nrm[p][:], RMS_EPS).then_inc(S["nre_done"], 1)
                dve.wait_ge(S["nre_done"], b.n + 1)
                if reached(b.n - 1):
                    dve.wait_ge(S["qn_done"], 4 * (b.n - 1))
                dve.reciprocal(rqk[p][:], nre[p][:]).then_inc(S["rqk_done"], 1)

            def turn_v(b):
                dve.wait_ge(S["vc_done"], b.n + 1)
                if reached(b.n - 3):
                    dve.wait_ge(S["s_mm"], b.n - 3)
                dve.transpose(vT[b.quad][:], vc[b.quad][:]).then_inc(S["vT_done"], 1)

            def operands(b):
                p = b.par
                q, k = qk[p][:, 0:T], qk[p][:, T:2 * T]
                dve.wait_ge(S["qk_exp"], b.n + 1)
                if reached(b.n - 1):
                    dve.wait_ge(S["qz_done"], b.n - 1)
                dve.tensor_tensor_scan(zc[p][:], wrow[:], k, 0.0, ALU.mult, ALU.add).then_inc(S["zscan"], 1)
                if reached(b.n):
                    dve.wait_ge(S["kT_done"], b.n)
                dve.tensor_tensor(k32[:].rearrange("p (n s) -> p n s", s=CH), k.rearrange("p (n s) -> p n s", s=CH),
                                  pwr[:].unsqueeze(1).broadcast_to([P, NCH, CH]), ALU.mult).then_inc(S["k32_done"], 1)
                if reached(b.n - 3):
                    dve.wait_ge(S["s_mm"], b.n - 3)
                dve.tensor_tensor(q32[b.quad][:].rearrange("p (n s) -> p n s", s=CH),
                                  q.rearrange("p (n s) -> p n s", s=CH),
                                  pw[:, 1:CH + 1].unsqueeze(1).broadcast_to([P, NCH, CH]), ALU.mult)\
                    .then_inc(S["q32_done"], 1)
                dve.wait_ge(S["k32_done"], b.n + 1)
                if reached(b.n - 1):
                    dve.wait_ge(S["u_mm"], b.n - 1)
                dve.transpose(kT[p][:], k32[:]).then_inc(S["kT_done"], 1)
                if reached(b.n - 1):
                    dve.wait_ge(S["bc_mm"], b.n - 1)
                q3 = q.rearrange("p (n s) -> p n s", s=BL)
                k3 = k.rearrange("p (n s) -> p n s", s=BL)
                for l in range(BL):
                    dst = pz[p][:, LAG_OFF[l]:LAG_OFF[l + 1]].rearrange("p (n s) -> p n s", s=BL - l)
                    if l == 0:
                        ins = dve.tensor_tensor(dst, q3, k3, ALU.mult)
                    else:
                        ins = dve.scalar_tensor_tensor(dst, k3[:, :, 0:BL - l], pw[:, l:l + 1], q3[:, :, l:BL],
                                                       ALU.mult, ALU.mult)
                    ins.then_inc(S["lag_done"], 1)

            def chunk_states(b):
                p = b.par
                dve.wait_ge(S["u_cp"], b.n + 1)
                if reached(b.n - 1):
                    dve.wait_ge(S["s_mm"], b.n - 1)
                dve.tensor_tensor_scan(Ast[p][:].rearrange("p e j -> p (e j)"), w32[:].rearrange("p e j -> p (e j)"),
                                       ue[p][:].rearrange("p e j -> p (e j)"), 0.0, ALU.mult, ALU.add)\
                    .then_inc(S["scan_done"], 1)
                dve.wait_ge(S["sc16"], b.n + 1)
                dve.sem_inc(S["passed_dve"], 1)
                dve.copy_predicated(sc[p][:], mask8[:], psL[:, T:2 * T]).then_inc(S["sc_done"], 1)

            def lag_sums(b):
                p = b.par
                dve.wait_ge(S["bc_mm"], b.n + 1)
                dve.wait_ge(S["eg_done"], b.n + 1)
                if reached(b.n - 1):
                    dve.wait_ge(S["rden_done"], b.n - 1)
                dve.scalar_tensor_tensor(den[p][:], eg[b.quad][:], 1.0, psB[:, LAGS:PZW], ALU.add, ALU.mult)\
                    .then_inc(S["den_done"], 1)
                if reached(b.n - 1):
                    dve.wait_ge(S["ssum_done"], b.n - 1)
                if reached(b.n):
                    dve.wait_ge(S["lagadd"], (BL - 1) * b.n)
                dve.wait_ge(S["vc_done"], b.n + 1)
                dve.tensor_tensor(slag[p][:], psB[:, 0:T], vc[b.quad][:], ALU.mult).then_inc(S["lag0"], 1)
                v3 = vc[b.quad][:].rearrange("p (n s) -> p n s", s=BL)
                for l in range(1, BL):
                    o = LAG_OFF[l]
                    n = NBL * (BL - l)
                    dve.tensor_tensor(tlag[:, o - T:o - T + n].rearrange("p (n s) -> p n s", s=BL - l),
                                      psB[:, o:o + n].rearrange("p (n s) -> p n s", s=BL - l),
                                      v3[:, :, 0:BL - l], ALU.mult).then_inc(S["lagmul"], 1)
                dve.wait_ge(S["den_done"], b.n + 1)
                if reached(b.n - 1):
                    dve.wait_ge(S["att_done"], b.n - 1)
                dve.reciprocal(rden[p][:], den[p][:]).then_inc(S["rden_done"], 1)

            def sum_up(b):
                p = b.par
                dve.wait_ge(S["s_mm"], b.n + 1)
                dve.wait_ge(S["lagadd"], (BL - 1) * (b.n + 1))
                if reached(b.n - 1):
                    dve.wait_ge(S["att_done"], b.n - 1)
                dve.tensor_tensor(ssum[p][:], psV[:, 0:T], slag[p][:], ALU.add).then_inc(S["ssum_done"], 1)

            def residual(b):
                p = b.par
                dve.wait_ge(S["w_mm"], b.n + 1)
                dve.wait_ge(ld_xr[p], 16 * b.turn)
                if reached(b.n - 1):
                    dve.wait_ge(S["fin_done"], b.n - 1)
                dve.tensor_tensor(x2[p][:].rearrange("p t c -> p (t c)"), psT[:, 0:T],
                                  xr[p][:].rearrange("p t c -> p (t c)"), ALU.add).then_inc(S["x2_done"], 1)
                dve.wait_ge(S["x2_done"], b.n + 1)
                stats(x2[p], st2[p], mv2[p], ve2[p], b.n, S["ln2_st"], S["ln2_ag"], S["ln2_ve"], S["ln2_xn"])

            def ln2_apply(b):
                p = b.par
                dve.wait_ge(S["ln2_pow"], b.n + 1)
                if reached(b.n - 1):
                    dve.wait_ge(S["u_done"], b.n - 1)
                for t in range(NT):
                    ins = dve.tensor_scalar(xn2[p][:, t, :], x2[p][:, t, :], mv2[p][:, t, 0:1], rs2[p][:, t:t + 1],
                                            ALU.subtract, ALU.mult)
                ins.then_inc(S["ln2_xn"], 1)

            def mean_square(b):
                p = b.par
                dve.wait_ge(S["squ_done"], NT * b.n + NT)
                if reached(b.n - 1):
                    dve.wait_ge(S["u_pow"], b.n - 1)
                dve.tensor_scalar_add(seu[p][:], ssu[p][:], FFN_EPS).then_inc(S["seu_done"], 1)

            def finish_u(b):
                p = b.par
                dve.wait_ge(S["gu_done"], b.n + 1)
                dve.tensor_tensor(Fin[:, bass.ds(b.n * (NT * C), NT * C)], gu[p][:].rearrange("p t c -> p (t c)"),
                                  x2[p][:].rearrange("p t c -> p (t c)"), ALU.add).then_inc(S["fin_done"], 1)
                dve.wait_ge(S["u_pow"], b.n + 1)
                if reached(b.n - 1):
                    dve.wait_ge(S["lg_done"], b.n - 1)
                dve.reciprocal(iru[b.quad][:], ru[p][:]).then_inc(S["iru_done"], 1)
                if reached(b.n - 1):
                    dve.wait_ge(S["t3_mm"], b.n - 1)
                    dve.wait_ge(st_z[p], 16 * (b.turn - 1))
                for t in range(NT):
                    ins = dve.tensor_scalar(zz[p][:, t, :], uu[p][:, t, :], ru[p][:, t:t + 1], None, ALU.mult)
                ins.then_inc(S["z_done"], 1)

            def logits(b):
                dve.wait_ge(S["lg_mm"], b.n + 1)
                dve.wait_ge(S["iru_done"], b.n + 1)
                for t in range(NT):
                    ins = dve.tensor_scalar(lgt[:, bass.ds(b.n * (NT * NE_R) + t * NE_R, NE_R)],
                                            psB[:, LG + t * NE_R:LG + (t + 1) * NE_R], iru[b.quad][:, t:t + 1], None,
                                            ALU.mult)
                ins.then_inc(S["lg_done"], 1)

            def step(st):
                for s, work in ((5, sum_up), (6, residual), (0, ln1_stats), (1, mix_qk), (6, ln2_apply),
                                (0, ln1_apply), (8, logits), (2, turn_v), (6, mean_square), (2, qk_norm),
                                (6, finish_u), (3, operands), (4, chunk_states), (4, lag_sums)):
                    if st[s] is not None:
                        work(st[s])

            pipeline(dve, step)

            NTT = NB * NT
            dve.wait_ge(S["ld_w1"], 16)
            dve.tensor_scalar(W1[:], W1[:], vec[:, 6:7], None, ALU.mult).then_inc(S["w1g_done"], 1)
            dve.wait_ge(S["sig_done"], 1)
            dve.tensor_reduce(ssc[:], score[:], AX.X, ALU.add).then_inc(S["rt_sum"], 1)
            for t in range(NTT):
                dve.max(top[:, t, :], score[:, t, :]).then_inc(S["rt_b"], 1)
            dve.wait_ge(S["rt_sum"], 1)
            dve.reciprocal(rsc[:], ssc[:]).then_inc(S["rt_sum"], 1)
            dve.wait_ge(S["rt_b"], NTT)
            for t in range(NTT):
                dve.max_index(topi[:, t, :], top[:, t, :], score[:, t, :]).then_inc(S["rt_d"], 1)
            dve.wait_ge(S["rt_sum"], 2)
            dve.wait_ge(S["rt_d"], NTT)
            dve.tensor_copy(topf[:], topi[:, :, 0:2]).then_inc(S["rt_e"], 1)
            dve.tensor_tensor(gk[:], top[:, :, 0:2], rsc[:].unsqueeze(2).broadcast_to([P, NTT, 2]), ALU.mult)\
                .then_inc(S["rt_e"], 1)
            dve.wait_ge(S["rt_e"], 2)
            for n in range(2):
                dve.tensor_tensor(hot[:, n], iota8[:].unsqueeze(1).broadcast_to([P, NTT, NE_R]),
                                  topf[:, :, n:n + 1].broadcast_to([P, NTT, NE_R]), ALU.is_equal)\
                    .then_inc(S["rt_f"], 1)
            dve.wait_ge(S["rt_f"], 2)
            dve.tensor_tensor(hits[:], hot[:, 0], hot[:, 1], ALU.add).then_inc(S["hits_done"], 1)
            dve.tensor_copy(extra[:, :, :, 0], gk[:].rearrange("p t n -> p n t")).then_inc(S["extra_done"], 1)
            dve.wait_ge(S["ld_c2"], 32)
            dve.tensor_tensor(b2s[:], b2t[:, 0:C], b2t[:, C:2 * C], ALU.add).then_inc(S["b2s_done"], 1)
            dve.memset(inner[:], 1.0).then_inc(S["inner_done"], 1)
            dve.wait_ge(S["inner_done"], 1)
            dve.memset(inner[:, :, 0:1], 0.0).then_inc(S["inner_done"], 1)

            NR = NTT * NE_R
            dve.wait_ge(S["rank_mm"], 1)
            dve.tensor_copy(total[:], psV[:, NR:2 * NR].rearrange("p (t e) -> p e t", e=NE_R)).then_inc(S["rank_step"], 1)
            dve.wait_ge(S["rank_step"], 1)
            dve.wait_ge(S["inner_done"], 2)
            dve.tensor_tensor_scan(incl[:].rearrange("p e t -> p (e t)"), inner[:].rearrange("p e t -> p (e t)"),
                                   total[:].rearrange("p e t -> p (e t)"), 0.0, ALU.mult, ALU.add)\
                .then_inc(S["rank_step"], 1)
            dve.wait_ge(S["rank_step"], 2)
            dve.tensor_scalar(tiles_i[:, 0, :], incl[:, :, NTT - 1], float(RT - 1), None, ALU.add)\
                .then_inc(S["rank_step"], 1)
            dve.wait_ge(S["rank_step"], 3)
            dve.tensor_scalar(tiles_i[:, 1, :], tiles_i[:, 0, :], RT.bit_length() - 1, None, ALU.logical_shift_right)\
                .then_inc(S["rank_step"], 1)
            dve.wait_ge(S["rank_step"], 4)
            dve.tensor_copy(tiles[:], tiles_i[:, 1, :]).then_inc(S["rank_step"], 1)
            dve.wait_ge(S["rank_step"], 5)
            dve.tensor_tensor_scan(ends[:], onesm[:, 0:NE_R], tiles[:], 0.0, ALU.mult, ALU.add).then_inc(S["rank_step"], 1)
            dve.wait_ge(S["rank_step"], 6)
            dve.tensor_tensor(begins[:], ends[:], tiles[:], ALU.subtract).then_inc(S["rank_step"], 1)
            dve.tensor_tensor(total[:], incl[:], total[:], ALU.subtract).then_inc(S["rank_step"], 1)
            dve.tensor_tensor(past[:], iota_t[:].unsqueeze(2).broadcast_to([P, NTILE, NE_R]),
                              ends[:].unsqueeze(1).broadcast_to([P, NTILE, NE_R]), ALU.is_ge).then_inc(S["expert_step"], 1)
            dve.wait_ge(S["rank_step"], 8)
            dve.scalar_tensor_tensor(base[:], begins[:].unsqueeze(2).broadcast_to([P, NE_R, NTT]), float(RT),
                                     total[:], ALU.mult, ALU.add).then_inc(S["rank_step"], 1)
            dve.wait_ge(S["rank_step"], 9)
            dve.tensor_tensor(place[:], psV[:, 0:NR].rearrange("p (t e) -> p t e", e=NE_R),
                              base[:].rearrange("p e t -> p t e"), ALU.add).then_inc(S["rank_step"], 1)
            dve.wait_ge(S["rank_step"], 10)
            for n in range(TOP):
                dve.tensor_tensor(hplace[:, n], hot[:, n], place[:], ALU.mult).then_inc(S["rank_step"], 1)
            dve.wait_ge(S["rank_step"], 10 + TOP)
            dve.tensor_reduce(slotf[:].rearrange("p n t -> p (n t)"), hplace[:].rearrange("p n t e -> p (n t) e"),
                              AX.X, ALU.add).then_inc(S["rank_step"], 1)
            dve.wait_ge(S["rank_step"], 11 + TOP)
            dve.tensor_copy(slot[:], slotf[:]).then_inc(S["slot_done"], 1)
            dve.wait_ge(S["rows_iota"], 2)
            dve.tensor_tensor(extra[:, :, :, 1], own_row[:], slotf[:], ALU.subtract).then_inc(S["extra_done"], 1)
            dve.wait_ge(S["expert_step"], 1)
            dve.tensor_reduce(expf[:], past[:], AX.X, ALU.add).then_inc(S["expert_step"], 1)
            dve.wait_ge(S["expert_step"], 2)
            dve.tensor_scalar(expert[:], expf[:], float(NE_R - 1), None, ALU.min).then_inc(S["expert_done"], 1)

            dve.wait_ge(S["b2s_done"], 1)
            dve.wait_ge(S["ld_g"], 16)

            def times_gb(g, t):
                return dve.tensor_tensor(t.rearrange("p (b t) c -> p b t c", t=NT),
                                         t.rearrange("p (b t) c -> p b t c", t=NT),
                                         grow[:, bass.ds(2 * g.n, 2), :].unsqueeze(2).broadcast_to([P, 2, NT, C]),
                                         ALU.mult)

            def add_shared(g):
                p = g.par
                dve.wait_ge(S["y_mm"], g.n + 1)
                if reached(g.n - 1):
                    dve.wait_ge(S["shared_sum"], g.n - 1)
                if isinstance(g.n, int) and g.n >= SH_FIRST:
                    dve.wait_ge(S["fout_done"], g.n)
                dve.tensor_tensor(acc[p][:], (psA, psQK)[p][:].rearrange("p (t c) -> p t c", c=C),
                                  b2s[:].unsqueeze(1).broadcast_to([P, FS, C]), ALU.add).then_inc(S["shared_done"], 1)
                dve.wait_ge(S["shared_done"], g.n + 1)
                times_gb(g, acc[p][:]).then_inc(S["shared_gb"], 1)
                dve.wait_ge(S["shared_gb"], g.n + 1)
                F = Fin[:, bass.ds(g.n * (FS * C), FS * C)]
                dve.tensor_tensor(F, F, acc[p][:].rearrange("p t c -> p (t c)"), ALU.add).then_inc(S["shared_sum"], 1)

            groups(dve, add_shared, 0, SH_FIRST)

            def turn_tile(i):
                dve.wait_ge(S["xt_mm"], i.n + 1)
                if reached(i.n - 1):
                    dve.wait_ge(S["rh_mm"], 2 * (i.n - 1))
                dve.tensor_scalar(xT[i.par][:], (psT, psV)[i.par][:, 0:RT], vec[:, 7:8], None, ALU.mult)\
                    .then_inc(S["xT_done"], 1)

            def fetch_weights(i):
                e = dve.value_load(expert[0:1, bass.ds(i.n, 1)], min_val=0, max_val=NE_R - 1)
                if reached(i.n - 3):
                    dve.wait_ge(S["ry_mm"], i.n - 3)
                    dve.wait_ge(S["yr_done"], i.n - 3)
                dve.tensor_copy(wrt[i.quad][:], wres[:, bass.ds(e, 1), :].rearrange("p o n -> p (o n)"))\
                    .then_inc(S["wrt_done"], 1)

            def routed_step(i):
                fetch_weights(i)
                turn_tile(i)
                if reached(i.n - 1):
                    routed_out(i.n - 2, (i.quad - 2) % 4, i.fourth if i.quad >= 2 else i.fourth - 1)

            def routed_out(n, q, fourth):
                p = q % 2
                dve.wait_ge(S["ry_mm"], n + 1)
                if reached(n - 1):
                    dve.wait_ge(S["yr_done"], n - 1)
                dve.tensor_tensor(yb[p][:], (psA, psQK)[p][:, 0:RT].rearrange("p (k c) -> p k c", c=C),
                                  wrt[q][:, WR:WR + C].unsqueeze(1).broadcast_to([P, RS, C]), ALU.add)\
                    .then_inc(S["yb_done"], 1)
                if reached(n - 3):
                    dve.wait_ge(st_y[q], 16 * RS * (fourth - 1))
                dve.tensor_tensor(yrow[q][:], xin[q][:, :, C + 1], empty_row[:, bass.ds(n * RS, RS)], ALU.add)
                dve.wait_ge(S["yb_done"], n + 1)
                dve.tensor_tensor(yr[q][:], yb[p][:], xin[q][:, :, C:C + 1].broadcast_to([P, RS, C]), ALU.mult)\
                    .then_inc(S["yr_done"], 1)

            dve.wait_ge(S["expert_done"], 1)
            dve.wait_ge(S["ld_wr"], 32)
            routed_tiles(dve, routed_step)
            for n in (NTILE - 2, NTILE - 1):
                routed_out(n, n % 4, n // 4 + 1)

            def sum_group(g):
                p = g.par
                dve.wait_ge(ld_y[p], 16 * g.turn)
                if reached(g.n - 1):
                    dve.wait_ge(S["fout_done"], g.n - 1)
                dve.tensor_tensor(acc[p][:], yg[p][:, :, 0, :], yg[p][:, :, 1, :], ALU.add).then_inc(S["sum_k"], 1)
                dve.wait_ge(S["sum_k"], g.n + 1)
                times_gb(g, acc[p][:]).then_inc(S["sum_gb"], 1)
                dve.wait_ge(S["sum_gb"], g.n + 1)
                F = Fin[:, bass.ds(g.n * (FS * C), FS * C)]
                dve.tensor_tensor(F, F, acc[p][:].rearrange("p t c -> p (t c)"), ALU.add).then_inc(S["fout_done"], 1)

            dve.wait_ge(S["shared_sum"], SH_FIRST)
            groups(dve, sum_group, 0, SH_FIRST)
            for n in range(SH_FIRST, NF):
                g = Group(n // 2, n % 2)
                add_shared(g)
                dve.wait_ge(S["shared_sum"], n + 1)
                sum_group(g)

        @block.tensor
        def _(pe):
            def mm(dst, lhsT, rhs, start=True, stop=True):
                return pe.matmul(dst, lhsT, rhs, start=start, stop=stop)

            pe.wait_ge(S["ld_c0"], 48)
            pe.wait_ge(S["silu_done"], 1)
            mm(psA[:, 0:NB], wm[:, 0:C], siluT[:]).then_inc(S["mod_mm"], 1)
            mm(psA[:, NB:2 * NB], wm[:, C:2 * C], siluT[:]).then_inc(S["mod_mm"], 1)
            mm(psQK[0:NB, :], siluT[:], wm[:, 2 * C:6 * C]).then_inc(S["mod_mm"], 1)
            pe.wait_ge(S["iota_done"], 14)
            pe.wait_ge(S["ld_c1"], 48)
            pe.wait_ge(S["consts_v"], NH + 1)
            pe.wait_ge(S["mod_done"], 2)
            pe.wait_ge(S["mod_row_st"], 3)

            def turn_x(b):
                pe.wait_ge(S["ln1_xn"], b.n + 1)
                if reached(b.n):
                    pe.wait_ge(S["hT_done"], b.n)
                if reached(b.n - 3):
                    pe.wait_ge(S["u_cp"], b.n - 3)
                for t in range(NT):
                    ins = pe.transpose(psA[:, t * P:(t + 1) * P], xn[b.par][:, t, :], ident[:])
                ins.then_inc(S["t1_mm"], 1)

            def project(b):
                p = b.par
                pe.wait_ge(S["mix_qk"], 2 * b.n + 2)
                pe.wait_ge(S["mix_vg"], 2 * b.n + 2)
                if reached(b.n):
                    pe.wait_ge(S["qn_done"], 4 * b.n)
                    pe.wait_ge(S["vc_done"], b.n)
                    pe.wait_ge(S["eg_done"], b.n)
                if reached(b.n - 2):
                    pe.wait_ge(S["ssum_done"], b.n - 2)
                for n, c in enumerate("qk"):
                    for t in range(NT):
                        o = (2 * n + t) * C
                        mm(psQK[:, o:o + C], xm[c][p][:, t * P:(t + 1) * P], W4[:, n, :])
                mm(psV[:, 0:T], W4[:, 2, :], xm["v"][p][:])
                mm(psV[:, T:2 * T], W4[:, 3, :], xm["g"][p][:]).then_inc(S["proj_mm"], 1)

            def turn_qk(b):
                pe.wait_ge(S["qn_done"], 4 * b.n + 4)
                if reached(b.n - 2):
                    pe.wait_ge(S["x2_done"], b.n - 2)
                if reached(b.n):
                    pe.wait_ge(S["qk_exp"], b.n)
                for n in range(4):
                    ins = pe.transpose(psT[:, n * C:(n + 1) * C], qn[b.par][:, n, :], ident[:])
                ins.then_inc(S["t2_mm"], 1)

            def scores(b):
                p = b.par
                pe.wait_ge(S["kT_done"], b.n + 1)
                pe.wait_ge(S["vT_done"], b.n + 1)
                pe.wait_ge(S["hT_done"], least(b.n + 4))
                if reached(b.n - 2):
                    pe.wait_ge(S["zT_done"], b.n - 2)
                if reached(b.n):
                    pe.wait_ge(S["u_cp"], b.n)
                pe.sem_inc(S["passed_pe"], 1)
                for j in range(NCH - 1):
                    for h in range(NH):
                        hs = slice(h * D, (h + 1) * D)
                        ins = mm(psA[hs, j * D:(j + 1) * D], kT[p][hs, j * CH:(j + 1) * CH],
                                 vT[b.quad][hs, j * D:(j + 1) * D])
                ins.then_inc(S["u_mm"], 1)
                pe.wait_ge(S["lvl_q"], 4 * b.n + 4)
                if reached(b.n):
                    pe.wait_ge(S["sc_done"], b.n)
                pe.sem_inc(S["passed_pe"], 1)
                for n, (kk, qq) in enumerate((("k16", "q16"), ("k8", "q8"))):
                    for j in range(NCH):
                        for h in range(NH):
                            hs = slice(h * D, (h + 1) * D)
                            js = slice(j * CH, (j + 1) * CH)
                            ins = mm(psL[hs, n * T + j * CH:n * T + (j + 1) * CH], lo[kk][p][hs, js], lo[qq][p][hs, js])
                ins.then_inc(S["lvl_mm"], 1)
                if reached(b.n - 3):
                    pe.wait_ge(S["lg_done"], b.n - 3)
                pe.wait_ge(S["lag_done"], BL * b.n + BL)
                pe.wait_ge(S["qz_done"], b.n + 1)
                if reached(b.n):
                    pe.wait_ge(S["lagmul"], (BL - 1) * b.n)
                    pe.wait_ge(S["lag0"], b.n)
                    pe.wait_ge(S["den_done"], b.n)
                for o in range(0, PZW, 512):
                    n = min(512, PZW - o)
                    ins = mm(psB[:, o:o + n], blkones[:], pz[p][:, o:o + n])
                ins.then_inc(S["bc_mm"], 1)

            def attend(b):
                p = b.par
                pe.wait_ge(S["sc_done"], b.n + 1)
                pe.wait_ge(S["scan_done"], b.n + 1)
                pe.wait_ge(S["q32_done"], b.n + 1)
                pe.wait_ge(S["vc_done"], least(b.n + 3))
                pe.wait_ge(S["eg_done"], least(b.n + 3))
                if reached(b.n):
                    pe.wait_ge(S["ssum_done"], b.n)
                pe.sem_inc(S["passed_pe"], 1)
                st_j = Ast[p][:].rearrange("p e j -> p j e")
                for j in range(NCH):
                    js = slice(j * CH, (j + 1) * CH)
                    for h in range(NH):
                        hs = slice(h * D, (h + 1) * D)
                        dst = psV[hs, j * CH:(j + 1) * CH]
                        ins = mm(dst, vT[b.quad][hs, js], sc[p][hs, js], start=True, stop=(j == 0))
                        if j:
                            ins = mm(dst, st_j[hs, j - 1, :], q32[b.quad][hs, js], start=False, stop=True)
                ins.then_inc(S["s_mm"], 1)

            def out_proj(b):
                p = b.par
                pe.wait_ge(S["att_done"], b.n + 1)
                pe.wait_ge(S["wog_done"], b.n + 1)
                pe.wait_ge(S["qk_exp"], least(b.n + 3))
                if reached(b.n):
                    pe.wait_ge(S["x2_done"], b.n)
                for t in range(NT):
                    ins = mm(psT[:, t * P:(t + 1) * P], att[p][:, t * P:(t + 1) * P], wog[p][:])
                ins.then_inc(S["w_mm"], 1)

            def turn_z(b):
                pe.wait_ge(S["z_done"], b.n + 1)
                pe.wait_ge(S["hT_done"], least(b.n + 7))
                pe.wait_ge(S["u_cp"], least(b.n + 3))
                if reached(b.n):
                    pe.wait_ge(S["zT_done"], b.n)
                for t in range(NT):
                    ins = pe.transpose(psA[:, t * P:(t + 1) * P], zz[b.par][:, t, :], ident[:])
                ins.then_inc(S["t3_mm"], 1)

            def route(b):
                pe.wait_ge(S["zTs_done"], b.n + 1)
                pe.wait_ge(S["lagmul"], (BL - 1) * least(b.n + 4))
                if isinstance(b.n, int) and reached(b.n):
                    pe.wait_ge(S["lg_done"], b.n)
                for t in range(NT):
                    ins = mm(psB[:, LG + t * NE_R:LG + (t + 1) * NE_R], zTs[b.par][:, t * P:(t + 1) * P], centt[:])
                ins.then_inc(S["lg_mm"], 1)

            def step(st):
                for s, work in ((5, attend), (6, out_proj), (1, turn_x), (7, turn_z), (2, project), (3, turn_qk),
                                (8, route), (4, scores)):
                    if st[s] is not None:
                        work(st[s])

            pipeline(pe, step)

            def rank():
                pe.wait_ge(S["hits_done"], 1)
                NR = NB * NT * NE_R
                hits_f = hits[:].rearrange("p t e -> p (t e)")
                mm(psV[:, 0:NR], below[:], hits_f)
                mm(psV[:, NR:2 * NR], onesm[:], hits_f).then_inc(S["rank_mm"], 1)

            pe.wait_ge(S["w1g_done"], 1)
            pe.wait_ge(S["ld_w2"], 16)
            pe.wait_ge(S["zT_done"], NB)
            pe.wait_ge(S["lg_done"], NB)
            pe.wait_ge(S["lagmul"], (BL - 1) * NB)

            def shared_up(g, e):
                for c in range(HC):
                    n = HC * (NE_S * g.n + e - 1) + c + 1
                    psH = psB[:, c * 512:(c + 1) * 512] if c < 3 else psL[:]
                    if reached(n):
                        pe.wait_ge(S["gelu_done"], n)
                    mm(psH, W1[:, e, c * P:(c + 1) * P], zT[:, bass.ds(g.n * FT, FT)]).then_inc(S["h_mm"], 1)

            def shared_down(n, par):
                pe.wait_ge(S["gelu_done"], HC * NE_S * (n + 1))
                if reached(n - 1):
                    pe.wait_ge(S["shared_done"], n - 1)
                for t in range(FS):
                    for e in range(NE_S):
                        for c in range(HC):
                            ins = mm((psA, psQK)[par][:, t * C:(t + 1) * C], hid[e][par][:, c, t * P:(t + 1) * P], W2[:, e, c, :],
                                     start=(e == 0 and c == 0), stop=(e == NE_S - 1 and c == HC - 1))
                ins.then_inc(S["y_mm"], 1)

            def shared_step(g):
                shared_up(g, 0)
                if not (isinstance(g.n, int) and g.n in (0, SH_FIRST)):
                    shared_down(g.n - 1, 1 - g.par)
                shared_up(g, 1)
                if isinstance(g.n, int) and g.n == 0:
                    rank()

            groups(pe, shared_step, 0, SH_FIRST)
            shared_down(SH_FIRST - 1, 1)

            pe.wait_ge(S["gelu_done"], HC * NE_S * SH_FIRST)
            pe.wait_ge(S["shared_done"], SH_FIRST)
            pe.wait_ge(S["slot_done"], 1)

            def turn_tile(i):
                pe.wait_ge(ld_tile[i.quad], 16 * i.fourth)
                if reached(i.n - 1):
                    pe.wait_ge(S["xT_done"], i.n - 1)
                for k in range(RS):
                    ins = pe.transpose((psT, psV)[i.par][:, k * P:(k + 1) * P], xin[i.quad][:, k, 0:C], ident[:])
                ins.then_inc(S["xt_mm"], 1)

            def routed_up(i):
                pe.wait_ge(S["wrt_done"], i.n + 1)
                pe.wait_ge(S["xT_done"], i.n + 1)
                for c in range(HC):
                    if c % 2 == 0 and reached(i.n - 1):
                        pe.wait_ge(S["rgelu_done"], 2 * (i.n - 1))
                    ins = mm(routed_h(i, c), wrt[i.quad][:, c * P:(c + 1) * P], xT[i.par][:])
                    if c % 2:
                        ins.then_inc(S["rh_mm"], 1)

            def routed_down(n, q):
                pe.wait_ge(S["rgelu_done"], 2 * (n + 1))
                if reached(n - 1):
                    pe.wait_ge(S["yr_done"], n - 1)
                W2r = wrt[q][:, HID + HC:WR].rearrange("p (k c) -> p k c", c=C)
                for t in range(RS):
                    for c in range(HC):
                        ins = mm((psA, psQK)[q % 2][:, t * C:(t + 1) * C], rhid[q % 2][:, c, t * P:(t + 1) * P],
                                 W2r[:, c, :], start=(c == 0), stop=(c == HC - 1))
                ins.then_inc(S["ry_mm"], 1)

            def before(i, n):
                return Tile(i.m + (i.quad - n) // 4, (i.quad - n) % 4)

            def routed_step(i):
                turn_tile(i)
                if reached(i.n):
                    routed_up(before(i, 1))
                if reached(i.n - 1):
                    routed_down(before(i, 2).n, before(i, 2).quad)

            routed_tiles(pe, routed_step)
            last = Tile(NTILE // 4, NTILE % 4)
            routed_up(before(last, 1))
            routed_down(NTILE - 2, (NTILE - 2) % 4)
            routed_down(NTILE - 1, (NTILE - 1) % 4)

            pe.wait_ge(S["rgelu_done"], 2 * NTILE)
            pe.wait_ge(S["yr_done"], NTILE)
            for n in range(SH_FIRST, NF):
                shared_step(Group(n // 2, n % 2))
            shared_down(NF - 1, 1)


def least(n):
    return min(n, NB) if isinstance(n, int) else n


def launch_inputs(a):
    import numpy as np

    def flat(name):
        return a["L0_attn_" + name].reshape(-1)

    vecs = np.stack([flat("time_decay"), flat("mix_q"), flat("mix_k"), flat("mix_v"), flat("mix_g"),
                     flat("norm_scale"), a["L0_ffn_g_shared"], a["L0_ffn_g_routed"]], axis=1)
    wr = np.concatenate([a["L0_ffn_W1_r"], a["L0_ffn_b1_r"].reshape(NE_R, HC, P).transpose(0, 2, 1),
                         a["L0_ffn_W2_r"].reshape(NE_R, HC, P, C).transpose(0, 2, 1, 3).reshape(NE_R, P, HC * C)],
                        axis=2)
    return {
        "x": a["L0_attn_x"], "vecs": vecs, "cT": a["L0_c"].T,
        "wqkvg": np.stack([a["L0_attn_W" + n].T for n in "qkvg"], axis=1),
        "wo": a["L0_attn_Wo"].T, "wmod": a["L0_wmod"],
        "w1s": a["L0_ffn_W1_s"], "b1": a["L0_ffn_b1_s"].reshape(NE_S * HC, P).T, "w2s": a["L0_ffn_W2_s"],
        "b2": a["L0_ffn_b2_s"].reshape(1, NE_S * C), "wr": wr, "b2r": a["L0_ffn_b2_r"],
        "cent": a["L0_ffn_centroids"],
    }


def kernel(**inputs):
    import numpy as np
    import concourse.bacc as bacc
    from concourse.bass_utils import run_bass_kernel_spmd

    nc = bacc.Bacc("TRN2", target_bir_lowering=False, num_devices=1)
    given = launch_inputs({k: np.asarray(v) for k, v in inputs.items()})
    arrays, args = {}, {}
    for name, a in given.items():
        a = np.ascontiguousarray(a)
        arrays[f"in_{name}"] = a
        args[name] = nc.dram_tensor(f"in_{name}", a.shape, mybir.dt.from_np(a.dtype), kind="ExternalInput").ap()
    args["out"] = nc.dram_tensor("out_0", (NB, T, C), F32, kind="ExternalOutput").ap()
    adaln_kernel(nc, **args)
    r = run_bass_kernel_spmd(nc, [arrays], core_ids=[0])
    return r.results[0]["out_0"]
```

```python
import concourse.bass as bass
from concourse import mybir
from contextlib import ExitStack

F32 = mybir.dt.float32
F32R = mybir.dt.float32r
I32 = mybir.dt.int32
U32 = mybir.dt.uint32
ALU = mybir.AluOpType
ACT = mybir.ActivationFunctionType
AX = mybir.AxisListType

P = 128
NB = 16
T = 256
C = 128
NH = 4
D = C // NH
NT = T // P
CH = 32
NCH = T // CH
BL = 8
NBL = T // BL
NE_S, NE_R = 2, 8
HID = 512
HC = HID // P
FT = 512
NF = NB * T // FT
FS = FT // P
TOP = 2
RT = 256
RS = RT // P
NTILE = (TOP * NB * T + NE_R * (RT - 1)) // RT
SH_FIRST = 6
EARLY = (NB - 4) * NT
RW = C + 2
WR = HID + HC + HC * C

LN_EPS = 1e-5
RMS_EPS = 1e-8
FFN_EPS = 1.1920929e-07

LAG_OFF = [NBL * sum(BL - m for m in range(l)) for l in range(BL + 1)]
LAGS = LAG_OFF[BL]
PZW = LAGS + T
LG = PZW

STAGES = 9


def reached(n):
    return not isinstance(n, int) or n > 0


class Group:

    def __init__(self, m, r):
        self.n, self.par, self.turn = 2 * m + r, r, m + 1


def groups(eng, step, last):
    step(Group(0, 0))
    step(Group(0, 1))
    with eng.Fori(1, last // 2) as m:
        step(Group(m, 0))
        step(Group(m, 1))
    if last % 2:
        step(Group(last // 2, 0))


class Tile:

    def __init__(self, m, r):
        self.m, self.n, self.par, self.quad, self.fourth = m, 4 * m + r, r % 2, r, m + 1
        self.turn = 2 * m + r // 2 + 1


def routed_tiles(eng, step):
    for r in range(4):
        step(Tile(0, r))
    with eng.Fori(1, NTILE // 4) as m:
        for r in range(4):
            step(Tile(m, r))
    for r in range(NTILE % 4):
        step(Tile(NTILE // 4, r))


class Batch:

    def __init__(self, m, r):
        self.n, self.par, self.quad = 4 * m + r, r % 2, r
        self.turn = 2 * m + r // 2 + 1

        self.fourth = m + 1
        self.left = NB - 1 - self.n if isinstance(m, int) else None
        self.is_first = isinstance(m, int) and self.n == 0

    @staticmethod
    def at(n, loop=0):
        return Batch(loop + n // 4, n % 4)


def pipeline(eng, step):
    first = STAGES - 1
    loops = (NB - first) // 4

    def fixed(i):
        step([Batch.at(i - s) if 0 <= i - s < NB else None for s in range(STAGES)])

    for i in range(first):
        fixed(i)
    with eng.Fori(0, loops) as j:
        for i in range(first, first + 4):
            step([Batch.at(i - s, j) for s in range(STAGES)])
    for i in range(first + 4 * loops, NB + STAGES - 1):
        fixed(i)


def adaln_kernel(nc, x, vecs, cT, wqkvg, wo, wmod, w1s, b1, w2s, b2, wr, b2r, cent, out):
    ctx = ExitStack()
    with ctx:
        def sb(name, shape, dt=F32):
            return ctx.enter_context(nc.sbuf_tensor(name, shape, dt))

        def pb(name, shape):
            return ctx.enter_context(nc.psum_tensor(name, shape, F32))

        def sem(name):
            return ctx.enter_context(nc.semaphore(name))

        modrow_dram = nc.dram_tensor("modrow_dram", (NB, 4 * C), F32, kind="Internal").ap()

        z_dram = nc.dram_tensor("z_dram", (NB, T, C), F32, kind="Internal").ap()
        xs_dram = nc.dram_tensor("xs_dram", (NTILE * RT, RW), F32, kind="Internal").ap()
        ys_dram = nc.dram_tensor("ys_dram", (TOP * NB * T + NTILE * RT, C), F32, kind="Internal").ap()

        vec = sb("vec", [P, 8])
        MIX = {"q": 1, "k": 2, "v": 3, "g": 4}
        cTt = sb("cTt", [P, NB])
        silu_e = sb("silu_e", [P, NB])
        silu_r = sb("silu_r", [P, NB])
        siluT = sb("siluT", [P, NB])
        W4 = sb("W4", [P, 4, C])
        WoT = sb("WoT", [P, C])
        wm = sb("wm", [P, 6 * C])
        W1 = sb("W1", [P, NE_S, HID])
        W2 = sb("W2", [P, NE_S, HC, C])
        b1t = sb("b1t", [P, NE_S * HC])
        b2t = sb("b2t", [P, NE_S * C])
        zeros = sb("zeros", [P, RW])
        below = sb("below", [P, P])
        onesm = sb("onesm", [P, P])
        centt = sb("centt", [P, NE_R])
        ident = sb("ident", [P, P])
        blkones = sb("blkones", [P, P])
        iota33 = sb("iota33", [P, CH + 1])
        iota_r = sb("iota_r", [P, CH])
        iota8 = sb("iota8", [P, NE_R])
        iota_t = sb("iota_t", [P, NTILE])
        expd = sb("expd", [P, 1])
        nexpd = sb("nexpd", [P, 1])
        pw = sb("pw", [P, CH + 1])
        pwr = sb("pwr", [P, CH])
        wrow = sb("wrow", [P, T])
        w32 = sb("w32", [P, D, NCH - 1])
        halfc = sb("halfc", [P, 4])
        nhalfc = sb("nhalfc", [P, 4])
        mask8 = sb("mask8", [P, T], I32)
        modT = sb("modT", [P, 2, NB])
        mrow = sb("mrow", [NB, 4, C])
        msgn = sb("msgn", [NB, 2, C])
        mneg = sb("mneg", [NB, 2, C])
        mabs = sb("mabs", [NB, 2, C])

        W1h = sb("W1h", [P, NE_S, HID], F32R)
        W1l = sb("W1l", [P, NE_S, HID], F32R)
        zh = [sb(f"zh{i}", [P, FT], F32R) for i in range(2)]
        zl = [sb(f"zl{i}", [P, FT], F32R) for i in range(2)]
        Fin = sb("Fin", [P, NB * NT * C])
        zT = sb("zT", [P, NB * T])
        lgt = sb("lgt", [P, NB * NT * NE_R])

        scope = ExitStack()

        def pbuf(name, shape, dt=F32):
            return scope.enter_context(nc.sbuf_tensor(name, shape, dt))

        xb = [pbuf(f"xb{i}", [P, NT, C]) for i in range(2)]
        st1 = [pbuf(f"st1{i}", [P, NT, 6]) for i in range(2)]
        mv1 = [pbuf(f"mv1{i}", [P, NT, 2]) for i in range(2)]
        ve1 = [pbuf(f"ve1{i}", [P, NT]) for i in range(2)]
        rs1 = [pbuf(f"rs1{i}", [P, NT]) for i in range(2)]
        xn = [pbuf(f"xn{i}", [P, NT, C]) for i in range(2)]
        hT = [pbuf(f"hT{i}", [P, T + 1]) for i in range(2)]
        dT = [pbuf(f"dT{i}", [P, T]) for i in range(2)]
        xm = {c: [pbuf(f"xm{c}{i}", [P, T]) for i in range(2)] for c in "qkvg"}
        sq = pbuf("sq", [P, C])
        ssq = [pbuf(f"ssq{i}", [P, 4]) for i in range(2)]
        nrm = [pbuf(f"nrm{i}", [P, 4]) for i in range(2)]
        nre = [pbuf(f"nre{i}", [P, 4]) for i in range(2)]
        rqk = [pbuf(f"rqk{i}", [P, 4]) for i in range(2)]
        eg = [pbuf(f"eg{i}", [P, T]) for i in range(4)]
        vc = [pbuf(f"vc{i}", [P, T]) for i in range(4)]
        vT = [pbuf(f"vT{i}", [P, T]) for i in range(4)]
        qn = [pbuf(f"qn{i}", [P, 4, C]) for i in range(2)]
        qk = [pbuf(f"qk{i}", [P, 2 * T]) for i in range(2)]
        zc = [pbuf(f"zc{i}", [P, T]) for i in range(2)]
        pz = [pbuf(f"pz{i}", [P, PZW]) for i in range(2)]
        it_s, it_t, it_x, it_m, it_y = (pz[1][:, n * T:(n + 1) * T].bitcast(I32) for n in range(5))
        lo = {n: [pbuf(f"{n}{i}", [P, T]) for i in range(2)] for n in ("q8", "k8", "q16", "k16")}
        q32 = [pbuf(f"q32{i}", [P, T]) for i in range(4)]
        k32 = pbuf("k32", [P, T])
        kT = [pbuf(f"kT{i}", [P, T]) for i in range(2)]
        ue = [pbuf(f"ue{i}", [P, D, NCH - 1]) for i in range(2)]
        Ast = [pbuf(f"Ast{i}", [P, D, NCH - 1]) for i in range(2)]
        sc = [pbuf(f"sc{i}", [P, T]) for i in range(2)]
        den = [pbuf(f"den{i}", [P, T]) for i in range(2)]
        rden = [pbuf(f"rden{i}", [P, T]) for i in range(2)]
        slag = [pbuf(f"slag{i}", [P, T]) for i in range(2)]
        tlag = pbuf("tlag", [P, LAGS - T])
        ssum = [pbuf(f"ssum{i}", [P, T]) for i in range(2)]
        att = [pbuf(f"att{i}", [P, T]) for i in range(2)]
        rows = [pbuf(f"rows{i}", [P, 4, C]) for i in range(4)]
        wog = [pbuf(f"wog{i}", [P, C]) for i in range(2)]
        xr = [pbuf(f"xr{i}", [P, NT, C]) for i in range(2)]
        x2 = [pbuf(f"x2{i}", [P, NT, C]) for i in range(2)]
        st2 = [pbuf(f"st2{i}", [P, NT, 6]) for i in range(2)]
        mv2 = [pbuf(f"mv2{i}", [P, NT, 2]) for i in range(2)]
        ve2 = [pbuf(f"ve2{i}", [P, NT]) for i in range(2)]
        rs2 = [pbuf(f"rs2{i}", [P, NT]) for i in range(2)]
        xn2 = [pbuf(f"xn2{i}", [P, NT, C]) for i in range(2)]
        uu = [pbuf(f"uu{i}", [P, NT, C]) for i in range(2)]
        squ = pbuf("squ", [P, C])
        ssu = [pbuf(f"ssu{i}", [P, NT]) for i in range(2)]
        seu = [pbuf(f"seu{i}", [P, NT]) for i in range(2)]
        ru = [pbuf(f"ru{i}", [P, NT]) for i in range(2)]
        iru = [pbuf(f"iru{i}", [P, NT]) for i in range(4)]
        zz = [pbuf(f"zz{i}", [P, NT, C]) for i in range(2)]
        gu = [pbuf(f"gu{i}", [P, NT, C]) for i in range(2)]
        zTs = [pbuf(f"zTs{i}", [P, T]) for i in range(2)]

        scope.close()

        score = sb("score", [P, NB * NT, NE_R])
        ssc = sb("ssc", [P, NB * NT])
        rsc = sb("rsc", [P, NB * NT])
        top = sb("top", [P, NB * NT, 8])
        topi = sb("topi", [P, NB * NT, 8], U32)
        topf = sb("topf", [P, NB * NT, 2])
        hot = sb("hot", [P, TOP, NB * NT, NE_R])
        extra = sb("extra", [P, TOP, NB * NT, 2])
        own_row = sb("own_row", [P, TOP, NB * NT])
        empty_row = sb("empty_row", [P, NTILE * RS])
        hits = sb("hits", [P, NB * NT, NE_R])
        gk = sb("gk", [P, NB * NT, TOP])
        total = sb("total", [P, NE_R, NB * NT])
        inner = sb("inner", [P, NE_R, NB * NT])
        incl = sb("incl", [P, NE_R, NB * NT])
        base = sb("base", [P, NE_R, NB * NT])
        place = sb("place", [P, NB * NT, NE_R])
        hplace = sb("hplace", [P, TOP, NB * NT, NE_R])
        slotf = sb("slotf", [P, TOP, NB * NT])
        slot = sb("slot", [P, TOP, NB * NT], U32)
        tiles_i = sb("tiles_i", [P, 2, NE_R], I32)
        tiles = sb("tiles", [P, NE_R])
        ends = sb("ends", [P, NE_R])
        begins = sb("begins", [P, NE_R])
        past = sb("past", [P, NTILE, NE_R])
        expf = sb("expf", [P, NTILE])
        expert = sb("expert", [P, NTILE], I32)

        scope = ExitStack()
        hid = [[scope.enter_context(nc.sbuf_tensor(f"hid{e}{i}", [P, HC, FT], F32)) for i in range(2)]
               for e in range(NE_S)]
        scope.close()
        w1t = [sb(f"w1t{i}", [P, 2 * HID], F32R) for i in range(4)]
        w2t = [sb(f"w2t{i}", [P, HC + HC * C + C]) for i in range(4)]
        rhid = [sb(f"rhid{i}", [P, HC, RT]) for i in range(2)]
        b2s = sb("b2s", [P, C])
        zg = [sb(f"zg{i}", [P, TOP, FS, RW]) for i in range(2)]
        slot_z = [sb(f"slot_z{i}", [P, TOP, FS], U32) for i in range(2)]
        wres = sb("wres", [P, NE_R, WR + C])
        xin = [sb(f"xin{i}", [P, RS, RW]) for i in range(4)]
        xh = [sb(f"xh{i}", [P, RT], F32R) for i in range(2)]
        xl = [sb(f"xl{i}", [P, RT], F32R) for i in range(2)]
        yr = [sb(f"yr{i}", [P, RS, C]) for i in range(4)]
        yb = [sb(f"yb{i}", [P, RS, C]) for i in range(2)]
        yrow = [sb(f"yrow{i}", [P, RS], U32) for i in range(4)]
        yg = [z[:].rearrange("p n t r -> p (n t r)")[:, 0:FS * TOP * C].rearrange("p (t n c) -> p t n c", n=TOP, c=C)
              for z in zg]
        acc = [sb(f"acc{i}", [P, FS, C]) for i in range(2)]
        grow = sb("grow", [P, NB, C])

        psA = pb("psA", [P, 512])
        psQK = pb("psQK", [P, 512])
        psV = pb("psV", [P, 512])
        psT = pb("psT", [P, 512])
        psB = pb("psB", [P, 1536])
        psL = pb("psL", [P, 512])

        names = """passed_dve passed_pool passed_pe ld_w1 ld_w2 ld_c0 ld_c1 ld_c2 st_rows slots_zero iota_done consts_v
            expd_done nexpd_done pw_done tabs_done silu_exp silu_step silu_done mask_step mod_mm mod_row_step
            mod_row_st mod_done zero_done w1g_done ln1_st ln1_ag ln1_ve ln1_pow ln1_xn t1_mm hT_done d_done
            mix_done proj_mm sq_done eg_done vc_done nrm_pow nre_done rqk_done qn_done vT_done t2_mm qk_exp
            zscan qz_done lag_done lvl_q k32_done q32_done kT_done u_mm lvl_mm bc_mm u_cp sc16 scan_done sc_done
            den_done rden_done lagmul lag0 lagadd s_mm ssum_done att_done wog_done w_mm x2_done ln2_st ln2_ag
            ln2_ve ln2_pow ln2_xn um_done u_done squ_done seu_done u_pow iru_done z_done gu_done fin_done t3_mm
            zTs_done zT_done lg_mm lg_done sig_done rt_sum hits_done rank_mm rows_iota ld_wr extra_done
            slots_copied zeros_done ld_g inner_done rank_step slot_done expert_step expert_done h_mm gelu_done
            y_mm shared_done b2s_done zh_done z_split xh_done wh_done xt_mm xT_done wrt_done rh_mm rgelu_done
            ry_mm yb_done yr_done shared_gb shared_sum sum_k sum_gb fout_done top_done hot_step""".split()
        S = {n: sem(n) for n in names}
        ld_x = [sem(f"ld_x{i}") for i in range(2)]
        ld_xr = [sem(f"ld_xr{i}") for i in range(2)]
        ld_rows = [sem(f"ld_rows{i}") for i in range(4)]
        st_z = [sem(f"st_z{i}") for i in range(2)]
        ld_z = [sem(f"ld_z{i}") for i in range(2)]
        scat = [sem(f"scat{i}") for i in range(2)]
        ld_tile = [sem(f"ld_tile{i}") for i in range(4)]
        st_y = [sem(f"st_y{i}") for i in range(4)]
        ld_y = [sem(f"ld_y{i}") for i in range(2)]
        st_o = [sem(f"st_o{i}") for i in range(2)]

        def routed_h(i, c):
            bank = (psB[:, 0:512], psB[:, 512:1024], psB[:, 1024:1536], psL[:])[2 * i.par + c // 2]
            return bank[:, (c % 2) * RT:(c % 2 + 1) * RT]

        block = ctx.enter_context(nc.Block())

        @block.sync
        def _(sp):
            def load_x(b):
                if reached(b.n - 1):
                    sp.wait_ge(S["ln1_xn"], b.n - 1)
                sp.dma_start(xb[b.par][:], x[bass.ds(b.n, 1)].rearrange("o (t p) c -> p (o t) c", p=P))\
                  .then_inc(ld_x[b.par], 16)

            def load_xr(b):
                if reached(b.n - 1):
                    sp.wait_ge(S["x2_done"], b.n - 1)
                sp.dma_start(xr[b.par][:], x[bass.ds(b.n, 1)].rearrange("o (t p) c -> p (o t) c", p=P))\
                  .then_inc(ld_xr[b.par], 16)

            def load_rows(b):
                if reached(b.n - 3):
                    sp.wait_ge(S["gu_done"], b.n - 3)
                sp.dma_start(rows[b.quad][:].rearrange("p k c -> p (k c)"),
                             modrow_dram[bass.ds(b.n, 1), :].partition_broadcast(P)
                             .rearrange("p o n -> p (o n)")).then_inc(ld_rows[b.quad], 16)

            sp.dma_start(cTt[:], cT).then_inc(S["ld_c0"], 16)
            sp.dma_start(vec[:], vecs).then_inc(S["ld_c0"], 16)
            sp.dma_start(wm[:], wmod).then_inc(S["ld_c0"], 16)
            load_x(Batch.at(0))
            load_x(Batch.at(1))
            sp.dma_start(W4[:], wqkvg).then_inc(S["ld_c1"], 16)
            sp.dma_start(WoT[:], wo).then_inc(S["ld_c1"], 16)
            sp.dma_start(centt[:], cent).then_inc(S["ld_c1"], 16)

            def store_rows():
                sp.wait_ge(S["mod_row_st"], 3)
                sp.dma_start(modrow_dram, mrow[:].rearrange("b k c -> b (k c)")).then_inc(S["st_rows"], 16)

            def load_ffn():
                sp.dma_start(b1t[:], b1).then_inc(S["ld_c2"], 16)
                sp.dma_start(b2t[:], b2.partition_broadcast(P)).then_inc(S["ld_c2"], 16)
                sp.dma_start(W1[:], w1s.rearrange("e c h -> c e h")).then_inc(S["ld_w1"], 16)
                sp.dma_start(W2[:], w2s.rearrange("e (k p) c -> p e k c", p=P)).then_inc(S["ld_w2"], 16)
                sp.wait_ge(S["zeros_done"], 1)
                sp.dma_start(xs_dram.rearrange("(n p) c -> p n c", p=P),
                             zeros[:].unsqueeze(1).broadcast_to([P, NTILE * RS, RW])).then_inc(S["slots_zero"], 16)

            def store_z(b):
                sp.wait_ge(S["z_done"], b.n + 1)
                sp.dma_start(z_dram[bass.ds(b.n, 1)].rearrange("o (t p) c -> p (o t) c", p=P), zz[b.par][:])\
                  .then_inc(st_z[b.par], 16)

            def step(st):
                if st[0] is not None and not (isinstance(st[0].n, int) and st[0].n < 2):
                    load_x(st[0])
                if st[5] is not None:
                    load_xr(st[5])
                if st[4] is not None:
                    if st[4].is_first:
                        sp.wait_ge(S["st_rows"], 16)
                    load_rows(st[4])
                if st[1] is not None and st[1].is_first:
                    store_rows()
                if st[3] is not None and st[3].is_first:
                    load_ffn()
                if st[7] is not None:
                    store_z(st[7])

            pipeline(sp, step)

            sp.wait_ge(S["lg_done"], NB)
            for p in range(2):
                sp.wait_ge(st_z[p], 16 * (NB // 2))
            sp.dma_start(grow[:], modrow_dram[:, 3 * C:4 * C].partition_broadcast(P)).then_inc(S["ld_g"], 16)

            def load_z(g):
                if reached(g.n - 1):
                    sp.wait_ge(scat[g.par], 16 * TOP * FS * (g.turn - 1))
                for n in range(TOP):
                    sp.dma_start(zg[g.par][:, n, :, 0:C],
                                 z_dram[bass.ds(2 * g.n, 2)].rearrange("b (t p) c -> p (b t) c", p=P))\
                      .then_inc(ld_z[g.par], 16)

            load_z(Group(0, 0))
            load_z(Group(0, 1))
            sp.dma_start(wres[:, :, 0:WR], wr.rearrange("e p n -> p e n")).then_inc(S["ld_wr"], 16)
            sp.dma_start(wres[:, :, WR:WR + C], b2r.partition_broadcast(P)).then_inc(S["ld_wr"], 16)
            with sp.Fori(1, NF // 2) as m:
                load_z(Group(m, 0))
                load_z(Group(m, 1))

            for p in range(2):
                sp.wait_ge(scat[p], 16 * TOP * FS * (NF // 2))

            def load_tile(i):
                q = i.quad
                if reached(i.n - 3):
                    sp.wait_ge(S["yr_done"], i.n - 3)
                sp.dma_start(xin[q][:], xs_dram[bass.ds(i.n * RT, RT), :].rearrange("(k p) c -> p k c", p=P))\
                  .then_inc(ld_tile[q], 16)
            routed_tiles(sp, load_tile)

            for q in range(4):
                sp.wait_ge(st_y[q], 16 * RS * ((NTILE - q + 3) // 4))

            def finish(g):
                if reached(g.n - 1):
                    sp.wait_ge(S["sum_k"], g.n - 1)
                sp.dma_start(yg[g.par].rearrange("p t k c -> p t (k c)"),
                             ys_dram[bass.ds(g.n * (TOP * FT), TOP * FT), :]
                             .rearrange("(t p k) c -> p t (k c)", p=P, k=TOP)).then_inc(ld_y[g.par], 16)
                if not (isinstance(g.n, int) and g.n == 0):
                    store_out(g.n - 1, 1 - g.par)

            def store_out(n, par):
                sp.wait_ge(S["fout_done"], n + 1)
                sp.dma_start(out[bass.ds(2 * n, 2)].rearrange("b (t p) c -> p (b t) c", p=P),
                             Fin[:, bass.ds(n * (FS * C), FS * C)].rearrange("p (t c) -> p t c", c=C))\
                  .then_inc(st_o[par], 16)

            groups(sp, finish, NF)
            store_out(NF - 1, 1)
            for p in range(2):
                sp.wait_ge(st_o[p], 16 * (NF // 2))

        @block.gpsimd
        def _(pool):
            pool.memset(ident[:], 0.0).then_inc(S["iota_done"], 1)
            pool.memset(blkones[:], 0.0).then_inc(S["iota_done"], 1)
            pool.memset(halfc[:], 0.5).then_inc(S["iota_done"], 1)
            pool.memset(nhalfc[:], -0.5).then_inc(S["iota_done"], 1)
            pool.iota(iota33[:], [[1, CH + 1]], base=0, channel_multiplier=0,
                      allow_small_or_imprecise_dtypes=True).then_inc(S["iota_done"], 1)
            pool.iota(iota_r[:], [[-1, CH]], base=CH - 1, channel_multiplier=0,
                      allow_small_or_imprecise_dtypes=True).then_inc(S["iota_done"], 1)
            pool.iota(iota8[:], [[1, NE_R]], base=0, channel_multiplier=0,
                      allow_small_or_imprecise_dtypes=True).then_inc(S["iota_done"], 1)
            pool.iota(iota_t[:], [[1, NTILE]], base=0, channel_multiplier=0,
                      allow_small_or_imprecise_dtypes=True).then_inc(S["iota_done"], 1)
            pool.memset(zeros[:], 0.0).then_inc(S["zeros_done"], 1)
            pool.memset(below[:], 1.0).then_inc(S["iota_done"], 1)
            pool.memset(onesm[:], 1.0).then_inc(S["iota_done"], 1)
            pool.iota(it_s, [[0, T]], base=0, channel_multiplier=1).then_inc(S["iota_done"], 1)
            pool.iota(it_t, [[1, T]], base=0, channel_multiplier=0).then_inc(S["iota_done"], 1)
            pool.wait_ge(S["iota_done"], 12)
            pool.affine_select(out=ident[:], in_=ident[:], compare_op=ALU.not_equal, fill=1.0, base=0,
                               pattern=[[-1, P]], channel_multiplier=1).then_inc(S["iota_done"], 1)
            pool.affine_select(out=below[:], in_=below[:], compare_op=ALU.is_gt, fill=0.0, base=0,
                               pattern=[[1, P]], channel_multiplier=-1).then_inc(S["iota_done"], 1)

            def powers(b):
                pool.wait_ge(S["ln1_ve"], b.n + 1)
                if reached(b.n - 1):
                    pool.wait_ge(S["ln1_xn"], b.n - 1)
                pool.tensor_tensor(rs1[b.par][:], ve1[b.par][:], nhalfc[:, 0:NT], ALU.pow).then_inc(S["ln1_pow"], 1)

            def differences(b):
                p = b.par
                pool.wait_ge(S["hT_done"], b.n + 1)
                if reached(b.n - 1):
                    pool.wait_ge(S["mix_done"], 4 * (b.n - 1))
                pool.tensor_tensor(dT[p][:], hT[p][:, 1:T + 1], hT[p][:, 0:T], ALU.subtract).then_inc(S["d_done"], 1)
            def norms(b):
                pool.wait_ge(S["sq_done"], 4 * b.n + 4)
                if reached(b.n - 1):
                    pool.wait_ge(S["nre_done"], b.n - 1)
                pool.tensor_tensor(nrm[b.par][:], ssq[b.par][:], halfc[:], ALU.pow).then_inc(S["nrm_pow"], 1)

            def operands(b):
                p = b.par
                pool.wait_ge(S["qk_exp"], b.n + 1)
                if reached(b.n - 1):
                    pool.wait_ge(S["lvl_mm"], b.n - 1)
                for name, c, side, table in (("q16", 16, 1, pw[:, 1:17]), ("k16", 16, 0, pwr[:, 16:32]),
                                             ("q8", 8, 1, pw[:, 1:9]), ("k8", 8, 0, pwr[:, 24:32])):
                    src = qk[p][:, 0:T] if side else qk[p][:, T:2 * T]
                    half = slice(c, 2 * c) if side else slice(0, c)
                    pool.tensor_tensor(
                        lo[name][p][:].rearrange("p (n s) -> p n s", s=2 * c)[:, :, half],
                        src.rearrange("p (n s) -> p n s", s=2 * c)[:, :, half],
                        table.unsqueeze(1).broadcast_to([P, T // (2 * c), c]), ALU.mult).then_inc(S["lvl_q"], 1)

            def q_times_z(b):
                p = b.par
                pool.wait_ge(S["zscan"], b.n + 1)
                if reached(b.n - 1):
                    pool.wait_ge(S["bc_mm"], b.n - 1)
                pool.tensor_tensor(pz[p][:, LAGS:PZW], qk[p][:, 0:T], zc[p][:], ALU.mult).then_inc(S["qz_done"], 1)

            def add_lags(b):
                p = b.par
                pool.wait_ge(S["lag0"], b.n + 1)
                for l in range(1, BL):
                    pool.wait_ge(S["lagmul"], (BL - 1) * b.n + l)
                    if l > 1:
                        pool.wait_ge(S["lagadd"], (BL - 1) * b.n + l - 1)
                    dst = slag[p][:].rearrange("p (n s) -> p n s", s=BL)[:, :, l:BL]
                    o = LAG_OFF[l] - T
                    src = tlag[:, o:o + NBL * (BL - l)].rearrange("p (n s) -> p n s", s=BL - l)
                    pool.tensor_tensor(dst, dst, src, ALU.add).then_inc(S["lagadd"], 1)

            def scale_wo(b):
                p = b.par
                pool.wait_ge(ld_rows[b.quad], 16 * b.fourth)
                if reached(b.n - 1):
                    pool.wait_ge(S["w_mm"], b.n - 1)
                pool.tensor_tensor(wog[p][:], WoT[:], rows[b.quad][:, 0, :], ALU.mult).then_inc(S["wog_done"], 1)

            def divide(b):
                p = b.par
                pool.wait_ge(S["ssum_done"], b.n + 1)
                pool.wait_ge(S["rden_done"], b.n + 1)
                if reached(b.n - 1):
                    pool.wait_ge(S["w_mm"], b.n - 1)
                pool.tensor_tensor(att[p][:], ssum[p][:], rden[p][:], ALU.mult).then_inc(S["att_done"], 1)

            def second_norm(b):
                p = b.par
                pool.wait_ge(S["ln2_ve"], b.n + 1)
                if reached(b.n - 1):
                    pool.wait_ge(S["ln2_xn"], b.n - 1)
                pool.tensor_tensor(rs2[p][:], ve2[p][:], nhalfc[:, 0:NT], ALU.pow).then_inc(S["ln2_pow"], 1)

            def modulate(b):
                p = b.par
                pool.wait_ge(S["ln2_xn"], b.n + 1)
                pool.tensor_tensor(xn2[p][:], xn2[p][:], rows[b.quad][:, 2, :].unsqueeze(1).broadcast_to([P, NT, C]),
                                   ALU.mult).then_inc(S["um_done"], 1)
                pool.wait_ge(S["um_done"], b.n + 1)
                if reached(b.n - 1):
                    pool.wait_ge(S["z_done"], b.n - 1)
                    pool.wait_ge(S["gu_done"], b.n - 1)
                pool.tensor_tensor(uu[p][:], xn2[p][:], rows[b.quad][:, 1, :].unsqueeze(1).broadcast_to([P, NT, C]),
                                   ALU.add).then_inc(S["u_done"], 1)

            def gate_u(b):
                p = b.par
                pool.wait_ge(S["u_done"], b.n + 1)
                if reached(b.n - 1):
                    pool.wait_ge(S["fin_done"], b.n - 1)
                pool.tensor_tensor(gu[p][:], uu[p][:], rows[b.quad][:, 3, :].unsqueeze(1).broadcast_to([P, NT, C]),
                                   ALU.mult).then_inc(S["gu_done"], 1)

            def third_norm(b):
                p = b.par
                pool.wait_ge(S["seu_done"], b.n + 1)
                if reached(b.n - 1):
                    pool.wait_ge(S["z_done"], b.n - 1)
                    pool.wait_ge(S["iru_done"], b.n - 1)
                pool.tensor_tensor(ru[p][:], seu[p][:], nhalfc[:, 0:NT], ALU.pow).then_inc(S["u_pow"], 1)

            def step(st):
                for s, work in ((1, differences), (5, divide), (6, second_norm), (0, powers), (6, modulate),
                                (2, norms), (6, gate_u), (6, third_norm), (5, scale_wo), (3, operands),
                                (4, add_lags), (3, q_times_z)):
                    if st[s] is not None:
                        work(st[s])

            pool.wait_ge(S["ld_c0"], 48)
            pool.wait_ge(S["ld_c1"], 48)
            pool.wait_ge(S["tabs_done"], 2)
            pool.wait_ge(S["zero_done"], 10)
            pipeline(pool, step)

            pool.wait_ge(S["lg_done"], NB)
            pool.iota(own_row[:], [[1, TOP], [TOP * P, NB * NT]], base=-TOP * NB * T, channel_multiplier=TOP,
                      allow_small_or_imprecise_dtypes=True).then_inc(S["rows_iota"], 1)
            pool.iota(empty_row[:], [[P, NTILE * RS]], base=TOP * NB * T, channel_multiplier=1,
                      allow_small_or_imprecise_dtypes=True).then_inc(S["rows_iota"], 1)
            pool.wait_ge(S["slot_done"], 1)
            pool.wait_ge(S["extra_done"], 2)
            pool.wait_ge(S["slots_zero"], 16)

            def scatter(g):
                p = g.par
                if reached(g.n - 1):
                    pool.wait_ge(scat[p], 16 * TOP * FS * (g.turn - 1))
                pool.sem_inc(S["passed_pool"], 1)
                pool.tensor_copy(slot_z[p][:], slot[:, :, bass.ds(g.n * FS, FS)]).then_inc(S["slots_copied"], 1)
                pool.tensor_copy(zg[p][:, :, :, C:RW], extra[:, :, bass.ds(g.n * FS, FS), :]).then_inc(S["slots_copied"], 1)
                pool.wait_ge(S["slots_copied"], 2 * (g.n + 1))
                pool.wait_ge(ld_z[p], 16 * TOP * g.turn)
                pool.sem_inc(S["passed_pool"], 1)
                for t in range(FS):
                    for n in range(TOP):
                        pool.indirect_dma_start(
                            out=xs_dram, out_offset=bass.IndirectOffsetOnAxis(ap=slot_z[p][:, n, t:t + 1], axis=0),
                            in_=zg[p][:, n, t, :], in_offset=None).then_inc(scat[p], 16)

            groups(pool, scatter, NF)

            def return_tile(i):
                q = i.quad
                pool.wait_ge(S["yr_done"], i.n + 1)
                pool.sem_inc(S["passed_pool"], 1)
                for k in range(RS):
                    pool.indirect_dma_start(
                        out=ys_dram, out_offset=bass.IndirectOffsetOnAxis(ap=yrow[q][:, k:k + 1], axis=0),
                        in_=yr[q][:, k, :], in_offset=None).then_inc(st_y[q], 16)

            routed_tiles(pool, return_tile)

        @block.scalar
        def _(act):
            act.wait_ge(S["ld_c0"], 48)
            act.activation(silu_e[:], cTt[:], ACT.Exp, scale=-1.0).then_inc(S["silu_exp"], 1)
            act.activation(expd[:], vec[:, 0:1], ACT.Exp).then_inc(S["expd_done"], 1)
            act.wait_ge(S["nexpd_done"], 1)
            act.wait_ge(S["iota_done"], 12)
            act.activation(pw[:], iota33[:], ACT.Exp, scale=nexpd[:, 0:1]).then_inc(S["pw_done"], 1)
            act.activation(pwr[:], iota_r[:], ACT.Exp, scale=nexpd[:, 0:1]).then_inc(S["pw_done"], 1)

            def evac_h(b):
                p = b.par
                act.wait_ge(S["t1_mm"], b.n + 1)
                if reached(b.n - 1):
                    act.wait_ge(S["mix_done"], 4 * (b.n - 1))
                act.activation(hT[p][:, 1:T + 1], psA[:, 0:T], ACT.Identity, scale=modT[:, 1, bass.ds(b.n, 1)],
                               bias=modT[:, 0, bass.ds(b.n, 1)]).then_inc(S["hT_done"], 1)

            def after_proj(b):
                p = b.par
                act.wait_ge(S["proj_mm"], b.n + 1)
                if reached(b.n - 1):
                    act.wait_ge(S["nrm_pow"], b.n - 1)
                for n in range(4):
                    if n or reached(b.n):
                        act.wait_ge(S["sq_done"], 4 * b.n + n)
                    act.activation(sq[:], psQK[:, n * C:(n + 1) * C], ACT.Square, scale=float(C) ** -0.5,
                                   accum_out=ssq[p][:, n:n + 1]).then_inc(S["sq_done"], 1)

            def evac_vg(b):
                act.wait_ge(S["proj_mm"], b.n + 1)
                if reached(b.n - 3):
                    act.wait_ge(S["den_done"], b.n - 3)
                act.activation(eg[b.quad][:], psV[:, T:2 * T], ACT.Exp, scale=-1.0).then_inc(S["eg_done"], 1)
                if reached(b.n - 3):
                    act.wait_ge(S["lagmul"], (BL - 1) * (b.n - 3))
                act.activation(vc[b.quad][:], psV[:, 0:T], ACT.Copy).then_inc(S["vc_done"], 1)

            def scale_qk(b):
                p = b.par
                act.wait_ge(S["rqk_done"], b.n + 1)
                if reached(b.n - 1):
                    act.wait_ge(S["t2_mm"], b.n - 1)
                for n in range(4):
                    act.activation(qn[p][:, n, :], psQK[:, n * C:(n + 1) * C], ACT.Copy, scale=rqk[p][:, n:n + 1])\
                       .then_inc(S["qn_done"], 1)

            def exp_qk(b):
                p = b.par
                act.wait_ge(S["t2_mm"], b.n + 1)
                if reached(b.n - 1):
                    act.wait_ge(S["lvl_q"], 4 * (b.n - 1))
                    act.wait_ge(S["qz_done"], b.n - 1)
                    act.wait_ge(S["lag_done"], BL * (b.n - 1))
                    act.wait_ge(S["q32_done"], b.n - 1)
                    act.wait_ge(S["k32_done"], b.n - 1)
                act.activation(qk[p][:], psT[:], ACT.Exp, scale=vec[:, 5:6]).then_inc(S["qk_exp"], 1)

            def copy_chunks(b):
                p = b.par
                act.wait_ge(S["u_mm"], b.n + 1)
                if reached(b.n - 1):
                    act.wait_ge(S["scan_done"], b.n - 1)
                act.activation(ue[p][:].rearrange("p e j -> p j e"),
                               psA[:, 0:D * (NCH - 1)].rearrange("p (j e) -> p j e", e=D), ACT.Copy)\
                   .then_inc(S["u_cp"], 1)

            def copy_level16(b):
                p = b.par
                act.wait_ge(S["lvl_mm"], b.n + 1)
                if reached(b.n - 1):
                    act.wait_ge(S["s_mm"], b.n - 1)
                act.activation(sc[p][:], psL[:, 0:T], ACT.Copy).then_inc(S["sc16"], 1)

            def square_u(b):
                p = b.par
                act.wait_ge(S["u_done"], b.n + 1)
                if reached(b.n - 1):
                    act.wait_ge(S["seu_done"], b.n - 1)
                for t in range(NT):
                    if t or reached(b.n):
                        act.wait_ge(S["squ_done"], NT * b.n + t)
                    act.activation(squ[:], uu[p][:, t, :], ACT.Square, scale=float(C) ** -0.5,
                                   accum_out=ssu[p][:, t:t + 1]).then_inc(S["squ_done"], 1)

            def scale_z(b):
                p = b.par
                act.wait_ge(S["u_pow"], b.n + 1)
                if reached(b.n - 1):
                    act.wait_ge(S["t3_mm"], b.n - 1)
                    act.wait_ge(st_z[p], 16 * (b.turn - 1))
                for t in range(NT):
                    ins = act.activation(zz[p][:, t, :], uu[p][:, t, :], ACT.Copy, scale=ru[p][:, t:t + 1])
                ins.then_inc(S["z_done"], 1)

            def evac_z(b):
                p = b.par
                act.wait_ge(S["t3_mm"], b.n + 1)
                act.activation(zTs[p][:], psT[:, 0:T], ACT.Copy).then_inc(S["zTs_done"], 1)
                act.activation(zT[:, bass.ds(b.n * T, T)], psT[:, 0:T], ACT.Copy).then_inc(S["zT_done"], 1)

            def scores(first, last, batches):
                act.wait_ge(S["lg_done"], batches)
                act.activation(score[:, first:last, :].rearrange("p t e -> p (t e)"),
                               lgt[:, first * NE_R:last * NE_R], ACT.Sigmoid).then_inc(S["sig_done"], 1)

            def step(st):
                for s, work in ((1, evac_h), (7, evac_z), (2, evac_vg), (2, after_proj), (3, exp_qk),
                                (6, square_u), (4, copy_level16), (4, copy_chunks), (6, scale_z), (2, scale_qk)):
                    if st[s] is not None:
                        work(st[s])
                if st[STAGES - 1] is not None and st[STAGES - 1].left == 3:
                    scores(0, EARLY, NB - 4)

            act.wait_ge(S["ld_c1"], 48)
            act.wait_ge(S["mod_done"], 2)
            act.wait_ge(S["zero_done"], 10)
            pipeline(act, step)

            scores(EARLY, NB * NT, NB)
            act.wait_ge(S["ld_c2"], 32)

            def gelu_shared(g):
                for e in range(NE_S):
                    for c in range(HC):
                        act.wait_ge(S["h_mm"], HC * (NE_S * g.n + e) + c + 1)
                        if reached(g.n - 1):
                            act.wait_ge(S["y_mm"], g.n - 1)
                        psH = psB[:, c * 512:(c + 1) * 512] if c < 3 else psL[:]
                        act.activation(hid[e][g.par][:, c, :], psH, ACT.Gelu, bias=b1t[:, e * HC + c:e * HC + c + 1])\
                           .then_inc(S["gelu_done"], 1)

            groups(act, gelu_shared, SH_FIRST)

            def round_x(i):
                act.wait_ge(S["xt_mm"], i.n + 1)
                if reached(i.n - 1):
                    act.wait_ge(S["rh_mm"], 2 * (i.n - 1))
                act.activation(xh[i.par][:], (psT, psV)[i.par][:, 0:RT], ACT.Copy, scale=vec[:, 7:8])\
                   .then_inc(S["xh_done"], 1)

            def gelu_routed(i):
                for half in range(2):
                    act.wait_ge(S["rh_mm"], 2 * i.n + half + 1)
                    if reached(i.n - 1):
                        act.wait_ge(S["ry_mm"], i.n - 1)
                    for c in (2 * half, 2 * half + 1):
                        ins = act.activation(rhid[i.par][:, c, :], routed_h(i, c), ACT.Gelu,
                                             bias=w2t[i.quad][:, c:c + 1])
                    ins.then_inc(S["rgelu_done"], 1)

            def routed_step(i):
                round_x(i)
                if reached(i.n):
                    gelu_routed(Tile(i.m + (i.quad - 1) // 4, (i.quad - 1) % 4))

            routed_tiles(act, routed_step)
            gelu_routed(Tile((NTILE - 1) // 4, (NTILE - 1) % 4))
            act.wait_ge(S["ry_mm"], NTILE)
            act.wait_ge(S["yr_done"], NTILE)
            for n in range(SH_FIRST, NF):
                gelu_shared(Group(n // 2, n % 2))
        @block.vector
        def _(dve):
            for p in range(2):
                dve.memset(hT[p][:, 0:1], 0.0).then_inc(S["zero_done"], 1)
                for n in lo:
                    dve.memset(lo[n][p][:], 0.0).then_inc(S["zero_done"], 1)
            dve.wait_ge(S["silu_exp"], 1)
            dve.tensor_scalar_add(silu_r[:], silu_e[:], 1.0).then_inc(S["silu_step"], 1)
            dve.wait_ge(S["silu_step"], 1)
            dve.reciprocal(silu_e[:], silu_r[:]).then_inc(S["silu_step"], 1)
            dve.wait_ge(S["silu_step"], 2)
            dve.tensor_tensor(siluT[:], silu_e[:], cTt[:], ALU.mult).then_inc(S["silu_done"], 1)
            dve.wait_ge(S["expd_done"], 1)
            dve.tensor_scalar(nexpd[:], expd[:], 1e30, -1.0, ALU.min, ALU.mult).then_inc(S["nexpd_done"], 1)
            dve.wait_ge(S["iota_done"], 12)
            for h in range(NH):
                dve.memset(blkones[h * D:(h + 1) * D, h * D:(h + 1) * D], 1.0).then_inc(S["consts_v"], 1)
            dve.tensor_tensor(it_x, it_s, it_t, ALU.bitwise_xor).then_inc(S["mask_step"], 1)
            dve.wait_ge(S["mask_step"], 1)
            dve.tensor_scalar(it_m, it_x, 24, 8, ALU.bitwise_and, ALU.bitwise_xor).then_inc(S["mask_step"], 1)
            dve.tensor_scalar(it_y, it_t, 8, 8, ALU.bitwise_and, ALU.bitwise_xor).then_inc(S["mask_step"], 1)
            dve.wait_ge(S["mask_step"], 3)
            dve.tensor_tensor(it_x, it_m, it_y, ALU.bitwise_or).then_inc(S["mask_step"], 1)
            dve.wait_ge(S["mask_step"], 4)
            dve.tensor_scalar(mask8[:], it_x, 0, None, ALU.is_equal).then_inc(S["mask_step"], 1)
            dve.wait_ge(S["pw_done"], 2)
            dve.tensor_copy(wrow[:], pw[:, 1:2].broadcast_to([P, T])).then_inc(S["tabs_done"], 1)
            dve.memset(w32[:, :, 0:1], 0.0).then_inc(S["consts_v"], 1)
            dve.tensor_copy(w32[:, :, 1:NCH - 1], pw[:, CH:CH + 1].unsqueeze(2).broadcast_to([P, D, NCH - 2]))\
                .then_inc(S["tabs_done"], 1)
            dve.wait_ge(S["mod_mm"], 3)
            dve.tensor_copy(modT[:, 0, :], psA[:, 0:NB]).then_inc(S["mod_done"], 1)
            dve.tensor_scalar_add(modT[:, 1, :], psA[:, NB:2 * NB], 1.0).then_inc(S["mod_done"], 1)
            mg = psQK[0:NB, :].rearrange("b (k c) -> b k c", c=C)
            dve.tensor_copy(mrow[:, 1, :], mg[:, 1, :]).then_inc(S["mod_row_st"], 1)
            dve.tensor_scalar_add(mrow[:, 2, :], mg[:, 2, :], 1.0).then_inc(S["mod_row_st"], 1)
            dve.tensor_scalar(msgn[:], mg[:, 0:4:3, :], 0.0, 2.0, ALU.is_ge, ALU.mult).then_inc(S["mod_row_step"], 1)
            dve.tensor_scalar(mneg[:], mg[:, 0:4:3, :], -1.0, 0.25, ALU.mult, ALU.max).then_inc(S["mod_row_step"], 1)
            dve.wait_ge(S["mod_row_step"], 2)
            dve.tensor_tensor(mabs[:], mg[:, 0:4:3, :], mneg[:], ALU.max).then_inc(S["mod_row_step"], 1)
            dve.wait_ge(S["mod_row_step"], 3)
            dve.scalar_tensor_tensor(mrow[:, 0:4:3, :], msgn[:], 1.0, mabs[:], ALU.subtract, ALU.mult)\
                .then_inc(S["mod_row_st"], 1)
            dve.wait_ge(S["consts_v"], NH + 1)
            dve.wait_ge(S["tabs_done"], 2)
            dve.wait_ge(S["mask_step"], 5)

            def stats(src, st, mv, ve, n, s_st, s_ag, s_ve, s_used):
                for t in range(NT):
                    dve.bn_stats(st[:, t, :], src[:, t, :]).then_inc(s_st, 1)
                dve.wait_ge(s_st, NT * n + NT)
                if reached(n - 1):
                    dve.wait_ge(s_used, n - 1)
                dve.sem_inc(S["passed_dve"], 1)
                for t in range(NT):
                    dve.bn_aggr(mv[:, t, :], st[:, t, :]).then_inc(s_ag, 1)
                dve.wait_ge(s_ag, NT * n + NT)
                dve.tensor_scalar_add(ve[:], mv[:, :, 1], LN_EPS).then_inc(s_ve, 1)

            def ln1_stats(b):
                p = b.par
                dve.wait_ge(ld_x[p], 16 * b.turn)
                stats(xb[p], st1[p], mv1[p], ve1[p], b.n, S["ln1_st"], S["ln1_ag"], S["ln1_ve"], S["ln1_xn"])

            def ln1_apply(b):
                p = b.par
                dve.wait_ge(S["ln1_pow"], b.n + 1)
                if reached(b.n - 1):
                    dve.wait_ge(S["t1_mm"], b.n - 1)
                for t in range(NT):
                    ins = dve.tensor_scalar(xn[p][:, t, :], xb[p][:, t, :], mv1[p][:, t, 0:1], rs1[p][:, t:t + 1],
                                            ALU.subtract, ALU.mult)
                ins.then_inc(S["ln1_xn"], 1)

            def mix(b):
                p = b.par
                dve.wait_ge(S["d_done"], b.n + 1)
                if reached(b.n - 1):
                    dve.wait_ge(S["proj_mm"], b.n - 1)
                for c in "qkvg":
                    dve.scalar_tensor_tensor(xm[c][p][:], dT[p][:], vec[:, MIX[c]:MIX[c] + 1], hT[p][:, 0:T],
                                             ALU.mult, ALU.add).then_inc(S["mix_done"], 1)

            def qk_norm(b):
                p = b.par
                dve.wait_ge(S["nrm_pow"], b.n + 1)
                dve.tensor_scalar_add(nre[p][:], nrm[p][:], RMS_EPS).then_inc(S["nre_done"], 1)
                dve.wait_ge(S["nre_done"], b.n + 1)
                if reached(b.n - 1):
                    dve.wait_ge(S["qn_done"], 4 * (b.n - 1))
                dve.reciprocal(rqk[p][:], nre[p][:]).then_inc(S["rqk_done"], 1)

            def turn_v(b):
                dve.wait_ge(S["vc_done"], b.n + 1)
                if reached(b.n - 3):
                    dve.wait_ge(S["s_mm"], b.n - 3)
                dve.transpose(vT[b.quad][:], vc[b.quad][:]).then_inc(S["vT_done"], 1)

            def scan_z(b):
                p = b.par
                q, k = qk[p][:, 0:T], qk[p][:, T:2 * T]
                dve.wait_ge(S["qk_exp"], b.n + 1)
                if reached(b.n - 1):
                    dve.wait_ge(S["qz_done"], b.n - 1)
                dve.tensor_tensor_scan(zc[p][:], wrow[:], k, 0.0, ALU.mult, ALU.add).then_inc(S["zscan"], 1)

            def chunk_operands(b):
                p = b.par
                q, k = qk[p][:, 0:T], qk[p][:, T:2 * T]
                dve.wait_ge(S["qk_exp"], b.n + 1)
                if reached(b.n):
                    dve.wait_ge(S["kT_done"], b.n)
                dve.tensor_tensor(k32[:].rearrange("p (n s) -> p n s", s=CH), k.rearrange("p (n s) -> p n s", s=CH),
                                  pwr[:].unsqueeze(1).broadcast_to([P, NCH, CH]), ALU.mult).then_inc(S["k32_done"], 1)
                if reached(b.n - 3):
                    dve.wait_ge(S["s_mm"], b.n - 3)
                dve.tensor_tensor(q32[b.quad][:].rearrange("p (n s) -> p n s", s=CH),
                                  q.rearrange("p (n s) -> p n s", s=CH),
                                  pw[:, 1:CH + 1].unsqueeze(1).broadcast_to([P, NCH, CH]), ALU.mult)\
                    .then_inc(S["q32_done"], 1)
                dve.wait_ge(S["k32_done"], b.n + 1)
                if reached(b.n - 1):
                    dve.wait_ge(S["u_mm"], b.n - 1)
                dve.transpose(kT[p][:], k32[:]).then_inc(S["kT_done"], 1)

            def lags(b):
                p = b.par
                q, k = qk[p][:, 0:T], qk[p][:, T:2 * T]
                dve.wait_ge(S["qk_exp"], b.n + 1)
                if reached(b.n - 1):
                    dve.wait_ge(S["bc_mm"], b.n - 1)
                q3 = q.rearrange("p (n s) -> p n s", s=BL)
                k3 = k.rearrange("p (n s) -> p n s", s=BL)
                for l in range(BL):
                    dst = pz[p][:, LAG_OFF[l]:LAG_OFF[l + 1]].rearrange("p (n s) -> p n s", s=BL - l)
                    if l == 0:
                        ins = dve.tensor_tensor(dst, q3, k3, ALU.mult)
                    else:
                        ins = dve.scalar_tensor_tensor(dst, k3[:, :, 0:BL - l], pw[:, l:l + 1], q3[:, :, l:BL],
                                                       ALU.mult, ALU.mult)
                    ins.then_inc(S["lag_done"], 1)

            def chunk_states(b):
                p = b.par
                dve.wait_ge(S["u_cp"], b.n + 1)
                if reached(b.n - 1):
                    dve.wait_ge(S["s_mm"], b.n - 1)
                dve.tensor_tensor_scan(Ast[p][:].rearrange("p e j -> p (e j)"), w32[:].rearrange("p e j -> p (e j)"),
                                       ue[p][:].rearrange("p e j -> p (e j)"), 0.0, ALU.mult, ALU.add)\
                    .then_inc(S["scan_done"], 1)

            def keep_level8(b):
                p = b.par
                dve.wait_ge(S["sc16"], b.n + 1)
                dve.sem_inc(S["passed_dve"], 1)
                dve.copy_predicated(sc[p][:], mask8[:], psL[:, T:2 * T]).then_inc(S["sc_done"], 1)

            def denominators(b):
                p = b.par
                dve.wait_ge(S["bc_mm"], b.n + 1)
                dve.wait_ge(S["eg_done"], b.n + 1)
                if reached(b.n - 1):
                    dve.wait_ge(S["rden_done"], b.n - 1)
                dve.scalar_tensor_tensor(den[p][:], eg[b.quad][:], 1.0, psB[:, LAGS:PZW], ALU.add, ALU.mult)\
                    .then_inc(S["den_done"], 1)

            def lag_products(b):
                p = b.par
                dve.wait_ge(S["bc_mm"], b.n + 1)
                if reached(b.n - 1):
                    dve.wait_ge(S["ssum_done"], b.n - 1)
                if reached(b.n):
                    dve.wait_ge(S["lagadd"], (BL - 1) * b.n)
                dve.wait_ge(S["vc_done"], b.n + 1)
                dve.tensor_tensor(slag[p][:], psB[:, 0:T], vc[b.quad][:], ALU.mult).then_inc(S["lag0"], 1)
                v3 = vc[b.quad][:].rearrange("p (n s) -> p n s", s=BL)
                for l in range(1, BL):
                    o = LAG_OFF[l]
                    n = NBL * (BL - l)
                    dve.tensor_tensor(tlag[:, o - T:o - T + n].rearrange("p (n s) -> p n s", s=BL - l),
                                      psB[:, o:o + n].rearrange("p (n s) -> p n s", s=BL - l),
                                      v3[:, :, 0:BL - l], ALU.mult).then_inc(S["lagmul"], 1)

            def reciprocals(b):
                p = b.par
                dve.wait_ge(S["den_done"], b.n + 1)
                if reached(b.n - 1):
                    dve.wait_ge(S["att_done"], b.n - 1)
                dve.reciprocal(rden[p][:], den[p][:]).then_inc(S["rden_done"], 1)

            def sum_up(b):
                p = b.par
                dve.wait_ge(S["s_mm"], b.n + 1)
                dve.wait_ge(S["lagadd"], (BL - 1) * (b.n + 1))
                if reached(b.n - 1):
                    dve.wait_ge(S["att_done"], b.n - 1)
                dve.tensor_tensor(ssum[p][:], psA[:, 0:T], slag[p][:], ALU.add).then_inc(S["ssum_done"], 1)

            def residual(b):
                p = b.par
                dve.wait_ge(S["w_mm"], b.n + 1)
                dve.wait_ge(ld_xr[p], 16 * b.turn)
                if reached(b.n - 1):
                    dve.wait_ge(S["fin_done"], b.n - 1)
                dve.tensor_tensor(x2[p][:].rearrange("p t c -> p (t c)"), psT[:, 0:T],
                                  xr[p][:].rearrange("p t c -> p (t c)"), ALU.add).then_inc(S["x2_done"], 1)

            def ln2_stats(b):
                p = b.par
                dve.wait_ge(S["x2_done"], b.n + 1)
                stats(x2[p], st2[p], mv2[p], ve2[p], b.n, S["ln2_st"], S["ln2_ag"], S["ln2_ve"], S["ln2_xn"])

            def ln2_apply(b):
                p = b.par
                dve.wait_ge(S["ln2_pow"], b.n + 1)
                if reached(b.n - 1):
                    dve.wait_ge(S["u_done"], b.n - 1)
                for t in range(NT):
                    ins = dve.tensor_scalar(xn2[p][:, t, :], x2[p][:, t, :], mv2[p][:, t, 0:1], rs2[p][:, t:t + 1],
                                            ALU.subtract, ALU.mult)
                ins.then_inc(S["ln2_xn"], 1)

            def mean_square(b):
                p = b.par
                dve.wait_ge(S["squ_done"], NT * b.n + NT)
                if reached(b.n - 1):
                    dve.wait_ge(S["u_pow"], b.n - 1)
                dve.tensor_scalar_add(seu[p][:], ssu[p][:], FFN_EPS).then_inc(S["seu_done"], 1)

            def finish_u(b):
                p = b.par
                dve.wait_ge(S["gu_done"], b.n + 1)
                dve.tensor_tensor(Fin[:, bass.ds(b.n * (NT * C), NT * C)], gu[p][:].rearrange("p t c -> p (t c)"),
                                  x2[p][:].rearrange("p t c -> p (t c)"), ALU.add).then_inc(S["fin_done"], 1)

            def scale_back(b):
                p = b.par
                dve.wait_ge(S["u_pow"], b.n + 1)
                if reached(b.n - 1):
                    dve.wait_ge(S["lg_done"], b.n - 1)
                dve.reciprocal(iru[b.quad][:], ru[p][:]).then_inc(S["iru_done"], 1)

            def logits(b):
                dve.wait_ge(S["lg_mm"], b.n + 1)
                dve.wait_ge(S["iru_done"], b.n + 1)
                for t in range(NT):
                    ins = dve.tensor_scalar(lgt[:, bass.ds(b.n * (NT * NE_R) + t * NE_R, NE_R)],
                                            psB[:, LG + t * NE_R:LG + (t + 1) * NE_R], iru[b.quad][:, t:t + 1], None,
                                            ALU.mult)
                ins.then_inc(S["lg_done"], 1)

            def split_z(n, par):
                if reached(n - 1):
                    dve.wait_ge(S["h_mm"], HC * NE_S * (n - 1))
                dve.wait_ge(S["zT_done"], 2 * n + 2)
                z = zT[:, bass.ds(n * FT, FT)]
                dve.tensor_copy(zh[par][:], z).then_inc(S["zh_done"], 1)
                dve.wait_ge(S["zh_done"], n + 1)
                dve.tensor_tensor(zl[par][:], z, zh[par][:].bitcast(F32), ALU.subtract).then_inc(S["z_split"], 1)

            def best_tiles(first, last):
                for t in range(first, last):
                    dve.max(top[:, t, :], score[:, t, :]).then_inc(S["top_done"], 1)
                dve.wait_ge(S["top_done"], first + last)
                for t in range(first, last):
                    dve.max_index(topi[:, t, :], top[:, t, :], score[:, t, :]).then_inc(S["top_done"], 1)

            def prepare_w1():
                dve.wait_ge(S["ld_w1"], 16)
                dve.tensor_scalar(W1[:], W1[:], vec[:, 6:7], None, ALU.mult).then_inc(S["w1g_done"], 1)
                dve.wait_ge(S["w1g_done"], 1)
                dve.tensor_copy(W1h[:], W1[:]).then_inc(S["w1g_done"], 1)
                dve.wait_ge(S["w1g_done"], 2)
                dve.tensor_tensor(W1l[:], W1[:], W1h[:].bitcast(F32), ALU.subtract).then_inc(S["w1g_done"], 1)


            def step(st):
                for s, work in ((6, residual), (5, sum_up), (0, ln1_stats), (1, mix), (6, ln2_stats),
                                (6, ln2_apply), (8, logits), (0, ln1_apply), (2, turn_v), (3, chunk_operands),
                                (3, scan_z), (6, mean_square), (3, lags), (2, qk_norm), (4, chunk_states),
                                (4, keep_level8), (4, lag_products), (6, scale_back), (4, denominators),
                                (6, finish_u), (4, reciprocals)):
                    if st[s] is not None:
                        work(st[s])
                left = st[STAGES - 1].left if st[STAGES - 1] is not None else None
                if left == 4:
                    prepare_w1()
                if left == 3:
                    split_z(0, 0)
                    split_z(1, 1)
                if left == 2:
                    dve.wait_ge(S["sig_done"], 1)
                    best_tiles(0, EARLY)

            pipeline(dve, step)

            NTT = NB * NT
            dve.wait_ge(S["sig_done"], 2)
            best_tiles(EARLY, NTT)
            dve.tensor_reduce(ssc[:], score[:], AX.X, ALU.add).then_inc(S["rt_sum"], 1)
            dve.wait_ge(S["rt_sum"], 1)
            dve.reciprocal(rsc[:], ssc[:]).then_inc(S["rt_sum"], 1)
            dve.wait_ge(S["rt_sum"], 2)
            dve.wait_ge(S["top_done"], 2 * NTT)
            dve.tensor_copy(topf[:], topi[:, :, 0:2]).then_inc(S["hot_step"], 1)
            dve.tensor_tensor(gk[:], top[:, :, 0:2], rsc[:].unsqueeze(2).broadcast_to([P, NTT, 2]), ALU.mult)\
                .then_inc(S["hot_step"], 1)
            dve.wait_ge(S["hot_step"], 2)
            for n in range(2):
                dve.tensor_tensor(hot[:, n], iota8[:].unsqueeze(1).broadcast_to([P, NTT, NE_R]),
                                  topf[:, :, n:n + 1].broadcast_to([P, NTT, NE_R]), ALU.is_equal)\
                    .then_inc(S["hot_step"], 1)
            dve.wait_ge(S["hot_step"], 4)
            dve.tensor_tensor(hits[:], hot[:, 0], hot[:, 1], ALU.add).then_inc(S["hits_done"], 1)
            dve.tensor_copy(extra[:, :, :, 0], gk[:].rearrange("p t n -> p n t")).then_inc(S["extra_done"], 1)
            dve.wait_ge(S["ld_c2"], 32)
            dve.tensor_tensor(b2s[:], b2t[:, 0:C], b2t[:, C:2 * C], ALU.add).then_inc(S["b2s_done"], 1)
            dve.memset(inner[:], 1.0).then_inc(S["inner_done"], 1)
            dve.wait_ge(S["inner_done"], 1)
            dve.memset(inner[:, :, 0:1], 0.0).then_inc(S["inner_done"], 1)

            NR = NTT * NE_R
            dve.wait_ge(S["rank_mm"], 1)
            dve.tensor_copy(total[:], psV[:, NR:2 * NR].rearrange("p (t e) -> p e t", e=NE_R)).then_inc(S["rank_step"], 1)
            dve.wait_ge(S["rank_step"], 1)
            dve.wait_ge(S["inner_done"], 2)
            dve.tensor_tensor_scan(incl[:].rearrange("p e t -> p (e t)"), inner[:].rearrange("p e t -> p (e t)"),
                                   total[:].rearrange("p e t -> p (e t)"), 0.0, ALU.mult, ALU.add)\
                .then_inc(S["rank_step"], 1)
            dve.wait_ge(S["rank_step"], 2)
            dve.tensor_scalar(tiles_i[:, 0, :], incl[:, :, NTT - 1], float(RT - 1), None, ALU.add)\
                .then_inc(S["rank_step"], 1)
            dve.wait_ge(S["rank_step"], 3)
            dve.tensor_scalar(tiles_i[:, 1, :], tiles_i[:, 0, :], RT.bit_length() - 1, None, ALU.logical_shift_right)\
                .then_inc(S["rank_step"], 1)
            dve.wait_ge(S["rank_step"], 4)
            dve.tensor_copy(tiles[:], tiles_i[:, 1, :]).then_inc(S["rank_step"], 1)
            dve.wait_ge(S["rank_step"], 5)
            dve.tensor_tensor_scan(ends[:], onesm[:, 0:NE_R], tiles[:], 0.0, ALU.mult, ALU.add).then_inc(S["rank_step"], 1)
            dve.wait_ge(S["rank_step"], 6)
            dve.tensor_tensor(begins[:], ends[:], tiles[:], ALU.subtract).then_inc(S["rank_step"], 1)
            dve.tensor_tensor(total[:], incl[:], total[:], ALU.subtract).then_inc(S["rank_step"], 1)
            dve.tensor_tensor(past[:], iota_t[:].unsqueeze(2).broadcast_to([P, NTILE, NE_R]),
                              ends[:].unsqueeze(1).broadcast_to([P, NTILE, NE_R]), ALU.is_ge).then_inc(S["expert_step"], 1)
            dve.wait_ge(S["rank_step"], 8)
            dve.scalar_tensor_tensor(base[:], begins[:].unsqueeze(2).broadcast_to([P, NE_R, NTT]), float(RT),
                                     total[:], ALU.mult, ALU.add).then_inc(S["rank_step"], 1)
            dve.wait_ge(S["rank_step"], 9)
            dve.tensor_tensor(place[:], psV[:, 0:NR].rearrange("p (t e) -> p t e", e=NE_R),
                              base[:].rearrange("p e t -> p t e"), ALU.add).then_inc(S["rank_step"], 1)
            dve.wait_ge(S["rank_step"], 10)
            for n in range(TOP):
                dve.tensor_tensor(hplace[:, n], hot[:, n], place[:], ALU.mult).then_inc(S["rank_step"], 1)
            dve.wait_ge(S["rank_step"], 10 + TOP)
            dve.tensor_reduce(slotf[:].rearrange("p n t -> p (n t)"), hplace[:].rearrange("p n t e -> p (n t) e"),
                              AX.X, ALU.add).then_inc(S["rank_step"], 1)
            dve.wait_ge(S["rank_step"], 11 + TOP)
            dve.tensor_copy(slot[:], slotf[:]).then_inc(S["slot_done"], 1)
            dve.wait_ge(S["rows_iota"], 2)
            dve.tensor_tensor(extra[:, :, :, 1], own_row[:], slotf[:], ALU.subtract).then_inc(S["extra_done"], 1)
            dve.wait_ge(S["expert_step"], 1)
            dve.tensor_reduce(expf[:], past[:], AX.X, ALU.add).then_inc(S["expert_step"], 1)
            dve.wait_ge(S["expert_step"], 2)
            dve.tensor_scalar(expert[:], expf[:], float(NE_R - 1), None, ALU.min).then_inc(S["expert_done"], 1)

            dve.wait_ge(S["b2s_done"], 1)
            dve.wait_ge(S["ld_g"], 16)

            def times_gb(g, t):
                return dve.tensor_tensor(t.rearrange("p (b t) c -> p b t c", t=NT),
                                         t.rearrange("p (b t) c -> p b t c", t=NT),
                                         grow[:, bass.ds(2 * g.n, 2), :].unsqueeze(2).broadcast_to([P, 2, NT, C]),
                                         ALU.mult)

            def add_shared(g):
                p = g.par
                dve.wait_ge(S["y_mm"], g.n + 1)
                if reached(g.n - 1):
                    dve.wait_ge(S["shared_sum"], g.n - 1)
                if isinstance(g.n, int) and g.n >= SH_FIRST:
                    dve.wait_ge(S["fout_done"], g.n)
                dve.tensor_tensor(acc[p][:], (psA, psQK)[p][:].rearrange("p (t c) -> p t c", c=C),
                                  b2s[:].unsqueeze(1).broadcast_to([P, FS, C]), ALU.add).then_inc(S["shared_done"], 1)
                dve.wait_ge(S["shared_done"], g.n + 1)
                if not (isinstance(g.n, int) and g.n + 2 >= NF):
                    split_z(g.n + 2, p)
                times_gb(g, acc[p][:]).then_inc(S["shared_gb"], 1)
                dve.wait_ge(S["shared_gb"], g.n + 1)
                F = Fin[:, bass.ds(g.n * (FS * C), FS * C)]
                dve.tensor_tensor(F, F, acc[p][:].rearrange("p t c -> p (t c)"), ALU.add).then_inc(S["shared_sum"], 1)

            groups(dve, add_shared, SH_FIRST)

            def turn_tile(i):
                dve.wait_ge(S["xh_done"], i.n + 1)
                dve.scalar_tensor_tensor(xl[i.par][:], (psT, psV)[i.par][:, 0:RT], vec[:, 7:8],
                                         xh[i.par][:].bitcast(F32), ALU.mult, ALU.subtract).then_inc(S["xT_done"], 1)

            def fetch_weights(i):
                e = dve.value_load(expert[0:1, bass.ds(i.n, 1)], min_val=0, max_val=NE_R - 1)
                if reached(i.n - 3):
                    dve.wait_ge(S["ry_mm"], i.n - 3)
                    dve.wait_ge(S["yr_done"], i.n - 3)
                w = wres[:, bass.ds(e, 1), :].rearrange("p o n -> p (o n)")
                high = w1t[i.quad][:, 0:HID]
                dve.tensor_copy(high, w[:, 0:HID]).then_inc(S["wh_done"], 1)
                dve.tensor_copy(w2t[i.quad][:], w[:, HID:]).then_inc(S["wrt_done"], 1)
                dve.wait_ge(S["wh_done"], i.n + 1)
                dve.tensor_tensor(w1t[i.quad][:, HID:2 * HID], w[:, 0:HID], high.bitcast(F32),
                                  ALU.subtract).then_inc(S["wrt_done"], 1)

            def routed_step(i):
                turn_tile(i)
                if reached(i.n - 1):
                    routed_out(i.n - 2, (i.quad - 2) % 4, i.fourth if i.quad >= 2 else i.fourth - 1)
                if not (isinstance(i.n, int) and i.n + 1 >= NTILE):
                    fetch_weights(Tile(i.m + (i.quad + 1) // 4, (i.quad + 1) % 4))

            def routed_out(n, q, fourth):
                p = q % 2
                dve.wait_ge(S["ry_mm"], n + 1)
                if reached(n - 1):
                    dve.wait_ge(S["yr_done"], n - 1)
                dve.tensor_tensor(yb[p][:], (psA, psQK)[p][:, 0:RT].rearrange("p (k c) -> p k c", c=C),
                                  w2t[q][:, HC + HC * C:].unsqueeze(1).broadcast_to([P, RS, C]), ALU.add)\
                    .then_inc(S["yb_done"], 1)
                if reached(n - 3):
                    dve.wait_ge(st_y[q], 16 * RS * (fourth - 1))
                dve.tensor_tensor(yrow[q][:], xin[q][:, :, C + 1], empty_row[:, bass.ds(n * RS, RS)], ALU.add)
                dve.wait_ge(S["yb_done"], n + 1)
                dve.tensor_tensor(yr[q][:], yb[p][:], xin[q][:, :, C:C + 1].broadcast_to([P, RS, C]), ALU.mult)\
                    .then_inc(S["yr_done"], 1)

            dve.wait_ge(S["expert_done"], 1)
            dve.wait_ge(S["ld_wr"], 32)
            dve.wait_ge(S["y_mm"], SH_FIRST)
            fetch_weights(Tile(0, 0))
            routed_tiles(dve, routed_step)
            for n in (NTILE - 2, NTILE - 1):
                routed_out(n, n % 4, n // 4 + 1)

            def sum_group(g):
                p = g.par
                dve.wait_ge(ld_y[p], 16 * g.turn)
                if reached(g.n - 1):
                    dve.wait_ge(S["fout_done"], g.n - 1)
                dve.tensor_tensor(acc[p][:], yg[p][:, :, 0, :], yg[p][:, :, 1, :], ALU.add).then_inc(S["sum_k"], 1)
                dve.wait_ge(S["sum_k"], g.n + 1)
                times_gb(g, acc[p][:]).then_inc(S["sum_gb"], 1)
                dve.wait_ge(S["sum_gb"], g.n + 1)
                F = Fin[:, bass.ds(g.n * (FS * C), FS * C)]
                dve.tensor_tensor(F, F, acc[p][:].rearrange("p t c -> p (t c)"), ALU.add).then_inc(S["fout_done"], 1)

            dve.wait_ge(S["shared_sum"], SH_FIRST)
            groups(dve, sum_group, SH_FIRST)
            for n in range(SH_FIRST, NF):
                g = Group(n // 2, n % 2)
                add_shared(g)
                dve.wait_ge(S["shared_sum"], n + 1)
                sum_group(g)

        @block.tensor
        def _(pe):
            def mm(dst, lhsT, rhs, start=True, stop=True):
                return pe.matmul(dst, lhsT, rhs, start=start, stop=stop)

            pe.wait_ge(S["ld_c0"], 48)
            pe.wait_ge(S["silu_done"], 1)
            mm(psA[:, 0:NB], wm[:, 0:C], siluT[:]).then_inc(S["mod_mm"], 1)
            mm(psA[:, NB:2 * NB], wm[:, C:2 * C], siluT[:]).then_inc(S["mod_mm"], 1)
            mm(psQK[0:NB, :], siluT[:], wm[:, 2 * C:6 * C]).then_inc(S["mod_mm"], 1)
            pe.wait_ge(S["iota_done"], 14)
            pe.wait_ge(S["ld_c1"], 48)
            pe.wait_ge(S["consts_v"], NH + 1)
            pe.wait_ge(S["mod_done"], 2)
            pe.wait_ge(S["mod_row_st"], 3)

            def turn_x(b):
                pe.wait_ge(S["ln1_xn"], b.n + 1)
                if reached(b.n):
                    pe.wait_ge(S["hT_done"], b.n)
                if reached(b.n - 3):
                    pe.wait_ge(S["u_cp"], b.n - 3)
                for t in range(NT):
                    ins = pe.transpose(psA[:, t * P:(t + 1) * P], xn[b.par][:, t, :], ident[:])
                ins.then_inc(S["t1_mm"], 1)

            def project(b):
                p = b.par
                pe.wait_ge(S["mix_done"], 4 * b.n + 4)
                if reached(b.n):
                    pe.wait_ge(S["qn_done"], 4 * b.n)
                    pe.wait_ge(S["vc_done"], b.n)
                    pe.wait_ge(S["eg_done"], b.n)
                for n, c in enumerate("qk"):
                    for t in range(NT):
                        o = (2 * n + t) * C
                        mm(psQK[:, o:o + C], xm[c][p][:, t * P:(t + 1) * P], W4[:, n, :])
                mm(psV[:, 0:T], W4[:, 2, :], xm["v"][p][:])
                mm(psV[:, T:2 * T], W4[:, 3, :], xm["g"][p][:]).then_inc(S["proj_mm"], 1)

            def turn_qk(b):
                pe.wait_ge(S["qn_done"], 4 * b.n + 4)
                if reached(b.n - 2):
                    pe.wait_ge(S["x2_done"], b.n - 2)
                if reached(b.n):
                    pe.wait_ge(S["qk_exp"], b.n)
                for n in range(4):
                    ins = pe.transpose(psT[:, n * C:(n + 1) * C], qn[b.par][:, n, :], ident[:])
                ins.then_inc(S["t2_mm"], 1)

            def chunk_sums(b):
                p = b.par
                pe.wait_ge(S["kT_done"], b.n + 1)
                pe.wait_ge(S["vT_done"], b.n + 1)
                if reached(b.n):
                    pe.wait_ge(S["ssum_done"], b.n)
                pe.wait_ge(S["hT_done"], least(b.n + 4))
                if reached(b.n):
                    pe.wait_ge(S["u_cp"], b.n)
                pe.sem_inc(S["passed_pe"], 1)
                for j in range(NCH - 1):
                    for h in range(NH):
                        hs = slice(h * D, (h + 1) * D)
                        ins = mm(psA[hs, j * D:(j + 1) * D], kT[p][hs, j * CH:(j + 1) * CH],
                                 vT[b.quad][hs, j * D:(j + 1) * D])
                ins.then_inc(S["u_mm"], 1)

            def levels(b):
                p = b.par
                pe.wait_ge(S["lvl_q"], 4 * b.n + 4)
                if reached(b.n):
                    pe.wait_ge(S["sc_done"], b.n)
                pe.sem_inc(S["passed_pe"], 1)
                for n, (kk, qq) in enumerate((("k16", "q16"), ("k8", "q8"))):
                    for j in range(NCH):
                        for h in range(NH):
                            hs = slice(h * D, (h + 1) * D)
                            js = slice(j * CH, (j + 1) * CH)
                            ins = mm(psL[hs, n * T + j * CH:n * T + (j + 1) * CH], lo[kk][p][hs, js], lo[qq][p][hs, js])
                ins.then_inc(S["lvl_mm"], 1)

            def sum_heads(b):
                p = b.par
                if reached(b.n - 3):
                    pe.wait_ge(S["lg_done"], b.n - 3)
                pe.wait_ge(S["lag_done"], BL * b.n + BL)
                pe.wait_ge(S["qz_done"], b.n + 1)
                if reached(b.n):
                    pe.wait_ge(S["lagmul"], (BL - 1) * b.n)
                    pe.wait_ge(S["lag0"], b.n)
                    pe.wait_ge(S["den_done"], b.n)
                for o in range(0, PZW, 512):
                    n = min(512, PZW - o)
                    ins = mm(psB[:, o:o + n], blkones[:], pz[p][:, o:o + n])
                ins.then_inc(S["bc_mm"], 1)

            def attend(b):
                p = b.par
                pe.wait_ge(S["sc_done"], b.n + 1)
                pe.wait_ge(S["scan_done"], b.n + 1)
                pe.wait_ge(S["q32_done"], b.n + 1)
                pe.wait_ge(S["hT_done"], least(b.n + 5))
                if reached(b.n):
                    pe.wait_ge(S["ssum_done"], b.n)
                pe.sem_inc(S["passed_pe"], 1)
                st_j = Ast[p][:].rearrange("p e j -> p j e")
                for j in range(NCH):
                    js = slice(j * CH, (j + 1) * CH)
                    for h in range(NH):
                        hs = slice(h * D, (h + 1) * D)
                        dst = psA[hs, j * CH:(j + 1) * CH]
                        ins = mm(dst, vT[b.quad][hs, js], sc[p][hs, js], start=True, stop=(j == 0))
                        if j:
                            ins = mm(dst, st_j[hs, j - 1, :], q32[b.quad][hs, js], start=False, stop=True)
                ins.then_inc(S["s_mm"], 1)

            def out_proj(b):
                p = b.par
                pe.wait_ge(S["att_done"], b.n + 1)
                pe.wait_ge(S["wog_done"], b.n + 1)
                if reached(b.n):
                    pe.wait_ge(S["zT_done"], b.n)
                pe.wait_ge(S["qk_exp"], least(b.n + 3))
                if reached(b.n):
                    pe.wait_ge(S["x2_done"], b.n)
                for t in range(NT):
                    ins = mm(psT[:, t * P:(t + 1) * P], att[p][:, t * P:(t + 1) * P], wog[p][:])
                ins.then_inc(S["w_mm"], 1)

            def turn_z(b):
                pe.wait_ge(S["z_done"], b.n + 1)
                pe.wait_ge(S["qk_exp"], least(b.n + 4))
                if reached(b.n):
                    pe.wait_ge(S["zT_done"], b.n)
                for t in range(NT):
                    ins = pe.transpose(psT[:, t * P:(t + 1) * P], zz[b.par][:, t, :], ident[:])
                ins.then_inc(S["t3_mm"], 1)

            def route(b):
                pe.wait_ge(S["zTs_done"], b.n + 1)
                pe.wait_ge(S["lagmul"], (BL - 1) * least(b.n + 4))
                pe.wait_ge(S["den_done"], least(b.n + 4))
                if isinstance(b.n, int) and reached(b.n):
                    pe.wait_ge(S["lg_done"], b.n)
                for t in range(NT):
                    ins = mm(psB[:, LG + t * NE_R:LG + (t + 1) * NE_R], zTs[b.par][:, t * P:(t + 1) * P], centt[:])
                ins.then_inc(S["lg_mm"], 1)

            def step(st):
                for s, work in ((1, turn_x), (7, turn_z), (5, attend), (6, out_proj), (2, project), (8, route),
                                (3, turn_qk), (4, chunk_sums), (4, levels), (4, sum_heads)):
                    if st[s] is not None:
                        work(st[s])

            pipeline(pe, step)

            def rank():
                pe.wait_ge(S["hits_done"], 1)
                NR = NB * NT * NE_R
                hits_f = hits[:].rearrange("p t e -> p (t e)")
                mm(psV[:, 0:NR], below[:], hits_f)
                mm(psV[:, NR:2 * NR], onesm[:], hits_f).then_inc(S["rank_mm"], 1)

            pe.wait_ge(S["w1g_done"], 3)
            pe.wait_ge(S["ld_w2"], 16)
            pe.wait_ge(S["zT_done"], NB)
            pe.wait_ge(S["lg_done"], NB)
            pe.wait_ge(S["lagmul"], (BL - 1) * NB)

            def mm3(dst, high, rest, vhigh, vrest):
                mm(dst, high, vhigh, start=True, stop=False)
                mm(dst, high, vrest, start=False, stop=False)
                return mm(dst, rest, vhigh, start=False, stop=True)

            def shared_up(g, e):
                pe.wait_ge(S["z_split"], g.n + 1)
                for c in range(HC):
                    n = HC * (NE_S * g.n + e - 1) + c + 1
                    psH = psB[:, c * 512:(c + 1) * 512] if c < 3 else psL[:]
                    if reached(n):
                        pe.wait_ge(S["gelu_done"], n)
                    cs = slice(c * P, (c + 1) * P)
                    mm3(psH, W1h[:, e, cs], W1l[:, e, cs], zh[g.par][:], zl[g.par][:]).then_inc(S["h_mm"], 1)

            def shared_down(n, par):
                pe.wait_ge(S["gelu_done"], HC * NE_S * (n + 1))
                if reached(n - 1):
                    pe.wait_ge(S["shared_done"], n - 1)
                for t in range(FS):
                    for e in range(NE_S):
                        for c in range(HC):
                            ins = mm((psA, psQK)[par][:, t * C:(t + 1) * C],
                                     hid[e][par][:, c, t * P:(t + 1) * P], W2[:, e, c, :],
                                     start=(e == 0 and c == 0), stop=(e == NE_S - 1 and c == HC - 1))
                ins.then_inc(S["y_mm"], 1)

            def shared_step(g):
                shared_up(g, 0)
                if not (isinstance(g.n, int) and g.n in (0, SH_FIRST)):
                    shared_down(g.n - 1, 1 - g.par)
                if isinstance(g.n, int) and g.n == 0:
                    rank()
                shared_up(g, 1)

            groups(pe, shared_step, SH_FIRST)
            shared_down(SH_FIRST - 1, (SH_FIRST - 1) % 2)

            pe.wait_ge(S["gelu_done"], HC * NE_S * SH_FIRST)
            pe.wait_ge(S["shared_done"], SH_FIRST)
            pe.wait_ge(S["slot_done"], 1)

            def turn_tile(i):
                pe.wait_ge(ld_tile[i.quad], 16 * i.fourth)
                if reached(i.n - 1):
                    pe.wait_ge(S["xT_done"], i.n - 1)
                for k in range(RS):
                    ins = pe.transpose((psT, psV)[i.par][:, k * P:(k + 1) * P], xin[i.quad][:, k, 0:C], ident[:])
                ins.then_inc(S["xt_mm"], 1)

            def routed_up(i):
                pe.wait_ge(S["wrt_done"], 2 * (i.n + 1))
                pe.wait_ge(S["xT_done"], i.n + 1)
                for c in range(HC):
                    if c % 2 == 0 and reached(i.n - 1):
                        pe.wait_ge(S["rgelu_done"], 2 * (i.n - 1))
                    w = w1t[i.quad]
                    ins = mm3(routed_h(i, c), w[:, c * P:(c + 1) * P], w[:, HID + c * P:HID + (c + 1) * P],
                              xh[i.par][:], xl[i.par][:])
                    if c % 2:
                        ins.then_inc(S["rh_mm"], 1)

            def routed_down(n, q):
                pe.wait_ge(S["rgelu_done"], 2 * (n + 1))
                if reached(n - 1):
                    pe.wait_ge(S["yr_done"], n - 1)
                W2r = w2t[q][:, HC:HC + HC * C].rearrange("p (k c) -> p k c", c=C)
                for t in range(RS):
                    for c in range(HC):
                        ins = mm((psA, psQK)[q % 2][:, t * C:(t + 1) * C], rhid[q % 2][:, c, t * P:(t + 1) * P],
                                 W2r[:, c, :], start=(c == 0), stop=(c == HC - 1))
                ins.then_inc(S["ry_mm"], 1)

            def before(i, n):
                return Tile(i.m + (i.quad - n) // 4, (i.quad - n) % 4)

            def routed_step(i):
                turn_tile(i)
                if reached(i.n):
                    routed_up(before(i, 1))
                if reached(i.n - 1):
                    routed_down(before(i, 2).n, before(i, 2).quad)

            routed_tiles(pe, routed_step)
            last = Tile(NTILE // 4, NTILE % 4)
            routed_up(before(last, 1))
            routed_down(NTILE - 2, (NTILE - 2) % 4)
            routed_down(NTILE - 1, (NTILE - 1) % 4)

            pe.wait_ge(S["rgelu_done"], 2 * NTILE)
            pe.wait_ge(S["yr_done"], NTILE)
            for n in range(SH_FIRST, NF):
                shared_step(Group(n // 2, n % 2))
            shared_down(NF - 1, (NF - 1) % 2)


def least(n):
    return min(n, NB) if isinstance(n, int) else n


def launch_inputs(a):
    import numpy as np

    def flat(name):
        return a["L0_attn_" + name].reshape(-1)

    vecs = np.stack([flat("time_decay"), flat("mix_q"), flat("mix_k"), flat("mix_v"), flat("mix_g"),
                     flat("norm_scale"), a["L0_ffn_g_shared"], a["L0_ffn_g_routed"]], axis=1)
    wr = np.concatenate([a["L0_ffn_W1_r"], a["L0_ffn_b1_r"].reshape(NE_R, HC, P).transpose(0, 2, 1),
                         a["L0_ffn_W2_r"].reshape(NE_R, HC, P, C).transpose(0, 2, 1, 3).reshape(NE_R, P, HC * C)],
                        axis=2)
    return {
        "x": a["L0_attn_x"], "vecs": vecs, "cT": a["L0_c"].T,
        "wqkvg": np.stack([a["L0_attn_W" + n].T for n in "qkvg"], axis=1),
        "wo": a["L0_attn_Wo"].T, "wmod": a["L0_wmod"],
        "w1s": a["L0_ffn_W1_s"], "b1": a["L0_ffn_b1_s"].reshape(NE_S * HC, P).T, "w2s": a["L0_ffn_W2_s"],
        "b2": a["L0_ffn_b2_s"].reshape(1, NE_S * C), "wr": wr, "b2r": a["L0_ffn_b2_r"],
        "cent": a["L0_ffn_centroids"],
    }


def kernel(**inputs):
    import numpy as np
    import concourse.bacc as bacc
    from concourse.bass_utils import run_bass_kernel_spmd

    nc = bacc.Bacc("TRN2", target_bir_lowering=False, num_devices=1)
    given = launch_inputs({k: np.asarray(v) for k, v in inputs.items()})
    arrays, args = {}, {}
    for name, a in given.items():
        a = np.ascontiguousarray(a)
        arrays[f"in_{name}"] = a
        args[name] = nc.dram_tensor(f"in_{name}", a.shape, mybir.dt.from_np(a.dtype), kind="ExternalInput").ap()
    args["out"] = nc.dram_tensor("out_0", (NB, T, C), F32, kind="ExternalOutput").ap()
    adaln_kernel(nc, **args)
    r = run_bass_kernel_spmd(nc, [arrays], core_ids=[0])
    return r.results[0]["out_0"]
```
